# Optimizing a Trainium2 kernel written in Bass

```python
import numpy as np
import jax
import jax.numpy as jnp

def _softmax(x, axis=-1):
    return jax.nn.softmax(x, axis=axis)

def _gelu(x):
    return jax.nn.gelu(x, approximate=True)

def _silu(x):
    return jax.nn.silu(x)

def _sigmoid(x):
    return jax.nn.sigmoid(x)

def _layernorm(x, axis=-1, eps=1e-05):
    m = jnp.mean(x, axis=axis, keepdims=True)
    v = jnp.var(x, axis=axis, keepdims=True)
    return (x - m) / jnp.sqrt(v + eps)

def _scatter_add(tgt, idx, src, axis=0):
    return tgt.at[idx].add(src)

def _segment_sum(src, seg, n):
    return jax.ops.segment_sum(src, seg, n)
kernel_name = 'mk_decoder_postln_d2_seqx_r4_b11fa6'

def setup_inputs(seed: int=0):
    np.random.seed(seed)
    _w = jnp.asarray

    def _rec_inputs():
        import jax
        import jax.numpy as jnp
        _rk = jax.random.key(seed)
        x = -0.0002928 + 1 * jax.random.normal(jax.random.fold_in(_rk, 1), (8, 512, 256), jnp.float32)
        _lenS = 512 - jax.random.randint(jax.random.fold_in(_rk, 7), (8,), 0, max(1, 512 // 4) + 1, jnp.int32)
        _lenS2 = 512 - jax.random.randint(jax.random.fold_in(_rk, 8), (8,), 0, max(1, 512 // 4) + 1, jnp.int32)
        _ctx_1024P = jax.random.normal(jax.random.fold_in(_rk, 11), (8, 16, 256), jnp.float32)
        _ctx_1024c = jax.random.dirichlet(jax.random.fold_in(_rk, 511), 0.3 * jnp.ones((16,), jnp.float32), (8, 512))
        _ctx_1024t = jnp.einsum('bsk,bkd->bsd', _ctx_1024c, _ctx_1024P)
        _ctx_1024t = _ctx_1024t * jax.lax.rsqrt(jnp.mean(jnp.square(_ctx_1024t)) + 1e-12) * 0.953939
        ctx_1024 = -1.39393e-06 + 0.999914 * (_ctx_1024t + 0.3 * jax.random.normal(jax.random.fold_in(_rk, 611), (8, 512, 256), jnp.float32))
        _validS = jnp.arange(512)[None, :] < _lenS[:, None]
        _validS2 = jnp.arange(512)[None, :] < _lenS2[:, None]
        _causal = jnp.tril(jnp.ones((512, 512), dtype=bool))
        mask_BxSxS2_bk1 = jnp.broadcast_to(_validS2[:, None, :], (8, 512, 512))
        return (x, ctx_1024, mask_BxSxS2_bk1)
    x, ctx_1024, mask_BxSxS2_bk1 = _rec_inputs()

    def _L0_attn_setup():
        import jax, jax.numpy as jnp
        import numpy as np
        EPS = 1e-06

        def _log_g(x):
            return jnp.where(x >= 0, jnp.log(jax.nn.relu(x) + 0.5), -jax.nn.softplus(-x))

        def _reference_tuple_inner(inputs, norm_weight, router_w, router_b, w_hg, w_out):
            D = inputs.shape[-1]
            x = inputs * jax.lax.rsqrt(jnp.mean(inputs * inputs, axis=-1, keepdims=True) + EPS) * norm_weight
            probs = jax.nn.softmax(jnp.mean(x, axis=1) @ router_w.T + router_b, axis=-1)
            W_hg = jnp.einsum('be,ekd->bkd', probs, w_hg)
            W_out = jnp.einsum('be,eod->bod', probs, w_out)
            hg = jnp.einsum('bsd,bkd->bsk', x, W_hg)
            hidden, gate = (hg[..., :D], hg[..., D:])
            log_coeffs = -jax.nn.softplus(gate)
            log_values = -jax.nn.softplus(-gate) + _log_g(hidden)
            a_star = jnp.cumsum(log_coeffs, axis=1)
            log_h = a_star + jax.lax.cumlogsumexp(log_values - a_star, axis=1)
            h = jnp.exp(log_h)
            new_state = h[:, -1:]
            out = jnp.einsum('bsk,bok->bso', h, W_out)
            aux_loss = jnp.zeros((), inputs.dtype)
            return (out + inputs, new_state, aux_loss)
        key = jax.random.key(seed)
        ks = jax.random.split(key, 4)
        B, S, D, E = (4, 512, 256, 8)
        scale = D ** (-0.5)
        return {'inputs': jax.random.normal(ks[0], (B, S, D), dtype=jnp.float32), 'norm_weight': jnp.ones((D,), jnp.float32), 'router_w': jax.random.normal(ks[1], (E, D), jnp.float32) * scale, 'router_b': jnp.zeros((E,), jnp.float32), 'w_hg': jax.random.normal(ks[2], (E, 2 * D, D), jnp.float32) * scale, 'w_out': jax.random.normal(ks[3], (E, D, D), jnp.float32) * scale}
    _L0_attn_all = _L0_attn_setup()
    _L0_attn_in = {k: v for k, v in _L0_attn_all.items() if k in ('norm_weight', 'router_w', 'router_b', 'w_hg', 'w_out')}
    del _L0_attn_all

    def _L0_xattn_setup():
        import jax, jax.numpy as jnp
        import numpy as np
        import math
        HEADS = 16
        D_MODEL = 256
        D_K = D_MODEL // HEADS
        PRUNE_KEEP = 0.9

        def _split_heads(x, B):
            return x.reshape(B, -1, HEADS, D_K).transpose(0, 2, 1, 3)

        def _pruned_attention(q, k, v):
            B, H, S, _ = q.shape
            scores = jnp.einsum('bhqd,bhkd->bhqk', q, k) / math.sqrt(D_K)
            scores = jax.nn.softmax(scores, axis=-1)
            keep = int(S * PRUNE_KEEP)
            col_sum = jnp.sum(scores, axis=2)
            _, idx = jax.lax.top_k(col_sum, keep)
            mask = jnp.zeros((B, H, S), scores.dtype).at[jnp.arange(B)[:, None, None], jnp.arange(H)[None, :, None], idx].set(1.0)
            pruned = scores * mask[:, :, None, :]
            return jnp.einsum('bhqk,bhkd->bhqd', pruned, v)
        key = jax.random.key(seed)
        ks = jax.random.split(key, 12)
        B, S = (2, 512)
        sc = 0.02
        return {'q': jax.random.normal(ks[0], (B, S, D_MODEL), jnp.float32), 'k': jax.random.normal(ks[1], (B, S, D_MODEL), jnp.float32), 'v': jax.random.normal(ks[2], (B, S, D_MODEL), jnp.float32), 'Wq': jax.random.normal(ks[3], (D_MODEL, D_MODEL), jnp.float32) * sc, 'bq': jnp.zeros((D_MODEL,), jnp.float32), 'Wk': jax.random.normal(ks[4], (D_MODEL, D_MODEL), jnp.float32) * sc, 'bk': jnp.zeros((D_MODEL,), jnp.float32), 'Wv': jax.random.normal(ks[5], (D_MODEL, D_MODEL), jnp.float32) * sc, 'bv': jnp.zeros((D_MODEL,), jnp.float32), 'Wo': jax.random.normal(ks[6], (D_MODEL, D_MODEL), jnp.float32) * sc, 'bo': jnp.zeros((D_MODEL,), jnp.float32)}
    _L0_xattn_all = _L0_xattn_setup()
    _L0_xattn_in = {k: v for k, v in _L0_xattn_all.items() if k in ('Wq', 'bq', 'Wk', 'bk', 'Wv', 'bv', 'Wo', 'bo')}
    del _L0_xattn_all

    def _L0_ffn_setup():
        import jax, jax.numpy as jnp
        import numpy as np
        TOP_K = 2
        CAPACITY = 1024
        EPS = 1e-06
        W_SCALE = 0.02

        def _rms(x, w):
            return x * jax.lax.rsqrt(jnp.mean(x * x, axis=-1, keepdims=True) + EPS) * w
        key = jax.random.key(seed)
        ks = jax.random.split(key, 8)
        B, S, H, F, E = (8, 1024, 256, 512, 8)
        F4 = F // 4
        return {'hidden_states': jax.random.normal(ks[0], (B, S, H), jnp.float32), 'Wr': jax.random.normal(ks[1], (H, E), jnp.float32) * W_SCALE, 'norm_w': jnp.ones((E, H), jnp.float32), 'Wg': jax.random.normal(ks[2], (E, H, F), jnp.float32) * W_SCALE, 'Wu': jax.random.normal(ks[3], (E, H, F), jnp.float32) * W_SCALE, 'Wd': jax.random.normal(ks[4], (E, F, H), jnp.float32) * W_SCALE, 'f_norm': jnp.ones((H,), jnp.float32), 'fWg': jax.random.normal(ks[5], (H, F4), jnp.float32) * W_SCALE, 'fWu': jax.random.normal(ks[6], (H, F4), jnp.float32) * W_SCALE, 'fWd': jax.random.normal(ks[7], (F4, H), jnp.float32) * W_SCALE}
    _L0_ffn_all = _L0_ffn_setup()
    _L0_ffn_in = {k: v for k, v in _L0_ffn_all.items() if k in ('Wr', 'norm_w', 'Wg', 'Wu', 'Wd', 'f_norm', 'fWg', 'fWu', 'fWd')}
    del _L0_ffn_all

    def _L1_attn_setup():
        import jax, jax.numpy as jnp
        import numpy as np
        DECAY_MIN = 0.9
        DECAY_MAX = 0.999

        def _reference_tuple_inner(x, Wq, Wk, Wv, Wo, bo, Wg, bg, decay_param):
            B, L, D = x.shape
            M = Wq.shape[1]
            decay = DECAY_MIN + jax.nn.sigmoid(decay_param) * (DECAY_MAX - DECAY_MIN)
            q = x @ Wq
            k = x @ Wk
            v = x @ Wv
            gates = jax.nn.sigmoid(x @ Wg + bg)[..., 0]
            S0 = jnp.zeros((B, M, M), x.dtype)

            def scan_fn(S, inp):
                q_t, k_t, v_t, g_t = inp
                gk = k_t * g_t[:, None]
                gv = v_t * g_t[:, None]
                S = decay * S + gk[:, :, None] * gv[:, None, :]
                out_t = jnp.einsum('bd,bde->be', q_t, S)
                return (S, out_t)
            S_final, outs = jax.lax.scan(scan_fn, S0, (q.transpose(1, 0, 2), k.transpose(1, 0, 2), v.transpose(1, 0, 2), gates.T))
            outs = outs.transpose(1, 0, 2)
            y = outs @ Wo + bo
            return (y, S_final)
        key = jax.random.key(seed)
        ks = jax.random.split(key, 6)
        B, L, D, M = (8, 1024, 256, 64)
        s = 0.02
        return {'x': jax.random.normal(ks[0], (B, L, D), jnp.float32), 'Wq': jax.random.normal(ks[1], (D, M), jnp.float32) * s, 'Wk': jax.random.normal(ks[2], (D, M), jnp.float32) * s, 'Wv': jax.random.normal(ks[3], (D, M), jnp.float32) * s, 'Wo': jax.random.normal(ks[4], (M, D), jnp.float32) * s, 'bo': jnp.zeros((D,), jnp.float32), 'Wg': jax.random.normal(ks[5], (D, 1), jnp.float32) * s, 'bg': jnp.zeros((1,), jnp.float32), 'decay_param': jnp.full((1,), 0.5, jnp.float32)}
    _L1_attn_all = _L1_attn_setup()
    _L1_attn_in = {k: v for k, v in _L1_attn_all.items() if k in ('Wq', 'Wk', 'Wv', 'Wo', 'bo', 'Wg', 'bg', 'decay_param')}
    del _L1_attn_all

    def _L1_xattn_setup():
        import jax, jax.numpy as jnp
        import numpy as np
        B, S, D = (4, 512, 256)
        key = jax.random.key(seed)
        ks = jax.random.split(key, 11)
        scale = 1.0 / np.sqrt(D)
        x = jax.random.normal(ks[0], (B, S, D), jnp.float32)
        y = jax.random.normal(ks[1], (B, S, D), jnp.float32)
        z = jax.random.normal(ks[2], (B, S, D), jnp.float32)
        mask = jnp.broadcast_to(jnp.triu(jnp.ones((S, S), bool), k=1), (B, S, S))
        Wq = jax.random.normal(ks[3], (D, D), jnp.float32) * scale
        bq = jax.random.normal(ks[4], (D,), jnp.float32) * scale
        Wk = jax.random.normal(ks[5], (D, D), jnp.float32) * scale
        bk = jax.random.normal(ks[6], (D,), jnp.float32) * scale
        Wv = jax.random.normal(ks[7], (D, D), jnp.float32) * scale
        bv = jax.random.normal(ks[8], (D,), jnp.float32) * scale
        Wo = jax.random.normal(ks[9], (D, D), jnp.float32) * scale
        bo = jax.random.normal(ks[10], (D,), jnp.float32) * scale
        return {'x': x, 'y': y, 'z': z, 'mask': mask, 'Wq': Wq, 'bq': bq, 'Wk': Wk, 'bk': bk, 'Wv': Wv, 'bv': bv, 'Wo': Wo, 'bo': bo}
    _L1_xattn_all = _L1_xattn_setup()
    _L1_xattn_in = {k: v for k, v in _L1_xattn_all.items() if k in ('Wq', 'bq', 'Wk', 'bk', 'Wv', 'bv', 'Wo', 'bo')}
    del _L1_xattn_all

    def _L1_ffn_setup():
        import jax, jax.numpy as jnp
        import numpy as np
        THRESHOLD = 0.1
        key = jax.random.key(seed)
        k1, k2, k3 = jax.random.split(key, 3)
        B, S, D, E = (4, 1024, 256, 8)
        inputs = jax.random.normal(k1, (B, S, D), dtype=jnp.float32)
        gate_w = jax.random.normal(k2, (D, E), dtype=jnp.float32) * 0.02
        gate_b = jnp.zeros((E,), dtype=jnp.float32)
        expert_w = jax.random.normal(k3, (E, D, D), dtype=jnp.float32) * 0.02
        expert_b = jnp.zeros((E, D), dtype=jnp.float32)
        return {'inputs': inputs, 'gate_w': gate_w, 'gate_b': gate_b, 'expert_w': expert_w, 'expert_b': expert_b}
    _L1_ffn_all = _L1_ffn_setup()
    _L1_ffn_in = {k: v for k, v in _L1_ffn_all.items() if k in ('gate_w', 'gate_b', 'expert_w', 'expert_b')}
    del _L1_ffn_all
    return {'x': x, 'ctx_1024': ctx_1024, 'mask_BxSxS2_bk1': mask_BxSxS2_bk1, 'L0_attn_norm_weight': _L0_attn_in['norm_weight'], 'L0_attn_router_w': _L0_attn_in['router_w'], 'L0_attn_router_b': _L0_attn_in['router_b'], 'L0_attn_w_hg': _L0_attn_in['w_hg'], 'L0_attn_w_out': _L0_attn_in['w_out'], 'L0_xattn_Wq': _L0_xattn_in['Wq'], 'L0_xattn_bq': _L0_xattn_in['bq'], 'L0_xattn_Wk': _L0_xattn_in['Wk'], 'L0_xattn_bk': _L0_xattn_in['bk'], 'L0_xattn_Wv': _L0_xattn_in['Wv'], 'L0_xattn_bv': _L0_xattn_in['bv'], 'L0_xattn_Wo': _L0_xattn_in['Wo'], 'L0_xattn_bo': _L0_xattn_in['bo'], 'L0_ffn_Wr': _L0_ffn_in['Wr'], 'L0_ffn_norm_w': _L0_ffn_in['norm_w'], 'L0_ffn_Wg': _L0_ffn_in['Wg'], 'L0_ffn_Wu': _L0_ffn_in['Wu'], 'L0_ffn_Wd': _L0_ffn_in['Wd'], 'L0_ffn_f_norm': _L0_ffn_in['f_norm'], 'L0_ffn_fWg': _L0_ffn_in['fWg'], 'L0_ffn_fWu': _L0_ffn_in['fWu'], 'L0_ffn_fWd': _L0_ffn_in['fWd'], 'L1_attn_Wq': _L1_attn_in['Wq'], 'L1_attn_Wk': _L1_attn_in['Wk'], 'L1_attn_Wv': _L1_attn_in['Wv'], 'L1_attn_Wo': _L1_attn_in['Wo'], 'L1_attn_bo': _L1_attn_in['bo'], 'L1_attn_Wg': _L1_attn_in['Wg'], 'L1_attn_bg': _L1_attn_in['bg'], 'L1_attn_decay_param': _L1_attn_in['decay_param'], 'L1_xattn_Wq': _L1_xattn_in['Wq'], 'L1_xattn_bq': _L1_xattn_in['bq'], 'L1_xattn_Wk': _L1_xattn_in['Wk'], 'L1_xattn_bk': _L1_xattn_in['bk'], 'L1_xattn_Wv': _L1_xattn_in['Wv'], 'L1_xattn_bv': _L1_xattn_in['bv'], 'L1_xattn_Wo': _L1_xattn_in['Wo'], 'L1_xattn_bo': _L1_xattn_in['bo'], 'L1_ffn_gate_w': _L1_ffn_in['gate_w'], 'L1_ffn_gate_b': _L1_ffn_in['gate_b'], 'L1_ffn_expert_w': _L1_ffn_in['expert_w'], 'L1_ffn_expert_b': _L1_ffn_in['expert_b']}

def reference(x, ctx_1024, mask_BxSxS2_bk1, L0_attn_norm_weight, L0_attn_router_w, L0_attn_router_b, L0_attn_w_hg, L0_attn_w_out, L0_xattn_Wq, L0_xattn_bq, L0_xattn_Wk, L0_xattn_bk, L0_xattn_Wv, L0_xattn_bv, L0_xattn_Wo, L0_xattn_bo, L0_ffn_Wr, L0_ffn_norm_w, L0_ffn_Wg, L0_ffn_Wu, L0_ffn_Wd, L0_ffn_f_norm, L0_ffn_fWg, L0_ffn_fWu, L0_ffn_fWd, L1_attn_Wq, L1_attn_Wk, L1_attn_Wv, L1_attn_Wo, L1_attn_bo, L1_attn_Wg, L1_attn_bg, L1_attn_decay_param, L1_xattn_Wq, L1_xattn_bq, L1_xattn_Wk, L1_xattn_bk, L1_xattn_Wv, L1_xattn_bv, L1_xattn_Wo, L1_xattn_bo, L1_ffn_gate_w, L1_ffn_gate_b, L1_ffn_expert_w, L1_ffn_expert_b):
    import jax
    import jax.numpy as jnp

    def _L0_attn_ref(inputs, norm_weight, router_w, router_b, w_hg, w_out):
        import jax, jax.numpy as jnp
        import numpy as np
        EPS = 1e-06

        def _log_g(x):
            return jnp.where(x >= 0, jnp.log(jax.nn.relu(x) + 0.5), -jax.nn.softplus(-x))

        def _reference_tuple_inner(inputs, norm_weight, router_w, router_b, w_hg, w_out):
            D = inputs.shape[-1]
            x = inputs * jax.lax.rsqrt(jnp.mean(inputs * inputs, axis=-1, keepdims=True) + EPS) * norm_weight
            probs = jax.nn.softmax(jnp.mean(x, axis=1) @ router_w.T + router_b, axis=-1)
            W_hg = jnp.einsum('be,ekd->bkd', probs, w_hg)
            W_out = jnp.einsum('be,eod->bod', probs, w_out)
            hg = jnp.einsum('bsd,bkd->bsk', x, W_hg)
            hidden, gate = (hg[..., :D], hg[..., D:])
            log_coeffs = -jax.nn.softplus(gate)
            log_values = -jax.nn.softplus(-gate) + _log_g(hidden)
            a_star = jnp.cumsum(log_coeffs, axis=1)
            log_h = a_star + jax.lax.cumlogsumexp(log_values - a_star, axis=1)
            h = jnp.exp(log_h)
            new_state = h[:, -1:]
            out = jnp.einsum('bsk,bok->bso', h, W_out)
            aux_loss = jnp.zeros((), inputs.dtype)
            return (out + inputs, new_state, aux_loss)
        return _reference_tuple_inner(inputs, norm_weight, router_w, router_b, w_hg, w_out)[0]

    def _L0_xattn_ref(q, k, v, Wq, bq, Wk, bk, Wv, bv, Wo, bo):
        import jax, jax.numpy as jnp
        import numpy as np
        import math
        HEADS = 16
        D_MODEL = 256
        D_K = D_MODEL // HEADS
        PRUNE_KEEP = 0.9

        def _split_heads(x, B):
            return x.reshape(B, -1, HEADS, D_K).transpose(0, 2, 1, 3)

        def _pruned_attention(q, k, v):
            B, H, S, _ = q.shape
            scores = jnp.einsum('bhqd,bhkd->bhqk', q, k) / math.sqrt(D_K)
            scores = jax.nn.softmax(scores, axis=-1)
            keep = int(S * PRUNE_KEEP)
            col_sum = jnp.sum(scores, axis=2)
            _, idx = jax.lax.top_k(col_sum, keep)
            mask = jnp.zeros((B, H, S), scores.dtype).at[jnp.arange(B)[:, None, None], jnp.arange(H)[None, :, None], idx].set(1.0)
            pruned = scores * mask[:, :, None, :]
            return jnp.einsum('bhqk,bhkd->bhqd', pruned, v)
        B = q.shape[0]
        qh = _split_heads(q @ Wq.T + bq, B)
        kh = _split_heads(k @ Wk.T + bk, B)
        vh = _split_heads(v @ Wv.T + bv, B)
        out = _pruned_attention(qh, kh, vh)
        concat = out.transpose(0, 2, 1, 3).reshape(B, -1, D_MODEL)
        return concat @ Wo.T + bo

    def _L0_ffn_ref(hidden_states, Wr, norm_w, Wg, Wu, Wd, f_norm, fWg, fWu, fWd):
        import jax, jax.numpy as jnp
        import numpy as np
        TOP_K = 2
        CAPACITY = 1024
        EPS = 1e-06
        W_SCALE = 0.02

        def _rms(x, w):
            return x * jax.lax.rsqrt(jnp.mean(x * x, axis=-1, keepdims=True) + EPS) * w
        B, S, H = hidden_states.shape
        E = Wr.shape[1]
        N = B * S
        x = hidden_states.reshape(N, H)
        probs = jax.nn.softmax(x @ Wr, axis=-1)
        w_topk, e_topk = jax.lax.top_k(probs, TOP_K)
        e_flat = e_topk.reshape(-1)
        oh = jax.nn.one_hot(e_flat, E, dtype=jnp.int32)
        pos = jnp.take_along_axis(jnp.cumsum(oh, axis=0) - 1, e_flat[:, None], axis=1)[:, 0]
        keep = pos < CAPACITY
        x_rep = jnp.repeat(x, TOP_K, axis=0)
        buf = jnp.zeros((E, CAPACITY, H), x.dtype).at[e_flat, pos].set(x_rep, mode='drop')
        h = _rms(buf, norm_w[:, None, :])
        gate = jax.nn.gelu(jnp.einsum('ech,ehf->ecf', h, Wg), approximate=False)
        up = jnp.einsum('ech,ehf->ecf', h, Wu)
        buf_out = jnp.einsum('ecf,efh->ech', gate * up, Wd) + buf
        exp_out = buf_out[e_flat, jnp.minimum(pos, CAPACITY - 1)]
        contrib = w_topk.reshape(-1)[:, None] * exp_out * keep[:, None].astype(x.dtype)
        combined = x + contrib.reshape(N, TOP_K, H).sum(axis=1)
        overflow = (~keep).reshape(N, TOP_K).any(axis=1)
        fh = _rms(x, f_norm)
        fout = jax.nn.gelu(fh @ fWg, approximate=False) * (fh @ fWu) @ fWd + x
        out = jnp.where(overflow[:, None], fout, combined)
        return out.reshape(B, S, H)

    def _L1_attn_ref(x, Wq, Wk, Wv, Wo, bo, Wg, bg, decay_param):
        import jax, jax.numpy as jnp
        import numpy as np
        DECAY_MIN = 0.9
        DECAY_MAX = 0.999

        def _reference_tuple_inner(x, Wq, Wk, Wv, Wo, bo, Wg, bg, decay_param):
            B, L, D = x.shape
            M = Wq.shape[1]
            decay = DECAY_MIN + jax.nn.sigmoid(decay_param) * (DECAY_MAX - DECAY_MIN)
            q = x @ Wq
            k = x @ Wk
            v = x @ Wv
            gates = jax.nn.sigmoid(x @ Wg + bg)[..., 0]
            S0 = jnp.zeros((B, M, M), x.dtype)

            def scan_fn(S, inp):
                q_t, k_t, v_t, g_t = inp
                gk = k_t * g_t[:, None]
                gv = v_t * g_t[:, None]
                S = decay * S + gk[:, :, None] * gv[:, None, :]
                out_t = jnp.einsum('bd,bde->be', q_t, S)
                return (S, out_t)
            S_final, outs = jax.lax.scan(scan_fn, S0, (q.transpose(1, 0, 2), k.transpose(1, 0, 2), v.transpose(1, 0, 2), gates.T))
            outs = outs.transpose(1, 0, 2)
            y = outs @ Wo + bo
            return (y, S_final)
        return _reference_tuple_inner(x, Wq, Wk, Wv, Wo, bo, Wg, bg, decay_param)[0]

    def _L1_xattn_ref(x, y, z, mask, Wq, bq, Wk, bk, Wv, bv, Wo, bo):
        import jax, jax.numpy as jnp
        import numpy as np
        B, S, D = (4, 512, 256)
        Q = jnp.einsum('bsd,ed->bse', x, Wq) + bq
        K = jnp.einsum('bsd,ed->bse', y, Wk) + bk
        V = jnp.einsum('bsd,ed->bse', z, Wv) + bv
        sim = jnp.einsum('bqd,bkd->bqk', Q, K)
        sim = jnp.where(mask, jnp.float32(-1000000000.0), sim)
        attn = jax.nn.softmax(sim, axis=-1)
        out = jnp.einsum('bqk,bkd->bqd', attn, V)
        return jnp.einsum('bsd,ed->bse', out, Wo) + bo

    def _L1_ffn_ref(inputs, gate_w, gate_b, expert_w, expert_b):
        import jax, jax.numpy as jnp
        import numpy as np
        THRESHOLD = 0.1
        d = inputs.shape[-1]
        x = inputs.reshape(-1, d)
        gate_logits = jax.nn.softmax(x @ gate_w + gate_b, axis=-1)
        selected = (gate_logits >= THRESHOLD).astype(x.dtype)
        weights = gate_logits * selected
        wsum = jnp.sum(weights, axis=-1, keepdims=True)
        weights = weights / jnp.where(wsum == 0, jnp.ones_like(wsum), wsum)
        E = expert_w.shape[0]
        out = jnp.zeros((x.shape[0], expert_w.shape[-1]), dtype=x.dtype)
        for e in range(E):
            out = out + weights[:, e:e + 1] * (x @ expert_w[e] + expert_b[e])
        return out.reshape(*inputs.shape[:-1], out.shape[-1])
    x = _layernorm(x + _L0_attn_ref(x, L0_attn_norm_weight, L0_attn_router_w, L0_attn_router_b, L0_attn_w_hg, L0_attn_w_out), axis=-1)
    x = _layernorm(x + _L0_xattn_ref(x, ctx_1024, ctx_1024, L0_xattn_Wq, L0_xattn_bq, L0_xattn_Wk, L0_xattn_bk, L0_xattn_Wv, L0_xattn_bv, L0_xattn_Wo, L0_xattn_bo), axis=-1)
    x = _layernorm(x + _L0_ffn_ref(x, L0_ffn_Wr, L0_ffn_norm_w, L0_ffn_Wg, L0_ffn_Wu, L0_ffn_Wd, L0_ffn_f_norm, L0_ffn_fWg, L0_ffn_fWu, L0_ffn_fWd), axis=-1)
    x = _layernorm(x + _L1_attn_ref(x, L1_attn_Wq, L1_attn_Wk, L1_attn_Wv, L1_attn_Wo, L1_attn_bo, L1_attn_Wg, L1_attn_bg, L1_attn_decay_param), axis=-1)
    x = _layernorm(x + _L1_xattn_ref(x, ctx_1024, ctx_1024, mask_BxSxS2_bk1, L1_xattn_Wq, L1_xattn_bq, L1_xattn_Wk, L1_xattn_bk, L1_xattn_Wv, L1_xattn_bv, L1_xattn_Wo, L1_xattn_bo), axis=-1)
    x = _layernorm(x + _L1_ffn_ref(x, L1_ffn_gate_w, L1_ffn_gate_b, L1_ffn_expert_w, L1_ffn_expert_b), axis=-1)
    return x

_drawn_inputs = setup_inputs


def setup_inputs(seed=0):
    import zlib

    import numpy as np

    out = dict(_drawn_inputs(seed))
    spreads = {'L0_attn_norm_weight': (1.0, 0.6),
     'L0_attn_router_b': (0.0, 0.409),
     'L0_xattn_bq': (0.0, 0.707),
     'L0_xattn_bk': (0.0, 0.8),
     'L0_xattn_bv': (0.0, 0.1),
     'L0_xattn_bo': (0.0, 0.1),
     'L0_ffn_norm_w': (1.0, 0.6),
     'L0_ffn_f_norm': (1.0, 0.6),
     'L1_attn_bo': (0.0, 0.1),
     'L1_ffn_gate_b': (0.0, 0.1),
     'L1_ffn_expert_b': (0.0, 0.1)}
    factors = {'L0_attn_router_w': 5.287,
     'L0_xattn_Wq': 8.0,
     'L0_xattn_Wk': 5.449,
     'L0_ffn_Wr': 7.743,
     'L0_ffn_Wg': 8.0,
     'L0_ffn_Wu': 8.0,
     'L0_ffn_Wd': 8.0,
     'L0_ffn_fWg': 8.0,
     'L0_ffn_fWu': 8.0,
     'L0_ffn_fWd': 8.0,
     'L1_xattn_bk': 8.0}
    for name, (base, spread) in spreads.items():
        noise = np.random.default_rng([zlib.crc32(name.encode()), seed]).standard_normal(out[name].shape)
        drawn = base * np.exp(spread * noise) if base else spread * noise
        out[name] = jnp.asarray(drawn.astype(out[name].dtype))
    for name, factor in factors.items():
        out[name] = (out[name] * factor).astype(out[name].dtype)
    return out
```

```python
from contextlib import ExitStack

import concourse.bass as bass
from concourse import mybir

F32 = mybir.dt.float32
BF16 = mybir.dt.bfloat16
U8 = mybir.dt.uint8
U32 = mybir.dt.uint32
ALU = mybir.AluOpType
ACT = mybir.ActivationFunctionType
AX = mybir.AxisListType

P = 128
B = 8
S = 512
D = 256
T = S // P
DH = D // P
E = 8


class Room:

    def __init__(self, nc, ctx, stage):
        self.nc, self.ctx, self.stage, self.sems = nc, ctx, stage, []
        ctx.callback(self.clear)

    def clear(self):
        self.nc.clear_and_free_semaphores(self.sems)
        self.nc.all_engine_barrier()

    def sb(self, name, shape, dt=F32):
        return self.ctx.enter_context(self.nc.sbuf_tensor(f"{self.stage}_{name}", shape, dt))

    def ps(self, name, shape, dt=F32):
        return self.ctx.enter_context(self.nc.psum_tensor(f"{self.stage}_{name}", shape, dt))

    def sem(self, name):
        self.sems.append(self.nc.alloc_semaphore(f"{self.stage}_{name}"))
        return self.sems[-1]


def tok(ap):
    return ap.rearrange("(t p) n -> p t n", p=P)


def apart(eng, past):
    eng.sem_inc(past, 1)


def layernorm(dve, z, st, mv, ve, rstd, out, b, i, steps, z_up, rstd_up, out_up, out_free, past_dve):
    dve.wait_ge(steps, b * 3 + 1)
    for t in range(T):
        ins = dve.bn_stats(st[:, t, :], z[:, t, :])
    ins.then_inc(steps, 1)
    dve.wait_ge(steps, b * 3 + 2)
    apart(dve, past_dve)
    for t in range(T):
        ins = dve.bn_aggr(mv[:, t, :], st[:, t, :])
    ins.then_inc(steps, 1)
    dve.wait_ge(steps, b * 3 + 3)
    dve.tensor_scalar(ve[:, :], mv[:, :, 1], 1e-5, None, ALU.add).then_inc(z_up, 1)
    dve.wait_ge(rstd_up, b + 1)
    dve.wait_ge(out_free, i * 16 + 16)
    for t in range(T):
        ins = dve.tensor_scalar(out[:, t, :], z[:, t, :], mv[:, t, 0:1], rstd[:, t:t + 1], ALU.subtract, ALU.mult)
    ins.then_inc(out_up, 1)



def stage_mix(nc, a, w_all):
    KC = P // E
    C = 4
    G = 3 * D // (KC * C)
    with ExitStack() as ctx:
        r = Room(nc, ctx, "mix")
        x_in = [r.sb(f"x{u}", [P, T, D]) for u in range(2)]
        junk = [r.sb(f"junk{u}", [P, T, D], BF16) for u in range(2)]
        ssq = [r.sb(f"ssq{u}", [P, T]) for u in range(2)]
        msq = [r.sb(f"msq{u}", [P, T]) for u in range(2)]
        inv = [r.sb(f"inv{u}", [P, T]) for u in range(2)]
        mhalf = r.sb("mhalf", [P, T])
        meanT = r.sb("meanT", [P, B, DH])
        nw = r.sb("nw", [P, DH])
        rwT = r.sb("rwT", [P, DH, E])
        rb = r.sb("rb", [B, E])
        lg, ex, pr = (r.sb(n, [B, E]) for n in ("lg", "ex", "pr"))
        nmax, esum, erec = (r.sb(n, [B, 1]) for n in ("nmax", "esum", "erec"))
        prT = r.sb("prT", [E, B])
        prP = r.sb("prP", [P, B, 1])
        ident = r.sb("ident", [P, P])
        sel = r.sb("sel", [E, E, KC])
        mask = r.sb("mask", [P, KC])
        blocks = r.sb("blocks", [P, B, KC])
        chunk = [r.sb(f"chunk{u}", [P, C, D]) for u in range(2)]
        ps_mean = r.ps("ps_mean", [P, B, DH])
        ps_small = r.ps("ps_small", [P, 3, 8])
        ps_w = [[r.ps(f"ps_w{u}{h}", [P, C, B, KC]) for h in range(DH)] for u in range(2)]
        c_ld = r.sem("c_ld")
        x_ld, w_ld = [r.sem(f"x_ld{u}") for u in range(2)], [r.sem(f"w_ld{u}") for u in range(2)]
        ssq_up, msq_up, inv_up, mean_up = (r.sem(n) for n in ("ssq_up", "msq_up", "inv_up", "mean_up"))
        const_up, soft_v, soft_s, soft_t = (r.sem(n) for n in ("const_up", "soft_v", "soft_s", "soft_t"))
        mixed, out_v, out_s = r.sem("mixed"), r.sem("out_v"), r.sem("out_s")
        zeros = r.sb("zeros", [P, 2048])
        zero_up, zero_st = r.sem("zero_up"), r.sem("zero_st")
        block = ctx.enter_context(nc.Block())

        @block.sync
        def _(sp):
            with nc.allow_non_contiguous_dma(reason="256 weights"):
                sp.dma_start(nw[:, :], a["L0_attn_norm_weight"].rearrange("(h p) -> p h", p=P)).then_inc(c_ld, 16)
            sp.dma_start(rwT[:, :, :], a["L0_router_wT"].rearrange("(h p) e -> p h e", p=P)).then_inc(c_ld, 16)
            sp.dma_start(rb[:, :], a["L0_attn_router_b"].rearrange("(o e) -> o e", o=1).to_broadcast([B, E])).then_inc(c_ld, 16)
            with sp.Fori(0, B // 2) as i:
                for u in range(2):
                    b = 2 * i + u
                    sp.wait_ge(mean_up, b + 1)
                    sp.dma_start(x_in[u][:, :, :], tok(a["x"][b])).then_inc(x_ld[u], 16)
            with sp.Fori(0, G // 2) as i:
                for u in range(2):
                    g = 2 * i + u
                    sp.wait_ge(mixed, g + 1)
                    sp.dma_start(chunk[u][:, :, :], a["L0_mix_w"][g].rearrange("p (c d) -> p c d", c=C)).then_inc(w_ld[u], 16)

        @block.scalar
        def _(act):
            with act.Fori(0, B // 2) as i:
                for u in range(2):
                    b = 2 * i + u
                    act.wait_ge(x_ld[u], i * 16 + 16)
                    act.wait_ge(msq_up, b + 1)
                    for t in range(T):
                        ins = act.activation(junk[u][:, t, :], x_in[u][:, t, :], ACT.Square, accum_out=ssq[u][:, t:t + 1])
                    ins.then_inc(ssq_up, 1)
            act.wait_ge(zero_up, 1)
            buf = a["buf"].rearrange("(n p r) d -> n p (r d)", p=P, r=2048 // D)
            for n in range(buf.shape[0]):
                act.dma_start(buf[n], zeros[:, :]).then_inc(zero_st, 16)
            act.wait_ge(soft_v, 4)
            act.activation(ex[:, :], lg[:, :], ACT.Exp, bias=nmax[:, :], accum_out=esum[:, :]).then_inc(soft_s, 1)
            act.sem_inc(out_s, 2)
            with act.Fori(0, G // 2) as i:
                for u in range(2):
                    g = 2 * i + u
                    act.wait_ge(mixed, g + 3)
                    act.activation(w_all[:, :, 1, bass.ds(g * (C * KC), C * KC)].rearrange("p b (c k) -> p b c k", c=C),
                                   ps_w[u][1][:, :, :, :].rearrange("p c b k -> p b c k"), ACT.Copy).then_inc(out_s, 1)
            act.wait_ge(zero_st, 16 * buf.shape[0])

        @block.gpsimd
        def _(pool):
            pool.memset(mhalf[:, :], -0.5).then_inc(const_up, 1)
            pool.memset(ident[:, :], 0.0).then_inc(const_up, 1)
            pool.memset(sel[:, :, :], 1.0).then_inc(const_up, 1)
            pool.wait_ge(const_up, 3)
            pool.affine_select(out=ident[:, :], in_=ident[:, :], compare_op=ALU.not_equal, fill=1.0, base=0,
                               pattern=[[-1, P]], channel_multiplier=1).then_inc(const_up, 1)
            pool.affine_select(out=sel[:, :, :], in_=sel[:, :, :], compare_op=ALU.is_equal, fill=0.0, base=0,
                               pattern=[[-1, E], [0, KC]], channel_multiplier=1).then_inc(const_up, 1)
            pool.memset(zeros[:, :], 0.0).then_inc(zero_up, 1)
            pool.sem_inc(inv_up, 2)
            with pool.Fori(0, B // 2) as i:
                for u in range(2):
                    b = 2 * i + u
                    pool.wait_ge(msq_up, b + 3)
                    pool.wait_ge(mean_up, b + 1)
                    pool.tensor_tensor(inv[u][:, :], msq[u][:, :], mhalf[:, :], ALU.pow).then_inc(inv_up, 1)

        @block.vector
        def _(dve):
            dve.wait_ge(const_up, 5)
            dve.tensor_reduce(mask[:, :], ident[:, :].rearrange("p (e k) -> p k e", e=E), AX.X, ALU.add).then_inc(soft_v, 1)
            dve.sem_inc(msq_up, 2)
            with dve.Fori(0, B // 2) as i:
                for u in range(2):
                    b = 2 * i + u
                    dve.wait_ge(ssq_up, b + 1)
                    dve.wait_ge(inv_up, b + 1)
                    dve.tensor_scalar(msq[u][:, :], ssq[u][:, :], 1.0 / D, 1e-6, ALU.mult, ALU.add).then_inc(msq_up, 1)
            dve.wait_ge(mean_up, 2 + B)
            dve.wait_ge(c_ld, 48)
            for h in range(DH):
                ins = dve.tensor_scalar(meanT[:, :, h], ps_mean[:, :, h], nw[:, h:h + 1], 1.0 / S, ALU.mult, ALU.mult)
            ins.then_inc(soft_v, 1)
            dve.wait_ge(soft_t, 1)
            dve.tensor_tensor(lg[:, :], ps_small[0:B, 0, 0:E], rb[:, :], ALU.add).then_inc(soft_v, 1)
            dve.wait_ge(soft_v, 3)
            dve.tensor_reduce(nmax[:, :], lg[:, :], AX.X, ALU.max, negate=True).then_inc(soft_v, 1)
            dve.wait_ge(soft_s, 1)
            dve.reciprocal(erec[:, :], esum[:, :]).then_inc(soft_v, 1)
            dve.wait_ge(soft_v, 5)
            dve.tensor_scalar(pr[:, :], ex[:, :], erec[:, :], None, ALU.mult).then_inc(soft_v, 1)
            dve.wait_ge(soft_t, 2)
            dve.tensor_copy(prT[:, :], ps_small[0:E, 1, 0:B]).then_inc(soft_v, 1)
            dve.wait_ge(soft_t, 3)
            dve.tensor_copy(prP[:, :, 0], ps_small[:, 2, 0:B]).then_inc(soft_v, 1)
            dve.wait_ge(soft_v, 8)
            dve.tensor_tensor(blocks[:, :, :], prP[:, :, :].to_broadcast([P, B, KC]),
                              mask[:, :].rearrange("p (o k) -> p o k", o=1).to_broadcast([P, B, KC]), ALU.mult).then_inc(soft_v, 1)
            dve.sem_inc(out_v, 2)
            with dve.Fori(0, G // 2) as i:
                for u in range(2):
                    g = 2 * i + u
                    dve.wait_ge(mixed, g + 3)
                    dve.tensor_copy(w_all[:, :, 0, bass.ds(g * (C * KC), C * KC)].rearrange("p b (c k) -> p b c k", c=C),
                                    ps_w[u][0][:, :, :, :].rearrange("p c b k -> p b c k")).then_inc(out_v, 1)

        @block.tensor
        def _(pe):
            pe.sem_inc(mean_up, 2)
            with pe.Fori(0, B // 2) as i:
                for u in range(2):
                    b = 2 * i + u
                    pe.wait_ge(inv_up, b + 3)
                    for h in range(DH):
                        for t in range(T):
                            ins = pe.matmul(ps_mean[:, bass.ds(b, 1), h], x_in[u][:, t, h * P:(h + 1) * P], inv[u][:, t:t + 1],
                                            start=(t == 0), stop=(t == T - 1))
                    ins.then_inc(mean_up, 1)
            pe.wait_ge(soft_v, 2)
            for h in range(DH):
                ins = pe.matmul(ps_small[0:B, 0, 0:E], meanT[:, :, h], rwT[:, h, :], start=(h == 0), stop=(h == DH - 1))
            ins.then_inc(soft_t, 1)
            pe.wait_ge(soft_v, 6)
            pe.transpose(ps_small[0:E, 1, 0:B], pr[:, :], ident[0:B, 0:B]).then_inc(soft_t, 1)
            pe.wait_ge(soft_v, 7)
            pe.matmul(ps_small[:, 2, 0:B], sel[:, :, :].rearrange("p e k -> p (e k)"), prT[:, :], start=True, stop=True).then_inc(soft_t, 1)
            pe.wait_ge(soft_v, 9)
            pe.sem_inc(mixed, 2)
            with pe.Fori(0, G // 2) as i:
                for u in range(2):
                    g = 2 * i + u
                    pe.wait_ge(w_ld[u], i * 16 + 16)
                    pe.wait_ge(out_v, g + 1)
                    pe.wait_ge(out_s, g + 1)
                    for h in range(DH):
                        for c in range(C):
                            ins = pe.matmul(ps_w[u][h][:, c, :, :].rearrange("p b k -> p (b k)"), chunk[u][:, c, h * P:(h + 1) * P],
                                            blocks[:, :, :].rearrange("p b k -> p (b k)"), start=True, stop=True)
                    ins.then_inc(mixed, 1)


def stage_rec(nc, a, w_all):
    NK = 2 * DH
    with ExitStack() as ctx:
        r = Room(nc, ctx, "rec")
        x_in = [r.sb(f"x{u}", [P, T, D]) for u in range(2)]
        w = [r.sb(f"w{u}", [P, DH, 3 * D]) for u in range(2)]
        xn = [r.sb(f"xn{u}", [P, T, D]) for u in range(2)]
        xnT = [r.sb(f"xnT{u}", [P, DH, S]) for u in range(2)]
        junk = [r.sb(f"junk{u}", [P, T, D], BF16) for u in range(2)]
        ssq = [r.sb(f"ssq{u}", [P, T]) for u in range(2)]
        msq = [r.sb(f"msq{u}", [P, T]) for u in range(2)]
        inv = [r.sb(f"inv{u}", [P, T]) for u in range(2)]
        mhalf = r.sb("mhalf", [P, T])
        nw = r.sb("nw", [P, DH])
        keep = [r.sb(f"keep{u}", [P, DH, S]) for u in range(2)]
        take = [r.sb(f"take{u}", [P, DH, S]) for u in range(2)]
        val = [r.sb(f"val{u}", [P, DH, S]) for u in range(2)]
        h = [r.sb(f"h{u}", [P, DH, S]) for u in range(2)]
        z = r.sb("z", [P, T, D])
        st = r.sb("st", [P, T, 6])
        mv = r.sb("mv", [P, T, 2])
        ve = r.sb("ve", [P, T])
        rstd = r.sb("rstd", [P, T])
        xo = [r.sb(f"xo{u}", [P, T, D]) for u in range(2)]
        ident = r.sb("ident", [P, P])
        ps_t = r.ps("ps_t", [P, DH, S])
        ps_h = r.ps("ps_h", [P, DH, S])
        ps_g = r.ps("ps_g", [P, DH, S])
        ps_o = r.ps("ps_o", [P, T, D])
        c_ld, const_up = r.sem("c_ld"), r.sem("const_up")
        ld, stored = [r.sem(f"ld{u}") for u in range(2)], [r.sem(f"stored{u}") for u in range(2)]
        ssq_up, msq_up, inv_up, xn_up, t_up, xnT_up = (r.sem(n) for n in ("ssq_up", "msq_up", "inv_up", "xn_up", "t_up", "xnT_up"))
        hg_up, sig_up, val_up, val2, h_up, o_up, z_up, rstd_up, xo_up = (r.sem(n) for n in
            ("hg_up", "sig_up", "val_up", "val2", "h_up", "o_up", "z_up", "rstd_up", "xo_up"))
        steps, past_dve = r.sem("steps"), r.sem("past_dve")
        block = ctx.enter_context(nc.Block())

        @block.sync
        def _(sp):
            with nc.allow_non_contiguous_dma(reason="256 weights"):
                sp.dma_start(nw[:, :], a["L0_attn_norm_weight"].rearrange("(h p) -> p h", p=P)).then_inc(c_ld, 16)
            def load(b, u):
                sp.dma_start(x_in[u][:, :, :], tok(a["x"][b])).then_inc(ld[u], 16)
                sp.dma_start(w[u][:, :, :], w_all[:, bass.ds(b, 1), :, :].rearrange("p o h n -> p (o h) n")).then_inc(ld[u], 16)

            def store(b, u):
                sp.wait_ge(xo_up, b + 3)
                sp.dma_start(tok(a["x1"][b]), xo[u][:, :, :]).then_inc(stored[u], 16)

            for u in range(2):
                sp.sem_inc(stored[u], 16)
                load(u, u)
            with sp.Fori(0, B // 2 - 1) as i:
                for u in range(2):
                    store(2 * i + u, u)
                    load(2 * i + u + 2, u)
            for u in range(2):
                store(B - 2 + u, u)
            for u in range(2):
                sp.wait_ge(stored[u], 16 + 8 * B)

        @block.gpsimd
        def _(pool):
            pool.memset(mhalf[:, :], -0.5).then_inc(const_up, 1)
            pool.memset(ident[:, :], 0.0).then_inc(const_up, 1)
            pool.wait_ge(const_up, 2)
            pool.affine_select(out=ident[:, :], in_=ident[:, :], compare_op=ALU.not_equal, fill=1.0, base=0,
                               pattern=[[-1, P]], channel_multiplier=1).then_inc(const_up, 1)
            pool.sem_inc(inv_up, 2)

            def front(b, u):
                pool.wait_ge(msq_up, b + 3)
                pool.wait_ge(xn_up, b + 1)
                pool.tensor_tensor(inv[u][:, :], msq[u][:, :], mhalf[:, :], ALU.pow).then_inc(inv_up, 1)

            with pool.Fori(0, B // 2) as i:
                for u in range(2):
                    b = 2 * i + u
                    front(b, u)
                    pool.wait_ge(z_up, b + 1)
                    pool.tensor_tensor(rstd[:, :], ve[:, :], mhalf[:, :], ALU.pow).then_inc(rstd_up, 1)

        @block.scalar
        def _(act):
            act.wait_ge(c_ld, 16)
            act.sem_inc(sig_up, 1)
            act.sem_inc(xnT_up, 1)
            with act.Fori(0, B // 2) as i:
                for u in range(2):
                    b = 2 * i + u
                    act.wait_ge(ld[u], i * 32 + 32)
                    act.wait_ge(msq_up, b + 1)
                    for t in range(T):
                        ins = act.activation(junk[u][:, t, :], x_in[u][:, t, :], ACT.Square, accum_out=ssq[u][:, t:t + 1])
                    ins.then_inc(ssq_up, 1)
                    act.wait_ge(t_up, b + 1)
                    for k in range(DH):
                        ins = act.activation(xnT[u][:, k, :], ps_t[:, k, :], ACT.Copy, scale=nw[:, k:k + 1])
                    ins.then_inc(xnT_up, 1)
                    act.wait_ge(hg_up, b + 1)
                    act.wait_ge(h_up, b + 1)
                    act.activation(val[u][:, :, :], ps_h[:, :, :], ACT.Sigmoid).then_inc(sig_up, 1)
                    act.activation(take[u][:, :, :], ps_g[:, :, :], ACT.Sigmoid).then_inc(sig_up, 1)
                    act.activation(keep[u][:, :, :], ps_g[:, :, :], ACT.Sigmoid, scale=-1.0).then_inc(sig_up, 1)

        @block.vector
        def _(dve):
            dve.sem_inc(msq_up, 2)
            dve.sem_inc(xn_up, 2)
            dve.sem_inc(h_up, 2)
            dve.sem_inc(xo_up, 2)
            with dve.Fori(0, B // 2) as i:
                for u in range(2):
                    b = 2 * i + u
                    dve.wait_ge(ssq_up, b + 1)
                    dve.wait_ge(inv_up, b + 1)
                    dve.tensor_scalar(msq[u][:, :], ssq[u][:, :], 1.0 / D, 1e-6, ALU.mult, ALU.add).then_inc(msq_up, 1)
                    dve.wait_ge(inv_up, b + 3)
                    for t in range(T):
                        ins = dve.tensor_scalar(xn[u][:, t, :], x_in[u][:, t, :], inv[u][:, t:t + 1], None, ALU.mult)
                    ins.then_inc(xn_up, 1)
                    dve.wait_ge(sig_up, b * 3 + 2)
                    dve.scalar_tensor_tensor(val[u][:, :, :], ps_h[:, :, :], 0.5, val[u][:, :, :], ALU.add, ALU.max).then_inc(val_up, 1)
                    dve.wait_ge(val_up, b + 1)
                    dve.wait_ge(sig_up, b * 3 + 3)
                    dve.tensor_tensor(val[u][:, :, :], val[u][:, :, :], take[u][:, :, :], ALU.mult).then_inc(val2, 1)
                    dve.wait_ge(val2, b + 1)
                    dve.wait_ge(sig_up, b * 3 + 4)
                    for k in range(DH):
                        ins = dve.tensor_tensor_scan(h[u][:, k, :], keep[u][:, k, :], val[u][:, k, :], 0.0, ALU.mult, ALU.add)
                    ins.then_inc(h_up, 1)
                    dve.wait_ge(o_up, b + 1)
                    for t in range(T):
                        ins = dve.scalar_tensor_tensor(z[:, t, :], x_in[u][:, t, :], 2.0, ps_o[:, t, :], ALU.mult, ALU.add)
                    ins.then_inc(steps, 1)
                    layernorm(dve, z, st, mv, ve, rstd, xo[u], b, i, steps, z_up, rstd_up, xo_up, stored[u], past_dve)

        @block.tensor
        def _(pe):
            pe.wait_ge(const_up, 3)
            with pe.Fori(0, B // 2) as i:
                for u in range(2):
                    b = 2 * i + u
                    pe.wait_ge(xn_up, b + 3)
                    pe.wait_ge(xnT_up, b + 1)
                    for k in range(DH):
                        for t in range(T):
                            ins = pe.transpose(ps_t[:, k, t * P:(t + 1) * P], xn[u][:, t, k * P:(k + 1) * P], ident[:, :])
                    ins.then_inc(t_up, 1)
                    pe.wait_ge(xnT_up, b + 2)
                    pe.wait_ge(h_up, b + 2)
                    pe.wait_ge(sig_up, b * 3 + 1)
                    for n in range(NK):
                        out = (ps_h if n < DH else ps_g)[:, n % DH, :]
                        for k in range(DH):
                            ins = pe.matmul(out, w[u][:, k, n * P:(n + 1) * P], xnT[u][:, k, :], start=(k == 0), stop=(k == DH - 1))
                    ins.then_inc(hg_up, 1)
                    pe.wait_ge(h_up, b + 3)
                    pe.wait_ge(xo_up, b + 2)
                    for t in range(T):
                        for k in range(DH):
                            ins = pe.matmul(ps_o[:, t, :], h[u][:, k, t * P:(t + 1) * P], w[u][:, k, 2 * D:3 * D],
                                            start=(k == 0), stop=(k == DH - 1))
                    ins.then_inc(o_up, 1)


H0 = 16
DK = D // H0
QH = 4
PARTS = 3


def wait(eng, sem, count):
    if not isinstance(count, int) or count > 0:
        eng.wait_ge(sem, count)


def row_bc(vec, n):
    return vec.rearrange("(o e) -> o e", o=1).to_broadcast([n, vec.shape[0]])


def stage_proj(nc, a):
    SC = DK ** -0.5
    with ExitStack() as ctx:
        r = Room(nc, ctx, "proj")
        x_in = [r.sb(f"x{u}", [P, T, D]) for u in range(2)]
        cT = [r.sb(f"cT{u}", [P, DH, S]) for u in range(2)]
        xT = [r.sb(f"xT{u}", [P, DH, S]) for u in range(2)]
        wq, wk, wv = (r.sb(n, [P, DH, D]) for n in ("wq", "wk", "wv"))
        bq, bqs, bk = (r.sb(n, [P, DH]) for n in ("bq", "bqs", "bk"))
        bv = r.sb("bv", [P, D])
        full = [[r.sb(f"full{n}{u}", [P, DH, S]) for u in range(2)] for n in "qk"]
        rest = [[r.sb(f"rest{n}{u}", [P, DH, S]) for u in range(2)] for n in "qk"]
        parts = [[r.sb(f"parts{n}{u}", [P, PARTS, DH, S], BF16) for u in range(2)] for n in "qk"]
        v = [r.sb(f"v{u}", [P, T, D]) for u in range(2)]
        ident = r.sb("ident", [P, P])
        ps_t, ps_q, ps_k = (r.ps(n, [P, DH, S]) for n in ("ps_t", "ps_q", "ps_k"))
        ps_v = r.ps("ps_v", [P, T, D])
        ps_qk = [ps_q, ps_k]
        c_ld, const_up, bqs_up, past_pool = (r.sem(n) for n in ("c_ld", "const_up", "bqs_up", "past_pool"))
        ld, st = [r.sem(f"ld{u}") for u in range(2)], [r.sem(f"st{u}") for u in range(2)]
        t_up, xT_up, mm_up, high_up, rest_up, mid_up, low_up, v_up = (r.sem(n) for n in
            ("t_up", "xT_up", "mm_up", "high_up", "rest_up", "mid_up", "low_up", "v_up"))
        block = ctx.enter_context(nc.Block())

        @block.sync
        def _(sp):
            for w, n in ((wq, "L0_xattn_WqT"), (wk, "L0_xattn_WkT"), (wv, "L0_xattn_WvT")):
                sp.dma_start(w[:, :, :], a[n].rearrange("(h p) n -> p h n", p=P)).then_inc(c_ld, 16)
            with nc.allow_non_contiguous_dma(reason="256 biases"):
                for w, n in ((bq, "L0_xattn_bq"), (bk, "L0_xattn_bk")):
                    sp.dma_start(w[:, :], a[n].rearrange("(h p) -> p h", p=P)).then_inc(c_ld, 16)
            sp.dma_start(bv[:, :], row_bc(a["L0_xattn_bv"], P)).then_inc(c_ld, 16)

            def load(b, u):
                sp.dma_start(x_in[u][:, :, :], tok(a["x1"][b])).then_inc(ld[u], 16)
                sp.dma_start(cT[u][:, :, :], a["ctxT"][b].rearrange("(h p) s -> p h s", p=P)).then_inc(ld[u], 16)

            def store(b, u):
                sp.wait_ge(low_up, 2 * b + 2)
                for n in range(2):
                    sp.dma_start(a["qk_parts"][b, n].rearrange("c (h p) s -> p (c h) s", p=P),
                                 parts[n][u][:, :, :, :].rearrange("p c h s -> p (c h) s")).then_inc(st[u], 16)
                sp.wait_ge(v_up, b + 1)
                sp.dma_start(tok(a["v"][b]), v[u][:, :, :]).then_inc(st[u], 16)

            for u in range(2):
                load(u, u)
            with sp.Fori(0, B // 2 - 1) as i:
                for u in range(2):
                    store(2 * i + u, u)
                    load(2 * i + u + 2, u)
            for u in range(2):
                store(B - 2 + u, u)
                sp.wait_ge(st[u], 48 * B // 2)

        @block.gpsimd
        def _(pool):
            pool.memset(ident[:, :], 0.0).then_inc(const_up, 1)
            pool.wait_ge(const_up, 1)
            pool.affine_select(out=ident[:, :], in_=ident[:, :], compare_op=ALU.not_equal, fill=1.0, base=0,
                               pattern=[[-1, P]], channel_multiplier=1).then_inc(const_up, 1)
            with pool.Fori(0, B // 2) as i:
                for u in range(2):
                    b = 2 * i + u
                    for n in range(2):
                        pool.wait_ge(rest_up, 2 * b + n + 1)
                        apart(pool, past_pool)
                        pool.tensor_copy(parts[n][u][:, 1, :, :], rest[n][u][:, :, :]).then_inc(mid_up, 1)

        def pairs(eng, body):
            for u in range(2):
                body(u, u, 0)
            with eng.Fori(1, B // 2) as i:
                for u in range(2):
                    body(2 * i + u, u, i)

        @block.scalar
        def _(act):
            act.wait_ge(c_ld, 96)
            act.mul(bqs[:, :], bq[:, :], SC).then_inc(bqs_up, 1)
            act.wait_ge(bqs_up, 1)

            def body(b, u, i):
                act.wait_ge(t_up, b + 1)
                act.activation(xT[u][:, :, :], ps_t[:, :, :], ACT.Copy).then_inc(xT_up, 1)
                for n in range(2):
                    act.wait_ge(mm_up, 3 * b + n + 1)
                    wait(act, low_up, 2 * b + n - 3)
                    wait(act, st[u], 48 * i)
                    for h in range(DH):
                        kw = dict(scale=SC, bias=bqs[:, h:h + 1]) if n == 0 else dict(bias=bk[:, h:h + 1])
                        act.activation(full[n][u][:, h, :], ps_qk[n][:, h, :], ACT.Identity, **kw)
                        ins = act.activation(parts[n][u][:, 0, h, :], ps_qk[n][:, h, :], ACT.Identity, **kw)
                    ins.then_inc(high_up, 1)
            pairs(act, body)

        @block.vector
        def _(dve):
            dve.wait_ge(c_ld, 96)

            def body(b, u, i):
                for n in range(2):
                    dve.wait_ge(high_up, 2 * b + n + 1)
                    dve.tensor_tensor(rest[n][u][:, :, :], full[n][u][:, :, :], parts[n][u][:, 0, :, :], ALU.subtract).then_inc(rest_up, 1)
                for n in range(2):
                    dve.wait_ge(mid_up, 2 * b + n + 1)
                    dve.tensor_tensor(parts[n][u][:, 2, :, :], rest[n][u][:, :, :], parts[n][u][:, 1, :, :], ALU.subtract).then_inc(low_up, 1)
                dve.wait_ge(mm_up, 3 * b + 3)
                wait(dve, st[u], 48 * i)
                dve.tensor_tensor(v[u][:, :, :], ps_v[:, :, :], bv[:, :].rearrange("p (o d) -> p o d", o=1).to_broadcast([P, T, D]),
                                  ALU.add).then_inc(v_up, 1)
            pairs(dve, body)

        @block.tensor
        def _(pe):
            pe.wait_ge(const_up, 2)
            pe.wait_ge(c_ld, 96)

            def body(b, u, i):
                pe.wait_ge(ld[u], 32 * i + 32)
                wait(pe, xT_up, b)
                for h in range(DH):
                    for t in range(T):
                        ins = pe.transpose(ps_t[:, h, t * P:(t + 1) * P], x_in[u][:, t, h * P:(h + 1) * P], ident[:, :])
                ins.then_inc(t_up, 1)
                pe.wait_ge(xT_up, b + 1)
                for n, (w, src) in enumerate(((wq, xT[u]), (wk, cT[u]))):
                    wait(pe, high_up, 2 * b + n - 1)
                    for m in range(DH):
                        for h in range(DH):
                            ins = pe.matmul(ps_qk[n][:, m, :], w[:, h, m * P:(m + 1) * P], src[:, h, :], start=(h == 0), stop=(h == DH - 1))
                    ins.then_inc(mm_up, 1)
                wait(pe, v_up, b)
                for t in range(T):
                    for h in range(DH):
                        ins = pe.matmul(ps_v[:, t, :], cT[u][:, h, t * P:(t + 1) * P], wv[:, h, :], start=(h == 0), stop=(h == DH - 1))
                ins.then_inc(mm_up, 1)
            pairs(pe, body)


def stage_xattn0(nc, a):
    HU = H0 // 2
    NK = 6 * DK
    QP, KP = (0, 0, 1, 1, 0, 2), (0, 1, 0, 1, 2, 0)
    CH = 4
    NP = 4
    DROP = S - int(S * 0.9)
    ROUNDS = -(-DROP // 8)
    PICK = 2 * ROUNDS + 1
    GONE = -3.0e38
    with ExitStack() as ctx:
        r = Room(nc, ctx, "xa")
        probT = [r.sb(f"probT{u}", [P, HU, T, S]) for u in range(2)]
        probs = [r.sb(f"probs{u}", [P, T, S]) for u in range(NP)]
        q = [r.sb(f"q{u}", [NK, CH, S], BF16) for u in range(2)]
        k = [r.sb(f"k{u}", [NK, CH, S], BF16) for u in range(2)]
        v = [r.sb(f"v{u}", [P, T, HU * DK]) for u in range(2)]
        vm = r.sb("vm", [P, T * HU, 32])
        oT = r.sb("oT", [P, 2 * DH, S])
        wo = r.sb("wo", [P, 2 * DH, D])
        bo = r.sb("bo", [P, D])
        x_in = r.sb("x_in", [P, T, D])
        ident = r.sb("ident", [P, P])
        colsum = [r.sb(f"colsum{u}", [P, T, HU]) for u in range(2)]
        left = r.sb("left", [HU, S])
        m8 = r.sb("m8", [HU, 8])
        kept = r.sb("kept", [HU, S])
        nmax, rsum, rinv = ([r.sb(f"{n}{u}", [P, T]) for u in range(2)] for n in ("nmax", "rsum", "rinv"))
        st6, mv = r.sb("st6", [P, T, 6]), r.sb("mv", [P, T, 2])
        ve, rstd, mhalf = (r.sb(n, [P, T]) for n in ("ve", "rstd", "mhalf"))
        ps_s = [r.ps(f"ps_s{j}", [P, 2, S]) for j in range(2)]
        ps_t = [r.ps(f"ps_t{j}", [P, S]) for j in range(2)]
        ps_m = [r.ps(f"ps_m{j}", [P, S]) for j in range(2)]
        c_ld, const_up, pad_up = r.sem("c_ld"), r.sem("const_up"), r.sem("pad_up")
        past_dve, past_pool, past_pe = (r.sem(n) for n in ("past_dve", "past_pool", "past_pe"))
        qk_ld, v_ld = [r.sem(f"qk_ld{u}") for u in range(2)], [r.sem(f"v_ld{u}") for u in range(2)]
        x_ld, x2_st = r.sem("x_ld"), r.sem("x2_st")
        s_up, max_up, exp_up, rinv_up, norm_up, t_up, copy_s, copy_v = (r.sem(n) for n in
            ("s_up", "max_up", "exp_up", "rinv_up", "norm_up", "t_up", "copy_s", "copy_v"))
        m_up, m_free = [r.sem(f"m_up{j}") for j in range(2)], [r.sem(f"m_free{j}") for j in range(2)]
        pick, found, xb_up, ln, rstd_up = (r.sem(n) for n in ("pick", "found", "xb_up", "ln", "rstd_up"))
        block = ctx.enter_context(nc.Block())

        def over0(b, u, back, use):
            return 3 * (2 * b + u - back) + use

        def over1(b, use):
            return 4 * (b - 1) + use

        def since(b, first):
            return not isinstance(b, int) or b >= first

        def batches(eng, body):
            body(0)
            body(1)
            with eng.Fori(2, B) as b:
                body(b)
            body(B)

        def slots(b):
            for u in range(2):
                for h in range(HU):
                    yield u, h, HU * u + h, 2 * HU * b + HU * u + h, not isinstance(b, int) or b < B

        def has_before(b, u):
            return not isinstance(b, int) or 1 <= 2 * b + u <= 2 * B

        def has_before2(b, u):
            return not isinstance(b, int) or 2 <= 2 * b + u <= 2 * B + 1

        COPY_V = 2

        def turning(b, u, h, n, real):
            return not (isinstance(b, int) and n < 2) and (real or (u == 0 and h < 2))

        def turned(eng, b, u, h, n, real, t):
            if not turning(b, u, h, n, real):
                return
            bb, g, hp = (b, u, h - 2) if h >= 2 else (b + u - 1, 1 - u, HU - 2 + h)
            if hp % QH == 0 and t in (0, COPY_V):
                if hp < QH:
                    wait(eng, m_up[0], 3 * (2 * bb - 2 + g) + 3)
                else:
                    wait(eng, m_up[1], 4 * (bb - 1) + 1 + g)
            eng.wait_ge(t_up, 4 * (n - 2) + t + 1)
            dst, src, out = probT[g][:, hp, t, :], ps_t[t % 2][:, :], colsum[g][:, t, hp:hp + 1]
            if t == COPY_V:
                eng.tensor_scalar(dst, src, 1.0, 0.0, ALU.mult, ALU.add, accum_out=out).then_inc(copy_v, 1)
            else:
                eng.activation(dst, src, ACT.Copy, accum_out=out).then_inc(copy_s, 1)

        @block.sync
        def _(sp):
            sp.dma_start(bo[:, :], row_bc(a["L0_xattn_bo"], P)).then_inc(c_ld, 16)
            sp.wait_ge(pad_up, 2)
            for g in range(2 * DH):
                for j in range(QH):
                    sp.dma_start(wo[32 * j:32 * j + DK, g, :],
                                 a["L0_xattn_WoT"][(QH * g + j) * DK:(QH * g + j + 1) * DK, :]).then_inc(c_ld, 16)

            def chunk(b, c):
                wait(sp, s_up, 32 * b + 8 * c - 8)
                for n, dst in ((0, q[c % 2]), (1, k[c % 2])):
                    for g in range(6):
                        src = a["qk_parts"][b, n, (QP, KP)[n][g], CH * DK * c:CH * DK * (c + 1), :]
                        sp.dma_start(dst[g * DK:(g + 1) * DK, :, :], src.rearrange("(h d) s -> d h s", d=DK)).then_inc(qk_ld[c % 2], 16)

            def value(b, u):
                wait(sp, m_free[0], 3 * (2 * b + u - 2) + 2)
                sp.dma_start(v[u][:, :, :], tok(a["v"][b])[:, :, u * P:(u + 1) * P]).then_inc(v_ld[u], 16)

            def store(b):
                sp.wait_ge(ln, 4 * b + 4)
                sp.dma_start(tok(a["x2"][b]), x_in[:, :, :]).then_inc(x2_st, 16)

            def body(b):
                if isinstance(b, int) and b == B:
                    store(b - 2)
                    sp.wait_ge(x2_st, 16 * (b - 1))
                    sp.dma_start(x_in[:, :, :], tok(a["x1"][b - 1])).then_inc(x_ld, 16)
                    return
                chunk(b, 0)
                chunk(b, 1)
                value(b, 0)
                chunk(b, 2)
                if since(b, 2):
                    store(b - 2)
                if since(b, 1):
                    wait(sp, x2_st, 16 * (b - 1))
                    sp.dma_start(x_in[:, :, :], tok(a["x1"][b - 1])).then_inc(x_ld, 16)
                chunk(b, 3)
                value(b, 1)
            batches(sp, body)
            store(B - 1)
            sp.wait_ge(x2_st, 16 * B)

        @block.gpsimd
        def _(pool):
            pool.memset(vm[:, :, :], 0.0).then_inc(pad_up, 1)
            pool.memset(wo[:, :, :], 0.0).then_inc(pad_up, 1)
            pool.memset(mhalf[:, :], -0.5).then_inc(const_up, 1)
            pool.memset(ident[:, :], 0.0).then_inc(const_up, 1)
            pool.wait_ge(const_up, 2)
            pool.affine_select(out=ident[:, :], in_=ident[:, :], compare_op=ALU.not_equal, fill=1.0, base=0,
                               pattern=[[-1, P]], channel_multiplier=1).then_inc(const_up, 1)
            pool.wait_ge(c_ld, 16 * (1 + H0))

            def root(b):
                pool.wait_ge(ln, 4 * b + 3)
                pool.tensor_tensor(rstd[:, :], ve[:, :], mhalf[:, :], ALU.pow).then_inc(rstd_up, 1)

            def body(b):
                for u, h, hh, n, real in slots(b):
                    if (u, h) == (0, 1) and since(b, 2):
                        root(b - 2)
                    if real:
                        pool.wait_ge(rinv_up, n + 1)
                        apart(pool, past_pool)
                        for t in range(T):
                            ins = pool.tensor_scalar(probs[h % NP][:, t, :], probs[h % NP][:, t, :], rinv[h % 2][:, t:t + 1], 1.0,
                                                     ALU.mult, ALU.mult)
                        ins.then_inc(norm_up, 1)
                    if (u, h) == (1, 2) and since(b, 1):
                        pool.wait_ge(x_ld, 16 * b)
                        pool.tensor_tensor(x_in[:, :, :], x_in[:, :, :], bo[:, :].rearrange("p (o d) -> p o d", o=1).to_broadcast([P, T, D]),
                                           ALU.add).then_inc(xb_up, 1)
            batches(pool, body)
            root(B - 1)

        @block.scalar
        def _(act):
            def body(b):
                def exponentials(h, n, j):
                    act.wait_ge(max_up, 2 * n + j + 1)
                    for t in (2 * j, 2 * j + 1):
                        ins = act.activation(probs[h % NP][:, t, :], ps_s[j][:, t % 2, :], ACT.Exp,
                                             bias=nmax[h % 2][:, t:t + 1], accum_out=rsum[h % 2][:, t:t + 1])
                    ins.then_inc(exp_up, 1)

                for u, h, hh, n, real in slots(b):
                    if h == 6 and has_before2(b, u):
                        act.wait_ge(m_up[1], over1(b, u + 1))
                        act.activation(oT[:, 2 * u + 1, :], ps_m[1][:, :], ACT.Copy).then_inc(m_free[1], 1)
                    turned(act, b, u, h, n, real, 0)
                    if real:
                        wait(act, t_up, 4 * (n - 3))
                        exponentials(h, n, 0)
                    turned(act, b, u, h, n, real, 1)
                    if real:
                        exponentials(h, n, 1)
                    turned(act, b, u, h, n, real, 3)
                    if h == 2 and has_before2(b, u):
                        act.wait_ge(m_up[0], over0(b, u, 2, 3))
                        act.activation(oT[:, 2 * u, :], ps_m[0][:, :], ACT.Copy).then_inc(m_free[0], 1)
            batches(act, body)

        @block.vector
        def _(dve):
            dve.wait_ge(pad_up, 2)

            def reciprocal(n, h):
                dve.wait_ge(exp_up, 2 * n + 2)
                wait(dve, norm_up, n - 1)
                dve.reciprocal(rinv[h % 2][:, :], rsum[h % 2][:, :]).then_inc(rinv_up, 1)

            def maxima(n, h, j):
                dve.wait_ge(s_up, 2 * n + j + 1)
                dve.tensor_reduce(nmax[h % 2][:, 2 * j:2 * j + 2], ps_s[j][:, :, :], AX.X, ALU.max, negate=True).then_inc(max_up, 1)

            def search(b, u, h, places):
                if not has_before(b, u) or h < 3:
                    return
                base = PICK * (2 * b + u - 1)
                for step in (3 * (h - 3) + place for place in places):
                    n = (step - 1) // 2
                    if step == 0:
                        dve.wait_ge(m_up[0], over0(b, u, 1, 1))
                        wait(dve, pick, base)
                        dve.tensor_scalar(left[:, ::-1], ps_m[0][0:HU, :], -1.0, None, ALU.mult).then_inc(m_free[0], 1)
                    elif step == 2 * ROUNDS + 1:
                        dve.wait_ge(found, 2 * b + u)
                        dve.tensor_scalar(kept[:, ::-1], left[:, :], GONE, None, ALU.not_equal).then_inc(pick, 1)
                    elif step % 2:
                        if n == 0:
                            dve.wait_ge(m_free[0], over0(b, u, 1, 1))
                        else:
                            wait(dve, pick, base + 2 * n)
                        apart(dve, past_dve)
                        dve.max(m8[:, :], left[:, :]).then_inc(pick, 1)
                        if n == ROUNDS - 1:
                            dve.wait_ge(pick, base + 2 * n + 1)
                            dve.memset(m8[:, DROP - 8 * n:8], GONE).then_inc(pick, 1)
                    else:
                        last = n == ROUNDS - 1
                        dve.wait_ge(pick, base + 2 * n + 1 + last)
                        apart(dve, past_dve)
                        dve.match_replace(left[:, :], m8[:, :], left[:, :], GONE).then_inc(found if last else pick, 1)

            def stats(b):
                dve.wait_ge(m_free[1], 4 * (b + 1))
                for t in range(T):
                    ins = dve.bn_stats(st6[:, t, :], x_in[:, t, :])
                ins.then_inc(ln, 1)
                dve.wait_ge(ln, 4 * b + 1)
                apart(dve, past_dve)
                for t in range(T):
                    ins = dve.bn_aggr(mv[:, t, :], st6[:, t, :])
                ins.then_inc(ln, 1)
                dve.wait_ge(ln, 4 * b + 2)
                dve.tensor_scalar(ve[:, :], mv[:, :, 1], 1e-5, None, ALU.add).then_inc(ln, 1)

            def body(b):
                for u, h, hh, n, real in slots(b):
                    if real:
                        maxima(n, h, 0)
                    search(b, u, h, (0,))
                    if (real or (u, h) == (0, 0)) and not (isinstance(b, int) and n == 0):
                        reciprocal(n - 1, h - 1)
                    if real:
                        maxima(n, h, 1)
                    if h == 0 and has_before2(b, u):
                        dve.wait_ge(m_up[0], over0(b, u, 2, 2))
                        dve.wait_ge(v_ld[u], 16 * b)
                        dve.tensor_tensor(vm[:, :, 0:DK], v[u][:, :, :].rearrange("p t (h d) -> p (t h) d", d=DK),
                                          ps_m[0][:, 0:T * HU].rearrange("p (n o) -> p n o", o=1).to_broadcast([P, T * HU, DK]),
                                          ALU.mult).then_inc(m_free[0], 1)
                    search(b, u, h, (1,))
                    turned(dve, b, u, h, n, real, COPY_V)
                    search(b, u, h, (2, 3) if h == HU - 1 else (2,))
                    if u == 1 and h in (6, 7) and since(b, 1):
                        i = h - 6
                        dve.wait_ge(m_up[1], over1(b, 3 + i))
                        dve.wait_ge(xb_up, b)
                        dve.tensor_tensor(x_in[:, 2 * i:2 * i + 2, :], ps_m[1][:, :].rearrange("p (t d) -> p t d", t=2),
                                          x_in[:, 2 * i:2 * i + 2, :], ALU.add).then_inc(m_free[1], 1)
                    if (u, h) == (0, 0) and since(b, 2):
                        stats(b - 2)
                    if (u, h) == (0, 2) and since(b, 2):
                        finish(b - 2)

            def finish(b):
                dve.wait_ge(rstd_up, b + 1)
                for t in range(T):
                    ins = dve.tensor_scalar(x_in[:, t, :], x_in[:, t, :], mv[:, t, 0:1], rstd[:, t:t + 1], ALU.subtract, ALU.mult)
                ins.then_inc(ln, 1)
            batches(dve, body)
            stats(B - 1)
            finish(B - 1)

        @block.tensor
        def _(pe):
            pe.wait_ge(const_up, 3)
            pe.wait_ge(c_ld, 16 * (1 + H0))

            def values(b, u, quads, t):
                for j in range(QH):
                    h = QH * quads + j
                    ins = pe.matmul(ps_m[quads][32 * j:32 * j + 32, :], vm[:, t * HU + h, :], probT[u][:, h, t, :],
                                    start=(t == 0), stop=(t == T - 1))
                if t == T - 1:
                    ins.then_inc(m_up[quads], 1)

            def scores(c, hh, n, j):
                wait(pe, exp_up, 2 * (n - 1) + j + 1)
                for t in (2 * j, 2 * j + 1):
                    ins = pe.matmul(ps_s[j][:, t % 2, :], q[c % 2][:, hh % CH, t * P:(t + 1) * P], k[c % 2][:, hh % CH, :],
                                    start=True, stop=True)
                ins.then_inc(s_up, 1)

            def turn(h, m, t):
                if t == 0:
                    wait(pe, copy_v, m)
                else:
                    wait(pe, copy_s, 3 * m + t - 1)
                for i in range(T):
                    ins = pe.transpose(ps_t[t % 2][:, i * P:(i + 1) * P], probs[(h - 2) % NP][:, i, t * P:(t + 1) * P], ident[:, :])
                ins.then_inc(t_up, 1)

            def body(b):
                for u, h, hh, n, real in slots(b):
                    if real:
                        c = hh // CH
                        if hh % CH == 0:
                            pe.wait_ge(qk_ld[c % 2], 192 * (2 * b + c // 2 + 1))
                        scores(c, hh, n, 0)
                        scores(c, hh, n, 1)
                    if h == 0 and has_before2(b, u):
                        pe.wait_ge(pick, PICK * (2 * b + u - 1))
                        pe.wait_ge(m_free[0], over0(b, u, 2, 1))
                        apart(pe, past_pe)
                        for t in range(T):
                            ins = pe.transpose(ps_m[0][:, t * HU:(t + 1) * HU], kept[:, t * P:(t + 1) * P], ident[0:HU, 0:HU])
                        ins.then_inc(m_up[0], 1)
                    if h == 2 and has_before2(b, u):
                        values(b, u, 0, 3)
                    if h == 3 and has_before(b, u):
                        pe.wait_ge(copy_s, 3 * HU * (2 * b + u))
                        pe.wait_ge(copy_v, HU * (2 * b + u))
                        wait(pe, m_free[0], over0(b, u, 1, 0))
                        for t in range(T):
                            ins = pe.transpose(ps_m[0][0:HU, t * P:(t + 1) * P], colsum[1 - u][:, t, :], ident[:, :])
                        ins.then_inc(m_up[0], 1)
                    if turning(b, u, h, n, real):
                        pe.wait_ge(norm_up, n - 1)
                        turn(h, n - 2, 0)
                        turn(h, n - 2, 1)
                    if 2 <= h < 2 + T and has_before2(b, u):
                        if h == 2:
                            wait(pe, m_free[1], over1(b, u))
                        values(b, u, 1, h - 2)
                    if u == 1 and h in (6, 7) and since(b, 1):
                        i = h - 6
                        pe.wait_ge(m_free[0], over0(b, u, 1, 0))
                        pe.wait_ge(m_free[1], over1(b, 2 + i))
                        for t in (2 * i, 2 * i + 1):
                            for g in range(2 * DH):
                                ins = pe.matmul(ps_m[1][:, (t % 2) * D:(t % 2 + 1) * D], oT[:, g, t * P:(t + 1) * P], wo[:, g, :],
                                                start=(g == 0), stop=(g == 2 * DH - 1))
                        ins.then_inc(m_up[1], 1)
                    if h == 1 and has_before2(b, u):
                        values(b, u, 0, 1)
                        values(b, u, 0, 2)
                    if turning(b, u, h, n, real):
                        turn(h, n - 2, 2)
                        turn(h, n - 2, 3)
                    if h == 0 and has_before2(b, u):
                        pe.wait_ge(m_free[0], over0(b, u, 2, 2))
                        values(b, u, 0, 0)
            batches(pe, body)


CAP = 1024
F = 512
FF = 128


def pairs(eng, body):
    for u in range(2):
        body(u, u, 0)
    with eng.Fori(1, B // 2) as i:
        for u in range(2):
            body(2 * i + u, u, i)


def col(ap):
    return ap.rearrange("p (n o) -> p n o", o=1)


def row(ap):
    return ap.rearrange("p (o n) -> p o n", o=1)


def stage_route(nc, a, route_w, route_i):
    BIG = 16384.0
    with ExitStack() as ctx:
        r = Room(nc, ctx, "ro")
        x_in, xs, xsT, fo = ([r.sb(f"{n}{u}", s) for u in range(2)] for n, s in
                             (("x", [P, T, D]), ("xs", [P, T, D]), ("xsT", [P, DH, S]), ("fo", [P, T, D])))
        junk = [r.sb(f"junk{u}", [P, T, D], BF16) for u in range(2)]
        ssq, msq, inv, rms = ([r.sb(f"{n}{u}", [P, T]) for u in range(2)] for n in ("ssq", "msq", "inv", "rms"))
        act_f = [r.sb(f"act_f{u}", [FF, S]) for u in range(2)]
        mhalf = r.sb("mhalf", [P, T])
        ident, before, ones = (r.sb(n, [P, P]) for n in ("ident", "before", "ones"))
        base_i = r.sb("base_i", [P, E], mybir.dt.int32)
        base = r.sb("base", [P, E])
        wr = r.sb("wr", [P, DH, E])
        fn = r.sb("fn", [P, DH])
        fwg, fwu = r.sb("fwg", [P, DH, FF]), r.sb("fwu", [P, DH, FF])
        fwd = r.sb("fwd", [FF, D])
        lg, ex, sel, pos, place, ap_, far, one, two = (r.sb(n, [P, T, E]) for n in
            ("lg", "ex", "sel", "pos", "place", "ap", "far", "one", "two"))
        pr, rep = r.sb("pr", [P, T, 2 * E]), r.sb("rep", [P, T, 2 * E])
        m8 = r.sb("m8", [P, T, 8])
        mx, sm, rs, top, tot, wab, ovf, nov = (r.sb(n, [P, T]) for n in ("mx", "sm", "rs", "top", "tot", "wab", "ovf", "nov"))
        pf = r.sb("pf", [P, 2, T])
        pi = [r.sb(f"pi{u}", [P, 2, T], U32) for u in range(2)]
        carry = r.sb("carry", [P, E])
        ps_t = r.ps("ps_t", [P, DH, S])
        ps_g, ps_u = r.ps("ps_g", [FF, S]), r.ps("ps_u", [FF, S])
        ps_f = r.ps("ps_f", [P, T, D])
        ps_l = r.ps("ps_l", [P, 3, T, E])
        c_ld, const_up, const_v, past_dve, past_pool = (r.sem(n) for n in ("c_ld", "const_up", "const_v", "past_dve", "past_pool"))
        ld, st, sent = ([r.sem(f"{n}{u}") for u in range(2)] for n in ("ld", "st", "sent"))
        sq_up, msq_up, inv_up, xs_up, t_up, xsT_up, lg_up, ffn_up, soft, soft_s, gelu_up, hid_up, f_up, fo_up, v, pos_up, ind_up = (
            r.sem(n) for n in ("sq_up", "msq_up", "inv_up", "xs_up", "t_up", "xsT_up", "lg_up", "ffn_up", "soft", "soft_s",
                               "gelu_up", "hid_up", "f_up", "fo_up", "v", "pos_up", "ind_up"))
        NV = 24
        block = ctx.enter_context(nc.Block())

        @block.sync
        def _(sp):
            with nc.allow_non_contiguous_dma(reason="small weights"):
                sp.dma_start(fn[:, :], a["L0_ffn_f_norm"].rearrange("(h p) -> p h", p=P)).then_inc(c_ld, 16)
            sp.dma_start(wr[:, :, :], a["L0_ffn_Wr"].rearrange("(h p) e -> p h e", p=P)).then_inc(c_ld, 16)
            sp.dma_start(fwg[:, :, :], a["L0_ffn_fWg"].rearrange("(h p) f -> p h f", p=P)).then_inc(c_ld, 16)
            sp.dma_start(fwu[:, :, :], a["L0_ffn_fWu"].rearrange("(h p) f -> p h f", p=P)).then_inc(c_ld, 16)
            sp.dma_start(fwd[:, :], a["L0_ffn_fWd"]).then_inc(c_ld, 16)

            def load(b, u):
                sp.dma_start(x_in[u][:, :, :], tok(a["x2"][b])).then_inc(ld[u], 16)

            def store(b, u, i):
                sp.wait_ge(fo_up, b + 1)
                sp.dma_start(tok(a["fallback"][b]), fo[u][:, :, :]).then_inc(st[u], 16)
                sp.wait_ge(sent[u], 16 * 2 * T * (i + 1))

            for u in range(2):
                load(u, u)
            with sp.Fori(0, B // 2 - 1) as i:
                for u in range(2):
                    store(2 * i + u, u, i)
                    load(2 * i + u + 2, u)
            for u in range(2):
                store(B - 2 + u, u, B // 2 - 1)
                sp.wait_ge(st[u], 16 * B // 2)

        @block.gpsimd
        def _(pool):
            pool.memset(mhalf[:, :], -0.5).then_inc(const_up, 1)
            pool.memset(ident[:, :], 0.0).then_inc(const_up, 1)
            pool.memset(before[:, :], 1.0).then_inc(const_up, 1)
            pool.memset(ones[:, :], 1.0).then_inc(const_up, 1)
            pool.memset(pr[:, :, :], -1.0).then_inc(const_up, 1)
            pool.memset(carry[:, :], 0.0).then_inc(const_up, 1)
            pool.iota(base_i[:, :], pattern=[[CAP, E]], base=1, channel_multiplier=0).then_inc(const_up, 1)
            pool.wait_ge(const_up, 7)
            pool.tensor_copy(base[:, :], base_i[:, :]).then_inc(const_up, 1)
            pool.affine_select(out=ident[:, :], in_=ident[:, :], compare_op=ALU.not_equal, fill=1.0, base=0,
                               pattern=[[-1, P]], channel_multiplier=1).then_inc(const_up, 1)
            pool.affine_select(out=before[:, :], in_=before[:, :], compare_op=ALU.is_gt, fill=0.0, base=0,
                               pattern=[[1, P]], channel_multiplier=-1).then_inc(const_up, 1)

            def body(b, u, i):
                pool.wait_ge(msq_up, b + 1)
                pool.tensor_tensor(inv[u][:, :], msq[u][:, :], mhalf[:, :], ALU.pow).then_inc(inv_up, 1)
                pool.wait_ge(ind_up, b + 1)
                apart(pool, past_pool)
                for n in range(2):
                    for t in range(T):
                        pool.indirect_dma_start(out=a["buf"], out_offset=bass.IndirectOffsetOnAxis(ap=pi[u][:, n, t:t + 1], axis=0),
                                                in_=x_in[u][:, t, :], in_offset=None, bounds_check=E * CAP - 1,
                                                oob_is_err=False).then_inc(sent[u], 16)
            pairs(pool, body)

        @block.scalar
        def _(act):
            def body(b, u, i):
                act.wait_ge(ld[u], 16 * i + 16)
                wait(act, msq_up, b - 1)
                for t in range(T):
                    ins = act.activation(junk[u][:, t, :], x_in[u][:, t, :], ACT.Square, accum_out=ssq[u][:, t:t + 1])
                ins.then_inc(sq_up, 1)
                act.wait_ge(t_up, b + 1)
                wait(act, ffn_up, b - 1)
                act.activation(xsT[u][:, :, :], ps_t[:, :, :], ACT.Copy).then_inc(xsT_up, 1)
                act.wait_ge(v, NV * b + 3)
                act.activation(ex[:, :, :], lg[:, :, :], ACT.Exp).then_inc(soft_s, 1)
                act.wait_ge(ffn_up, b + 1)
                wait(act, f_up, b - 1)
                act.activation(act_f[u][:, :], ps_g[:, :], ACT.Gelu).then_inc(gelu_up, 1)
            pairs(act, body)

        @block.vector
        def _(dve):
            dve.wait_ge(c_ld, 80)
            dve.wait_ge(const_up, 10)
            for h in range(DH):
                dve.tensor_scalar(fwg[:, h, :], fwg[:, h, :], fn[:, h:h + 1], None, ALU.mult).then_inc(const_v, 1)
                dve.tensor_scalar(fwu[:, h, :], fwu[:, h, :], fn[:, h:h + 1], None, ALU.mult).then_inc(const_v, 1)

            def body(b, u, i):
                step = [0]

                def then(ins):
                    step[0] += 1
                    ins.then_inc(v, 1)
                    dve.wait_ge(v, NV * b + step[0])
                    if step[0] in (6, 8):
                        apart(dve, past_dve)

                dve.wait_ge(sq_up, b + 1)
                wait(dve, inv_up, b - 1)
                dve.tensor_scalar(msq[u][:, :], ssq[u][:, :], 1.0 / D, 1e-6, ALU.mult, ALU.add).then_inc(msq_up, 1)
                dve.wait_ge(inv_up, b + 1)
                dve.reciprocal(rms[u][:, :], inv[u][:, :])
                for t in range(T):
                    ins = dve.tensor_scalar(xs[u][:, t, :], x_in[u][:, t, :], inv[u][:, t:t + 1], None, ALU.mult)
                ins.then_inc(xs_up, 1)
                dve.wait_ge(lg_up, b + 1)
                dve.wait_ge(xs_up, b + 1)
                then(dve.tensor_tensor(lg[:, :, :], ps_l[:, 0, :, :], col(rms[u][:, :]).to_broadcast([P, T, E]), ALU.mult))
                then(dve.tensor_reduce(mx[:, :], lg[:, :, :], AX.X, ALU.max))
                then(dve.tensor_tensor(lg[:, :, :], lg[:, :, :], col(mx[:, :]).to_broadcast([P, T, E]), ALU.subtract))
                dve.wait_ge(soft_s, b + 1)
                then(dve.tensor_reduce(sm[:, :], ex[:, :, :], AX.X, ALU.add))
                then(dve.reciprocal(rs[:, :], sm[:, :]))
                then(dve.tensor_tensor(pr[:, :, 0:E], ex[:, :, :], col(rs[:, :]).to_broadcast([P, T, E]), ALU.mult))
                for t in range(T):
                    ins = dve.max(m8[:, t, :], pr[:, t, :])
                then(ins)
                then(dve.memset(m8[:, :, 2:8], -1.0))
                for t in range(T):
                    ins = dve.match_replace(rep[:, t, :], m8[:, t, :], pr[:, t, :], -1.0)
                then(ins)
                then(dve.tensor_tensor(sel[:, :, :], pr[:, :, 0:E], rep[:, :, 0:E], ALU.not_equal))
                dve.wait_ge(pos_up, b + 1)
                then(dve.tensor_tensor(pos[:, :, :], ps_l[:, 1, :, :], row(carry[:, :]).to_broadcast([P, T, E]), ALU.add))
                then(dve.tensor_tensor(carry[:, :], carry[:, :], ps_l[:, 2, 0, :], ALU.add))
                then(dve.tensor_scalar(far[:, :, :], pos[:, :, :], float(CAP), BIG, ALU.is_ge, ALU.mult))
                then(dve.tensor_tensor(pos[:, :, :], pos[:, :, :], far[:, :, :], ALU.add))
                then(dve.tensor_tensor(pos[:, :, :], pos[:, :, :], row(base[:, :]).to_broadcast([P, T, E]), ALU.add))
                then(dve.tensor_tensor(place[:, :, :], pos[:, :, :], sel[:, :, :], ALU.mult))
                then(dve.tensor_reduce(top[:, :], place[:, :, :], AX.X, ALU.max))
                dve.tensor_reduce(tot[:, :], place[:, :, :], AX.X, ALU.add)
                dve.tensor_scalar(ovf[:, :], top[:, :], BIG, None, ALU.is_gt)
                dve.tensor_tensor(ap_[:, :, :], pr[:, :, 0:E], sel[:, :, :], ALU.mult)
                dve.tensor_tensor(one[:, :, :], place[:, :, :], col(top[:, :]).to_broadcast([P, T, E]), ALU.is_equal)
                then(dve.tensor_tensor(two[:, :, :], place[:, :, :], col(top[:, :]).to_broadcast([P, T, E]), ALU.not_equal))
                dve.tensor_scalar(pf[:, 0, :], top[:, :], -1.0, None, ALU.add)
                dve.tensor_scalar(nov[:, :], ovf[:, :], -1.0, 1.0, ALU.mult, ALU.add)
                dve.tensor_tensor(one[:, :, :], one[:, :, :], ap_[:, :, :], ALU.mult)
                dve.tensor_tensor(two[:, :, :], two[:, :, :], ap_[:, :, :], ALU.mult)
                then(dve.scalar_tensor_tensor(pf[:, 1, :], tot[:, :], -1.0, top[:, :], ALU.add, ALU.subtract))
                wait(dve, sent[u], 16 * 2 * T * i)
                dve.tensor_copy(pi[u][:, :, :], pf[:, :, :]).then_inc(ind_up, 1)
                dve.tensor_scalar(route_i[:, bass.ds(b, 1), :, :].rearrange("p o n t -> p (o n) t"), pf[:, :, :], float(E * CAP - 1), None, ALU.min)
                dve.tensor_copy(route_w[:, bass.ds(b, 1), 2, :].rearrange("p o t -> p (o t)"), ovf[:, :])
                dve.tensor_reduce(wab[:, :], one[:, :, :], AX.X, ALU.add)
                then(dve.tensor_reduce(mx[:, :], two[:, :, :], AX.X, ALU.add))
                dve.tensor_tensor(route_w[:, bass.ds(b, 1), 0, :].rearrange("p o t -> p (o t)"), wab[:, :], nov[:, :], ALU.mult)
                then(dve.tensor_tensor(route_w[:, bass.ds(b, 1), 1, :].rearrange("p o t -> p (o t)"), mx[:, :], nov[:, :], ALU.mult))
                while step[0] < NV:
                    then(dve.memset(m8[:, 0, 0:1], -1.0))
                dve.wait_ge(gelu_up, b + 1)
                dve.tensor_tensor(act_f[u][:, :], act_f[u][:, :], ps_u[:, :], ALU.mult).then_inc(hid_up, 1)
                dve.wait_ge(f_up, b + 1)
                wait(dve, st[u], 16 * i)
                dve.tensor_tensor(fo[u][:, :, :], ps_f[:, :, :], x_in[u][:, :, :], ALU.add).then_inc(fo_up, 1)
            pairs(dve, body)

        @block.tensor
        def _(pe):
            pe.wait_ge(const_v, 4)

            def body(b, u, i):
                pe.wait_ge(xs_up, b + 1)
                wait(pe, xsT_up, b)
                for h in range(DH):
                    for t in range(T):
                        ins = pe.transpose(ps_t[:, h, t * P:(t + 1) * P], xs[u][:, t, h * P:(h + 1) * P], ident[:, :])
                ins.then_inc(t_up, 1)
                pe.wait_ge(xsT_up, b + 1)
                wait(pe, v, NV * b)
                for t in range(T):
                    for h in range(DH):
                        ins = pe.matmul(ps_l[:, 0, t, :], xsT[u][:, h, t * P:(t + 1) * P], wr[:, h, :], start=(h == 0), stop=(h == DH - 1))
                ins.then_inc(lg_up, 1)
                wait(pe, hid_up, b)
                for w, ps in ((fwg, ps_g), (fwu, ps_u)):
                    for h in range(DH):
                        ins = pe.matmul(ps[:, :], w[:, h, :], xsT[u][:, h, :], start=(h == 0), stop=(h == DH - 1))
                ins.then_inc(ffn_up, 1)
                pe.wait_ge(v, NV * b + 10)
                for t in range(T):
                    for s in range(t + 1):
                        pe.matmul(ps_l[:, 1, t, :], (before if s == t else ones)[:, :], sel[:, s, :], start=(s == 0), stop=(s == t))
                for s in range(T):
                    ins = pe.matmul(ps_l[:, 2, 0, :], ones[:, :], sel[:, s, :], start=(s == 0), stop=(s == T - 1))
                ins.then_inc(pos_up, 1)
                pe.wait_ge(hid_up, b + 1)
                wait(pe, fo_up, b)
                for t in range(T):
                    ins = pe.matmul(ps_f[:, t, :], act_f[u][:, t * P:(t + 1) * P], fwd[:, :], start=True, stop=True)
                ins.then_inc(f_up, 1)
            pairs(pe, body)


def stage_experts(nc, a):
    FT = F // P
    NU = 2 * E
    with ExitStack() as ctx:
        r = Room(nc, ctx, "ex")
        x_in, xs, xsT, out = ([r.sb(f"{n}{u}", s) for u in range(2)] for n, s in
                              (("x", [P, T, D]), ("xs", [P, T, D]), ("xsT", [P, DH, S]), ("out", [P, T, D])))
        junk = [r.sb(f"junk{u}", [P, T, D], BF16) for u in range(2)]
        ssq, msq, inv = ([r.sb(f"{n}{u}", [P, T]) for u in range(2)] for n in ("ssq", "msq", "inv"))
        hid = [r.sb(f"hid{u}", [P, FT, S]) for u in range(2)]
        wg, wu = ([r.sb(f"{n}{u}", [P, DH, F]) for u in range(2)] for n in ("wg", "wu"))
        wd = [r.sb(f"wd{u}", [P, FT, D]) for u in range(2)]
        nw = [r.sb(f"nw{u}", [P, DH]) for u in range(2)]
        mhalf = r.sb("mhalf", [P, T])
        ident = r.sb("ident", [P, P])
        ps_t = r.ps("ps_t", [P, DH, S])
        ps_g = [r.ps(f"ps_g{j}", [P, S]) for j in range(2)]
        ps_u = [r.ps(f"ps_u{j}", [P, S]) for j in range(2)]
        ps_d = r.ps("ps_d", [P, T, D])
        const_up = r.sem("const_up")
        ld, st, w_ld = ([r.sem(f"{n}{u}") for u in range(2)] for n in ("ld", "st", "w_ld"))
        sq_up, msq_up, inv_up, xs_up, t_up, xsT_up, gu_up, gelu_up, hid_up, d_up, out_up = (r.sem(n) for n in
            ("sq_up", "msq_up", "inv_up", "xs_up", "t_up", "xsT_up", "gu_up", "gelu_up", "hid_up", "d_up", "out_up"))
        block = ctx.enter_context(nc.Block())

        def quads(eng, body, first=None):
            if first:
                first()
            for j in range(4):
                body(j, j // 2, j % 2, 0, True)
            with eng.Fori(1, E // 2 - 1) as i:
                for j in range(4):
                    body(4 * i + j, j // 2, j % 2, i, True)
            for j in range(4):
                body(NU - 4 + j, j // 2, j % 2, E // 2 - 1, j < 3)

        @block.sync
        def _(sp):
            def weights(e, w):
                sp.dma_start(wg[w][:, :, :], a["L0_ffn_Wg"][e].rearrange("(h p) f -> p h f", p=P)).then_inc(w_ld[w], 16)
                sp.dma_start(wu[w][:, :, :], a["L0_ffn_Wu"][e].rearrange("(h p) f -> p h f", p=P)).then_inc(w_ld[w], 16)
                sp.dma_start(wd[w][:, :, :], a["L0_ffn_Wd"][e].rearrange("(h p) n -> p h n", p=P)).then_inc(w_ld[w], 16)
                sp.dma_start(nw[w][:, :], a["L0_ffn_norm_wP"][e]).then_inc(w_ld[w], 16)

            def rows(ap, m):
                return ap[bass.ds(m * S, S), :] if not isinstance(m, int) else ap[m * S:(m + 1) * S, :]

            def load(m, u):
                sp.dma_start(x_in[u][:, :, :], tok(rows(a["buf"], m))).then_inc(ld[u], 16)

            for u in range(2):
                load(u, u)
            weights(0, 0)
            weights(1, 1)

            def body(m, j, u, last):
                sp.wait_ge(out_up, m + 1)
                sp.dma_start(tok(rows(a["results"], m)), out[u][:, :, :]).then_inc(st[u], 16)
                if not last or j < 2:
                    load(m + 2, u)

            with sp.Fori(0, E // 2 - 1) as i:
                for j in range(4):
                    body(4 * i + j, j, j % 2, False)
                    if j % 2:
                        weights(2 * i + 2 + j // 2, j // 2)
            for j in range(4):
                body(NU - 4 + j, j, j % 2, True)
            for u in range(2):
                sp.wait_ge(st[u], 16 * NU // 2)

        @block.gpsimd
        def _(pool):
            pool.memset(mhalf[:, :], -0.5).then_inc(const_up, 1)
            pool.memset(ident[:, :], 0.0).then_inc(const_up, 1)
            pool.wait_ge(const_up, 2)
            pool.affine_select(out=ident[:, :], in_=ident[:, :], compare_op=ALU.not_equal, fill=1.0, base=0,
                               pattern=[[-1, P]], channel_multiplier=1).then_inc(const_up, 1)

            def body(m, w, u, i, more):
                pool.wait_ge(msq_up, m + 1)
                pool.tensor_tensor(inv[u][:, :], msq[u][:, :], mhalf[:, :], ALU.pow).then_inc(inv_up, 1)
            quads(pool, body)

        @block.scalar
        def _(act):
            def square(m, u):
                act.wait_ge(ld[u], 16 * (m // 2 + 1) if isinstance(m, int) else 8 * (m - u) + 16)
                wait(act, msq_up, m - 1)
                for t in range(T):
                    ins = act.activation(junk[u][:, t, :], x_in[u][:, t, :], ACT.Square, accum_out=ssq[u][:, t:t + 1])
                ins.then_inc(sq_up, 1)

            def turn(m, w, u):
                act.wait_ge(t_up, m + 1)
                wait(act, gu_up, FT * (m - 1))
                for h in range(DH):
                    ins = act.activation(xsT[u][:, h, :], ps_t[:, h, :], ACT.Copy, scale=nw[w][:, h:h + 1])
                ins.then_inc(xsT_up, 1)

            def first():
                act.wait_ge(w_ld[0], 64)
                square(0, 0)
                turn(0, 0, 0)

            def body(m, w, u, i, more):
                if more:
                    square(m + 1, 1 - u)
                wait(act, d_up, m - 1)
                for j in range(FT):
                    act.wait_ge(gu_up, FT * m + j + 1)
                    act.activation(hid[u][:, j, :], ps_g[j % 2][:, :], ACT.Gelu).then_inc(gelu_up, 1)
                if more:
                    if u:
                        act.wait_ge(w_ld[1 - w], 64 * (i + 1 + w))
                    turn(m + 1, w if u == 0 else 1 - w, 1 - u)
            quads(act, body, first)

        @block.vector
        def _(dve):
            def norm(m, u):
                dve.wait_ge(sq_up, m + 1)
                wait(dve, inv_up, m - 1)
                dve.tensor_scalar(msq[u][:, :], ssq[u][:, :], 1.0 / D, 1e-6, ALU.mult, ALU.add).then_inc(msq_up, 1)
                dve.wait_ge(inv_up, m + 1)
                wait(dve, t_up, m - 1)
                for t in range(T):
                    ins = dve.tensor_scalar(xs[u][:, t, :], x_in[u][:, t, :], inv[u][:, t:t + 1], None, ALU.mult)
                ins.then_inc(xs_up, 1)

            def body(m, w, u, i, more):
                if more:
                    norm(m + 1, 1 - u)
                for j in range(FT):
                    dve.wait_ge(gelu_up, FT * m + j + 1)
                    dve.tensor_tensor(hid[u][:, j, :], hid[u][:, j, :], ps_u[j % 2][:, :], ALU.mult).then_inc(hid_up, 1)
                dve.wait_ge(d_up, m + 1)
                wait(dve, st[u], 16 * (m // 2) if isinstance(m, int) else 8 * (m - u))
                dve.tensor_tensor(out[u][:, :, :], ps_d[:, :, :], x_in[u][:, :, :], ALU.add).then_inc(out_up, 1)
            quads(dve, body, lambda: norm(0, 0))

        @block.tensor
        def _(pe):
            pe.wait_ge(const_up, 3)

            def turn(m, u):
                pe.wait_ge(xs_up, m + 1)
                wait(pe, xsT_up, m)
                for h in range(DH):
                    for t in range(T):
                        ins = pe.transpose(ps_t[:, h, t * P:(t + 1) * P], xs[u][:, t, h * P:(h + 1) * P], ident[:, :])
                ins.then_inc(t_up, 1)

            def body(m, w, u, i, more):
                if u == 0:
                    pe.wait_ge(w_ld[w], 64 * (i + 1))
                pe.wait_ge(xsT_up, m + 1)
                for j in range(FT):
                    wait(pe, hid_up, FT * m + j - 1)
                    for wt, ps in ((wg[w], ps_g[j % 2]), (wu[w], ps_u[j % 2])):
                        for h in range(DH):
                            ins = pe.matmul(ps[:, :], wt[:, h, j * P:(j + 1) * P], xsT[u][:, h, :], start=(h == 0), stop=(h == DH - 1))
                    ins.then_inc(gu_up, 1)
                if more:
                    turn(m + 1, 1 - u)
                pe.wait_ge(hid_up, FT * m + FT)
                wait(pe, out_up, m)
                for t in range(T):
                    for j in range(FT):
                        ins = pe.matmul(ps_d[:, t, :], hid[u][:, j, t * P:(t + 1) * P], wd[w][:, j, :], start=(j == 0), stop=(j == FT - 1))
                ins.then_inc(d_up, 1)
            quads(pe, body, lambda: turn(0, 0))


M = 64


def moments(dve, then, z, st6, mv, ve, past_dve):
    for t in range(T):
        ins = dve.bn_stats(st6[:, t, :], z[:, t, :])
    then(ins)
    apart(dve, past_dve)
    for t in range(T):
        ins = dve.bn_aggr(mv[:, t, :], st6[:, t, :])
    then(ins)
    return dve.tensor_scalar(ve[:, :], mv[:, :, 1], 1e-5, None, ALU.add)


def normalized(dve, out, z, mv, rstd):
    for t in range(T):
        ins = dve.tensor_scalar(out[:, t, :], z[:, t, :], mv[:, t, 0:1], rstd[:, t:t + 1], ALU.subtract, ALU.mult)
    return ins


def stage_memory(nc, a, route_w, route_i):
    FADE = S.bit_length() - 1
    with ExitStack() as ctx:
        r = Room(nc, ctx, "me")
        x_in, fb = ([r.sb(f"{n}{u}", [P, T, D]) for u in range(2)] for n in ("x", "fb"))
        rows = [r.sb(f"rows{u}", [P, 2, T, D]) for u in range(2)]
        idx = [r.sb(f"idx{u}", [P, 2, T], U32) for u in range(2)]
        wt = [r.sb(f"wt{u}", [P, 4, T]) for u in range(2)]
        x3, x3b, x4 = ([r.sb(f"{n}{u}", [P, T, D]) for u in range(2)] for n in ("x3", "x3b", "x4"))
        x3T = [r.sb(f"x3T{u}", [P, DH, S]) for u in range(2)]
        z, z2 = r.sb("z", [P, T, D]), r.sb("z2", [P, T, D])
        st6, st6b, mv, mvb = r.sb("st6", [P, T, 6]), r.sb("st6b", [P, T, 6]), r.sb("mv", [P, T, 2]), r.sb("mvb", [P, T, 2])
        ve, veb, rstd, rstdb, mhalf = (r.sb(n, [P, T]) for n in ("ve", "veb", "rstd", "rstdb", "mhalf"))
        wq, wk = r.sb("wq", [P, DH, P]), r.sb("wk", [P, DH, P])
        wv = r.sb("wv", [P, DH, M + 2])
        wo = r.sb("wo", [P, D])
        bo = r.sb("bo", [P, D])
        bg, dp, sg = (r.sb(n, [P, 1]) for n in ("bg", "dp", "sg"))
        decay = r.sb("decay", [P, FADE + 1])
        age_i = r.sb("age_i", [P, 1], mybir.dt.int32)
        age, fade = r.sb("age", [P, 1]), r.sb("fade", [P, S])
        ident = r.sb("ident", [P, P])
        qT, kT, oT = ([r.sb(f"{n}{u}", [P, S]) for u in range(2)] for n in ("qT", "kT", "oT"))
        gv = r.sb("gv", [P, T, P])
        g, g2 = r.sb("g", [P, T]), r.sb("g2", [P, T])
        aT = [r.sb(f"aT{j}", [P, S]) for j in range(2)]
        ps_t, ps_y = r.ps("ps_t", [P, DH, S]), r.ps("ps_y", [P, T, D])
        ps_v, ps_o = r.ps("ps_v", [P, T, P]), r.ps("ps_o", [P, S])
        ps_a = [r.ps(f"ps_a{j}", [P, S]) for j in range(2)]
        c_ld, const_up, pad_up, fade_up, past_dve, past_pool = (r.sem(n) for n in
            ("c_ld", "const_up", "pad_up", "fade_up", "past_dve", "past_pool"))
        ld, gat, st = ([r.sem(f"{n}{u}") for u in range(2)] for n in ("ld", "gat", "st"))
        idx_up, vf, vb, var_up, rstd_up, x3_up, xb_up, varb_up, rstdb_up = (r.sem(n) for n in
            ("idx_up", "vf", "vb", "var_up", "rstd_up", "x3_up", "xb_up", "varb_up", "rstdb_up"))
        t_up, xT_up, q_up, qk_s, v_up, g_up, gv_up, a_up, at_up, o_up, oT_up, y_up, z2_up, x4_up = (r.sem(n) for n in
            ("t_up", "xT_up", "q_up", "qk_s", "v_up", "g_up", "gv_up", "a_up", "at_up", "o_up", "oT_up", "y_up", "z2_up", "x4_up"))
        grown = r.sem("grown")
        z_up, at_free = r.sem("z_up"), r.sem("at_free")
        NF, NB = 6, 3
        block = ctx.enter_context(nc.Block())

        @block.sync
        def _(sp):
            sp.wait_ge(pad_up, 4)
            for w, n in ((wq, "Wq"), (wk, "Wk"), (wv, "Wv")):
                sp.dma_start(w[:, :, 0:M], a[f"L1_attn_{n}"].rearrange("(h p) m -> p h m", p=P)).then_inc(c_ld, 16)
            with nc.allow_non_contiguous_dma(reason="256 weights"):
                sp.dma_start(wv[:, :, M:M + 1], a["L1_attn_Wg"].rearrange("(h p) m -> p h m", p=P)).then_inc(c_ld, 16)
            sp.dma_start(wo[0:M, :], a["L1_attn_Wo"]).then_inc(c_ld, 16)
            for w, n in ((bo, "bo"), (bg, "bg"), (dp, "decay_param")):
                sp.dma_start(w[:, :], row_bc(a[f"L1_attn_{n}"], P)).then_inc(c_ld, 16)

            def load(b, u):
                sp.dma_start(x_in[u][:, :, :], tok(a["x2"][b])).then_inc(ld[u], 16)
                sp.dma_start(fb[u][:, :, :], tok(a["fallback"][b])).then_inc(ld[u], 16)

            def store(b, u):
                sp.wait_ge(x4_up, b + 1)
                sp.dma_start(tok(a["x4"][b]), x4[u][:, :, :]).then_inc(st[u], 16)

            for u in range(2):
                load(u, u)
            with sp.Fori(0, B // 2 - 1) as i:
                for u in range(2):
                    sp.wait_ge(x3_up, 2 * i + u + 1)
                    load(2 * i + u + 2, u)
                    store(2 * i + u, u)
            for u in range(2):
                store(B - 2 + u, u)
            for u in range(2):
                sp.wait_ge(st[u], 16 * B // 2)

        @block.gpsimd
        def _(pool):
            for w in (wq[:, :, :], wk[:, :, :], wv[:, :, :], wo[:, :]):
                pool.memset(w, 0.0).then_inc(pad_up, 1)
            pool.memset(gv[:, :, :], 0.0).then_inc(const_up, 1)
            pool.memset(mhalf[:, :], -0.5).then_inc(const_up, 1)
            pool.memset(ident[:, :], 0.0).then_inc(const_up, 1)
            pool.iota(age_i[:, :], pattern=[[1, 1]], base=0, channel_multiplier=-1).then_inc(const_up, 1)
            pool.wait_ge(const_up, 4)
            pool.tensor_copy(age[:, :], age_i[:, :]).then_inc(const_up, 1)
            pool.affine_select(out=ident[:, :], in_=ident[:, :], compare_op=ALU.not_equal, fill=1.0, base=0,
                               pattern=[[-1, P]], channel_multiplier=1).then_inc(const_up, 1)

            def gather(b, u):
                pool.wait_ge(idx_up, b + 1)
                apart(pool, past_pool)
                for n in range(2):
                    for t in range(T):
                        pool.indirect_dma_start(out=rows[u][:, n, t, :], out_offset=None, in_=a["results"],
                                                in_offset=bass.IndirectOffsetOnAxis(ap=idx[u][:, n, t:t + 1], axis=0)).then_inc(gat[u], 16)

            gather(0, 0)
            gather(1, 1)
            pool.wait_ge(fade_up, 2)
            pool.wait_ge(const_up, 6)
            pool.tensor_tensor(fade[:, 0:1], decay[:, 0:1], age[:, 0:1], ALU.pow).then_inc(fade_up, 1)
            pool.wait_ge(grown, 2 * FADE)
            pool.affine_select(out=fade[:, :], in_=fade[:, :], compare_op=ALU.is_ge, fill=0.0, base=0,
                               pattern=[[1, S]], channel_multiplier=-1).then_inc(fade_up, 1)
            pool.wait_ge(c_ld, 128)

            def front(b, u, i):
                pool.wait_ge(var_up, b + 1)
                pool.tensor_tensor(rstd[:, :], ve[:, :], mhalf[:, :], ALU.pow).then_inc(rstd_up, 1)
                pool.wait_ge(x3_up, b + 1)
                wait(pool, z2_up, b - 1)
                pool.tensor_tensor(x3b[u][:, :, :], x3[u][:, :, :], row(bo[:, :]).to_broadcast([P, T, D]), ALU.add).then_inc(xb_up, 1)

            def back(b):
                pool.wait_ge(varb_up, b + 1)
                pool.tensor_tensor(rstdb[:, :], veb[:, :], mhalf[:, :], ALU.pow).then_inc(rstdb_up, 1)

            front(0, 0, 0)
            gather(2, 0)
            front(1, 1, 0)
            gather(3, 1)
            back(0)
            with pool.Fori(1, B // 2 - 1) as i:
                for u in range(2):
                    front(2 * i + u, u, i)
                    gather(2 * i + u + 2, u)
                    back(2 * i + u - 1)
            for u in range(2):
                front(B - 2 + u, u, B // 2 - 1)
                back(B - 3 + u)
            back(B - 1)

        @block.scalar
        def _(act):
            act.wait_ge(c_ld, 128)
            act.activation(sg[:, :], dp[:, :], ACT.Sigmoid).then_inc(fade_up, 1)

            def body(b, u, i):
                act.wait_ge(t_up, b + 1)
                wait(act, v_up, b - 1)
                act.activation(x3T[u][:, :, :], ps_t[:, :, :], ACT.Copy).then_inc(xT_up, 1)
                for n, dst in enumerate((qT, kT)):
                    act.wait_ge(q_up, 2 * b + n + 1)
                    wait(act, a_up, 4 * (b - 1))
                    act.activation(dst[u][:, :], ps_a[n][:, :], ACT.Copy).then_inc(qk_s, 1)
                act.wait_ge(v_up, b + 1)
                wait(act, gv_up, b)
                act.activation(g[:, :], ps_v[:, :, M], ACT.Sigmoid, bias=bg[:, 0:1]).then_inc(g_up, 1)
                act.wait_ge(o_up, b + 1)
                wait(act, y_up, b - 1)
                act.activation(oT[u][:, :], ps_o[:, :], ACT.Copy).then_inc(oT_up, 1)
            pairs(act, body)

        @block.vector
        def _(dve):
            def stepper(sem, steps, b):
                step = [0]

                def then(ins):
                    step[0] += 1
                    ins.then_inc(sem, 1)
                    dve.wait_ge(sem, steps * b + step[0])
                return then

            def indices(b, u):
                wait(dve, gat[u], 64 * (b - u))
                dve.tensor_copy(idx[u][:, :, :], route_i[:, bass.ds(b, 1), :, :].rearrange("p o n t -> p (o n) t")).then_inc(idx_up, 1)

            def front(b, u, i, more=True):
                then = stepper(vf, NF, b)
                rw = route_w[:, bass.ds(b, 1), :, :]
                dve.tensor_scalar(wt[u][:, 0, :], rw[:, :, 2, :].rearrange("p o t -> p (o t)"), -1.0, 2.0, ALU.mult, ALU.add)
                dve.tensor_copy(wt[u][:, 1, :], rw[:, :, 2, :].rearrange("p o t -> p (o t)"))
                then(dve.tensor_copy(wt[u][:, 2:4, :], rw[:, :, 0:2, :].rearrange("p o n t -> p (o n) t")))
                dve.wait_ge(ld[u], 32 * i + 32)
                for t in range(T):
                    ins = dve.tensor_scalar(z[:, t, :], x_in[u][:, t, :], wt[u][:, 0, t:t + 1], None, ALU.mult)
                then(ins)
                dve.wait_ge(gat[u], 128 * i + 128)
                for n, src in ((1, fb[u]), (2, rows[u][:, 0, :, :]), (3, rows[u][:, 1, :, :])):
                    for t in range(T):
                        ins = dve.scalar_tensor_tensor(z[:, t, :], src[:, t, :], wt[u][:, n, t:t + 1], z[:, t, :], ALU.mult, ALU.add)
                    if n < 3:
                        then(ins)
                    else:
                        ins.then_inc(z_up, 1)
                if more:
                    indices(b + 2, u)
                dve.wait_ge(z_up, b + 1)
                moments(dve, then, z, st6, mv, ve, past_dve).then_inc(var_up, 1)
                dve.wait_ge(rstd_up, b + 1)
                normalized(dve, x3[u], z, mv, rstd).then_inc(x3_up, 1)

            def back(b, u, i):
                then = stepper(vb, NB, b)
                dve.wait_ge(g_up, b + 1)
                then(dve.tensor_tensor(g2[:, :], g[:, :], g[:, :], ALU.mult))
                wait(dve, o_up, b)
                dve.tensor_tensor(gv[:, :, 0:M], ps_v[:, :, 0:M], col(g2[:, :]).to_broadcast([P, T, M]), ALU.mult).then_inc(gv_up, 1)
                for j in range(T):
                    dve.wait_ge(a_up, 4 * b + j + 1)
                    if j < 2:
                        wait(dve, o_up, b)
                    else:
                        dve.wait_ge(at_free, 2 * b + j - 1)
                    dve.tensor_tensor(aT[j % 2][:, 0:S - j * P], ps_a[j % 2][:, 0:S - j * P], fade[:, 0:S - j * P], ALU.mult).then_inc(at_up, 1)
                dve.wait_ge(y_up, b + 1)
                dve.wait_ge(xb_up, b + 1)
                dve.tensor_tensor(z2[:, :, :], ps_y[:, :, :], x3b[u][:, :, :], ALU.add).then_inc(z2_up, 1)
                dve.wait_ge(z2_up, b + 1)
                moments(dve, then, z2, st6b, mvb, veb, past_dve).then_inc(varb_up, 1)
                dve.wait_ge(rstdb_up, b + 1)
                wait(dve, st[u], 16 * i)
                normalized(dve, x4[u], z2, mvb, rstdb).then_inc(x4_up, 1)

            indices(0, 0)
            indices(1, 1)
            dve.wait_ge(fade_up, 1)
            dve.tensor_scalar(decay[:, 0:1], sg[:, :], 0.999 - 0.9, 0.9, ALU.mult, ALU.add).then_inc(fade_up, 1)
            dve.wait_ge(fade_up, 3)
            for n in range(FADE):
                dve.tensor_tensor(decay[:, n + 1:n + 2], decay[:, n:n + 1], decay[:, n:n + 1], ALU.mult).then_inc(grown, 1)
                dve.tensor_scalar(fade[:, 1 << n:2 << n], fade[:, 0:1 << n], decay[:, n:n + 1], None, ALU.mult).then_inc(grown, 1)
                dve.wait_ge(grown, 2 * n + 2)
            dve.wait_ge(fade_up, 4)
            dve.wait_ge(const_up, 6)
            front(0, 0, 0)
            front(1, 1, 0)
            back(0, 0, 0)
            with dve.Fori(1, B // 2 - 1) as i:
                for u in range(2):
                    front(2 * i + u, u, i)
                    back(2 * i + u - 1, 1 - u, i - 1 + u)
            for u in range(2):
                front(B - 2 + u, u, B // 2 - 1, False)
                back(B - 3 + u, 1 - u, B // 2 - 2 + u)
            back(B - 1, 1, B // 2 - 1)

        @block.tensor
        def _(pe):
            pe.wait_ge(const_up, 6)
            pe.wait_ge(c_ld, 128)

            def body(b, u, i):
                pe.wait_ge(x3_up, b + 1)
                for h in range(DH):
                    for t in range(T):
                        ins = pe.transpose(ps_t[:, h, t * P:(t + 1) * P], x3[u][:, t, h * P:(h + 1) * P], ident[:, :])
                ins.then_inc(t_up, 1)
                pe.wait_ge(xT_up, b + 1)
                wait(pe, at_up, 4 * b)
                for n, w in enumerate((wq, wk)):
                    for h in range(DH):
                        ins = pe.matmul(ps_a[n][:, :], w[:, h, :], x3T[u][:, h, :], start=(h == 0), stop=(h == DH - 1))
                    ins.then_inc(q_up, 1)
                wait(pe, gv_up, b)
                for t in range(T):
                    for h in range(DH):
                        ins = pe.matmul(ps_v[:, t, 0:M + 2], x3T[u][:, h, t * P:(t + 1) * P], wv[:, h, :], start=(h == 0), stop=(h == DH - 1))
                ins.then_inc(v_up, 1)
                pe.wait_ge(qk_s, 2 * b + 2)

                def scores(j):
                    pe.matmul(ps_a[j % 2][:, 0:S - j * P], kT[u][:, j * P:(j + 1) * P], qT[u][:, j * P:S], start=True, stop=True).then_inc(a_up, 1)

                def reading(j):
                    pe.wait_ge(at_up, 4 * b + j + 1)
                    if j == 0:
                        pe.wait_ge(gv_up, b + 1)
                        wait(pe, oT_up, b)
                    ins = pe.matmul(ps_o[:, j * P:S], gv[:, j, :], aT[j % 2][:, 0:S - j * P], start=(j == 0), stop=(j == T - 1))
                    ins.then_inc(at_free if j < 2 else o_up, 1) if j != 2 else None

                scores(0)
                scores(1)
                for j in range(T):
                    reading(j)
                    if j < 2:
                        scores(j + 2)
                pe.wait_ge(oT_up, b + 1)
                wait(pe, z2_up, b)
                for t in range(T):
                    ins = pe.matmul(ps_y[:, t, :], oT[u][:, t * P:(t + 1) * P], wo[:, :], start=True, stop=True)
                ins.then_inc(y_up, 1)
            pairs(pe, body)


def stage_xattn1(nc, a):
    MASKED = -1.0e9
    with ExitStack() as ctx:
        r = Room(nc, ctx, "xb")
        x_in, xb = ([r.sb(f"{n}{u}", [P, T, D]) for u in range(2)] for n in ("x", "xb"))
        cT = [r.sb(f"cT{u}", [P, DH, S]) for u in range(2)]
        mask = [r.sb(f"mask{u}", [P, T, S], U8) for u in range(2)]
        wq, wk, wv, woT = (r.sb(n, [P, DH, D]) for n in ("wq", "wk", "wv", "woT"))
        wqk, wvo = r.sb("wqk", [P, DH, D]), r.sb("wvo", [P, DH, D])
        bq, bk, bv = (r.sb(n, [P, DH]) for n in ("bq", "bk", "bv"))
        bqw, bvw = r.sb("bqw", [P, DH, P]), r.sb("bvw", [P, DH, P])
        g_bias, cq_w = r.sb("g_bias", [P, DH]), r.sb("cq_w", [P, DH, 2])
        cq_b, v_bias, bo = r.sb("cq_b", [P, 1]), r.sb("v_bias", [P, D]), r.sb("bo", [P, D])
        xT, gT = ([r.sb(f"{n}{u}", [P, DH, S]) for u in range(2)] for n in ("xT", "gT"))
        v = [r.sb(f"v{u}", [P, T, D]) for u in range(2)]
        cq = [r.sb(f"cq{u}", [P, T]) for u in range(2)]
        s = [r.sb(f"s{j}", [P, S]) for j in range(2)]
        ex = [r.sb(f"ex{j}", [P, S]) for j in range(2)]
        exT = [r.sb(f"exT{j}", [P, T, P]) for j in range(2)]
        nmax, rsum, rinv = ([r.sb(f"{n}{j}", [P, 1]) for j in range(2)] for n in ("nmax", "rsum", "rinv"))
        masked = r.sb("masked", [P, S])
        z = r.sb("z", [P, T, D])
        st6, mv = r.sb("st6", [P, T, 6]), r.sb("mv", [P, T, 2])
        ve, rstd, mhalf = (r.sb(n, [P, T]) for n in ("ve", "rstd", "mhalf"))
        x5 = [r.sb(f"x5{u}", [P, T, D]) for u in range(2)]
        ident = r.sb("ident", [P, P])
        ps_x = r.ps("ps_x", [P, DH, S])
        ps_s = [r.ps(f"ps_s{j}", [P, S]) for j in range(2)]
        ps_t = r.ps("ps_t", [P, T, P])
        ps_o = r.ps("ps_o", [P, D])
        ps_v = r.ps("ps_v", [P, 2, D])
        ps_q = r.ps("ps_q", [P, T, 2])
        c_ld, const_up, w_up, wc, past_dve, past_sp = (r.sem(n) for n in ("c_ld", "const_up", "w_up", "wc", "past_dve", "past_sp"))
        ld, st = ([r.sem(f"{n}{u}") for u in range(2)] for n in ("ld", "st"))
        t_up, xT_up, g_up, gT_up, v_up, v_s, cq_up, cq_s = (r.sem(n) for n in ("t_up", "xT_up", "g_up", "gT_up", "v_up", "v_s", "cq_up", "cq_s"))
        s_up, s_s, s_m, max_up, exp_up, et_up, eT_up, o_up, rinv_up, z_up = (r.sem(n) for n in
            ("s_up", "s_s", "s_m", "max_up", "exp_up", "et_up", "eT_up", "o_up", "rinv_up", "z_up"))
        xb_up, steps, var_up, rstd_up, x5_up = (r.sem(n) for n in ("xb_up", "steps", "var_up", "rstd_up", "x5_up"))
        block = ctx.enter_context(nc.Block())

        def batches(eng, body):
            body(0, 0, 0, True)
            body(1, 1, 0, True)
            with eng.Fori(1, B // 2 - 1) as i:
                for u in range(2):
                    body(2 * i + u, u, i, True)
            body(B - 2, 0, B // 2 - 1, True)
            body(B - 1, 1, B // 2 - 1, False)

        @block.sync
        def _(sp):
            for w, n in ((wq, "Wq"), (wk, "Wk"), (wv, "Wv"), (woT, "WoT")):
                sp.dma_start(w[:, :, :], a[f"L1_xattn_{n}"].rearrange("(h p) n -> p h n", p=P)).then_inc(c_ld, 16)
            with nc.allow_non_contiguous_dma(reason="256 biases"):
                for w, n in ((bq, "bq"), (bk, "bk"), (bv, "bv")):
                    sp.dma_start(w[:, :], a[f"L1_xattn_{n}"].rearrange("(h p) -> p h", p=P)).then_inc(c_ld, 16)
            sp.dma_start(bo[:, :], row_bc(a["L1_xattn_bo"], P)).then_inc(c_ld, 16)

            def load(b, u):
                sp.dma_start(x_in[u][:, :, :], tok(a["x4"][b])).then_inc(ld[u], 16)
                sp.dma_start(cT[u][:, :, :], a["ctxT"][b].rearrange("(h p) s -> p h s", p=P)).then_inc(ld[u], 16)
                sp.dma_start(mask[u][:, :, :], a["mask"][b].rearrange("(t p) s -> p t s", p=P)).then_inc(ld[u], 16)

            def store(b, u):
                sp.wait_ge(x5_up, b + 1)
                sp.dma_start(tok(a["x5"][b]), x5[u][:, :, :]).then_inc(st[u], 16)

            for u in range(2):
                load(u, u)
            with sp.Fori(0, B // 2 - 1) as i:
                for u in range(2):
                    b = 2 * i + u
                    sp.wait_ge(s_m, T * b + T)
                    apart(sp, past_sp)
                    sp.wait_ge(t_up, b + 1)
                    sp.wait_ge(xb_up, b + 1)
                    load(b + 2, u)
                    store(b, u)
            for u in range(2):
                store(B - 2 + u, u)
            for u in range(2):
                sp.wait_ge(st[u], 16 * B // 2)

        @block.gpsimd
        def _(pool):
            pool.memset(mhalf[:, :], -0.5).then_inc(const_up, 1)
            pool.memset(masked[:, :], MASKED).then_inc(const_up, 1)
            pool.memset(ident[:, :], 0.0).then_inc(const_up, 1)
            pool.wait_ge(const_up, 3)
            pool.affine_select(out=ident[:, :], in_=ident[:, :], compare_op=ALU.not_equal, fill=1.0, base=0,
                               pattern=[[-1, P]], channel_multiplier=1).then_inc(const_up, 1)
            pool.wait_ge(c_ld, 128)
            pool.tensor_copy(bqw[:, :, :], col(bq[:, :]).to_broadcast([P, DH, P])).then_inc(wc, 1)
            pool.tensor_copy(bvw[:, :, :], col(bv[:, :]).to_broadcast([P, DH, P])).then_inc(wc, 1)

            def residual(b, u, i):
                pool.wait_ge(ld[u], 48 * i + 48)
                wait(pool, z_up, T * (b - 1))
                pool.tensor_tensor(xb[u][:, :, :], x_in[u][:, :, :], row(bo[:, :]).to_broadcast([P, T, D]), ALU.add).then_inc(xb_up, 1)

            def root(b):
                pool.wait_ge(var_up, b + 1)
                pool.tensor_tensor(rstd[:, :], ve[:, :], mhalf[:, :], ALU.pow).then_inc(rstd_up, 1)

            def body(b, u, i, more):
                residual(b, u, i)
                if not isinstance(b, int) or b > 0:
                    root(b - 1)
            batches(pool, body)
            root(B - 1)

        @block.scalar
        def _(act):
            act.wait_ge(w_up, 1)
            for h in range(DH):
                ins = act.activation(wqk[:, h, :], ps_x[:, h, 0:D], ACT.Copy)
                ins = act.activation(wvo[:, h, :], ps_x[:, h, D:2 * D], ACT.Copy)
            act.activation(v_bias[:, :], ps_v[:, 0, :], ACT.Copy)
            act.activation(g_bias[:, :], ps_q[:, 0, :], ACT.Copy)
            act.activation(cq_w[:, :, 0], ps_q[:, 1, :], ACT.Copy)
            act.activation(cq_w[:, :, 1], ps_q[:, 1, :], ACT.Copy)
            act.activation(cq_b[:, :], ps_q[:, 2, 0:1], ACT.Copy).then_inc(wc, 1)
            act.wait_ge(wc, 3)

            def turned(b, u):
                act.wait_ge(t_up, b + 1)
                wait(act, g_up, b - 1)
                wait(act, cq_up, b - 1)
                act.activation(xT[u][:, :, :], ps_x[:, :, :], ACT.Copy).then_inc(xT_up, 1)

            def side(b, u):
                act.wait_ge(cq_up, b + 1)
                wait(act, s_s, T * (b - 1))
                act.activation(cq[u][:, :], ps_q[:, :, 0], ACT.Identity, bias=cq_b[:, 0:1]).then_inc(cq_s, 1)
                act.wait_ge(g_up, b + 1)
                for h in range(DH):
                    ins = act.activation(gT[u][:, h, :], ps_x[:, h, :], ACT.Identity, bias=g_bias[:, h:h + 1])
                ins.then_inc(gT_up, 1)

            turned(0, 0)
            side(0, 0)
            act.wait_ge(cq_s, 1)

            def body(b, u, i, more):
                for t in range(T):
                    n, j = T * b + t, t % 2
                    act.wait_ge(s_up, n + 1)
                    wait(act, exp_up, n - 1)
                    act.activation(s[j][:, :], ps_s[j][:, :], ACT.Identity, bias=cq[u][:, t:t + 1]).then_inc(s_s, 1)
                    act.wait_ge(max_up, n + 1)
                    wait(act, et_up, n - 1)
                    wait(act, rinv_up, n - 1)
                    act.activation(ex[j][:, :], s[j][:, :], ACT.Exp, bias=nmax[j][:, 0:1], accum_out=rsum[j][:, 0:1]).then_inc(exp_up, 1)
                    if more and t == 1:
                        turned(b + 1, 1 - u)
                    if more and t == 3:
                        side(b + 1, 1 - u)
                        act.wait_ge(cq_s, b + 2)
            batches(act, body)

        @block.vector
        def _(dve):
            dve.wait_ge(wc, 3)

            def values(b, u, half):
                dve.wait_ge(v_up, 2 * b + half + 1)
                if half == 0:
                    wait(dve, o_up, T * (b - 1))
                dve.tensor_tensor(v[u][:, 2 * half:2 * half + 2, :], ps_v[:, :, :], row(v_bias[:, :]).to_broadcast([P, 2, D]), ALU.add).then_inc(v_s, 1)

            def exps(n, j, real=True):
                dve.wait_ge(et_up, n + 1)
                wait(dve, o_up, n - 1)
                dve.tensor_copy(exT[j][:, :, :], ps_t[:, :, :]).then_inc(eT_up, 1)

            def out(n, b, t, j, u):
                dve.wait_ge(exp_up, n + 1)
                dve.wait_ge(o_up, n + 1)
                dve.reciprocal(rinv[j][:, :], rsum[j][:, :]).then_inc(rinv_up, 1)
                dve.wait_ge(rinv_up, n + 1)
                dve.wait_ge(xb_up, b + 1)
                dve.scalar_tensor_tensor(z[:, t, :], ps_o[:, :], rinv[j][:, 0:1], xb[u][:, t, :], ALU.mult, ALU.add).then_inc(z_up, 1)

            def norm(b, u, i):
                def then(ins):
                    then.n += 1
                    ins.then_inc(steps, 1)
                    dve.wait_ge(steps, 2 * b + then.n)
                then.n = 0
                dve.wait_ge(z_up, T * b + T)
                moments(dve, then, z, st6, mv, ve, past_dve).then_inc(var_up, 1)

            def finish(b, u, i):
                dve.wait_ge(rstd_up, b + 1)
                wait(dve, st[u], 16 * i)
                normalized(dve, x5[u], z, mv, rstd).then_inc(x5_up, 1)

            values(0, 0, 0)
            values(0, 0, 1)

            def body(b, u, i, more):
                before = not isinstance(b, int) or b > 0
                pb, pu, pi = b - 1, 1 - u, i - 1 + u
                for t in range(T):
                    n, j = T * b + t, t % 2
                    dve.wait_ge(s_s, n + 1)
                    apart(dve, past_dve)
                    dve.copy_predicated(s[j][:, :], mask[u][:, t, :], masked[:, :]).then_inc(s_m, 1)
                    dve.wait_ge(s_m, n + 1)
                    dve.tensor_reduce(nmax[j][:, :], s[j][:, :], AX.X, ALU.max, negate=True).then_inc(max_up, 1)
                    if t > 0 or before:
                        exps(n - 1, 1 - j)
                    if t >= 2:
                        out(n - 2, b, t - 2, j, u)
                    elif before:
                        out(n - 2, pb, t + 2, j, pu)
                    if t == 1 and before:
                        norm(pb, pu, pi)
                    if more and t >= 2:
                        values(b + 1, 1 - u, t - 2)
                    if t == 1 and before:
                        finish(pb, pu, pi)
            batches(dve, body)
            exps(T * B - 1, 1)
            out(T * B - 2, B - 1, 2, 0, 1)
            out(T * B - 1, B - 1, 3, 1, 1)
            norm(B - 1, 1, B // 2 - 1)
            finish(B - 1, 1, B // 2 - 1)

        @block.tensor
        def _(pe):
            pe.wait_ge(const_up, 4)
            pe.wait_ge(wc, 2)
            for m in range(DH):
                for c, (lw, rw_) in enumerate(((wq, wk), (wv, woT))):
                    for h in range(DH):
                        pe.matmul(ps_x[:, m, c * D:(c + 1) * D], lw[:, h, m * P:(m + 1) * P], rw_[:, h, :], start=(h == 0), stop=(h == DH - 1))
                for c, (lw, rb_) in enumerate(((wk, bq), (wq, bk))):
                    for h in range(DH):
                        pe.matmul(ps_q[:, c, m:m + 1], lw[:, h, m * P:(m + 1) * P], rb_[:, h:h + 1], start=(h == 0), stop=(h == DH - 1))
            for h in range(DH):
                pe.matmul(ps_v[:, 0, :], bvw[:, h, :], woT[:, h, :], start=(h == 0), stop=(h == DH - 1))
            for h in range(DH):
                ins = pe.matmul(ps_q[:, 2, 0:1], bqw[:, h, :], bk[:, h:h + 1], start=(h == 0), stop=(h == DH - 1))
            ins.then_inc(w_up, 1)
            pe.wait_ge(wc, 3)

            def turn(b, u, i):
                pe.wait_ge(ld[u], 48 * i + 48)
                wait(pe, gT_up, b)
                for h in range(DH):
                    for t in range(T):
                        ins = pe.transpose(ps_x[:, h, t * P:(t + 1) * P], x_in[u][:, t, h * P:(h + 1) * P], ident[:, :])
                ins.then_inc(t_up, 1)

            def side(b, u):
                pe.wait_ge(xT_up, b + 1)
                wait(pe, cq_s, b)
                for t in range(T):
                    for h in range(DH):
                        ins = pe.matmul(ps_q[:, t, :], xT[u][:, h, t * P:(t + 1) * P], cq_w[:, h, :], start=(h == 0), stop=(h == DH - 1))
                ins.then_inc(cq_up, 1)
                for m in range(DH):
                    for h in range(DH):
                        ins = pe.matmul(ps_x[:, m, :], wqk[:, h, m * P:(m + 1) * P], xT[u][:, h, :], start=(h == 0), stop=(h == DH - 1))
                ins.then_inc(g_up, 1)

            def values(b, u, half):
                wait(pe, v_s, 2 * b + half)
                for t in range(2):
                    for h in range(DH):
                        ins = pe.matmul(ps_v[:, t, :], cT[u][:, h, (2 * half + t) * P:(2 * half + t + 1) * P], wvo[:, h, :],
                                        start=(h == 0), stop=(h == DH - 1))
                ins.then_inc(v_up, 1)

            def turn_exps(n, j):
                pe.wait_ge(exp_up, n + 1)
                wait(pe, eT_up, n)
                for k in range(T):
                    ins = pe.transpose(ps_t[:, k, :], ex[j][:, k * P:(k + 1) * P], ident[:, :])
                ins.then_inc(et_up, 1)

            def out(n, j, u):
                pe.wait_ge(eT_up, n + 1)
                wait(pe, z_up, n)
                for k in range(T):
                    ins = pe.matmul(ps_o[:, :], exT[j][:, k, :], v[u][:, k, :], start=(k == 0), stop=(k == T - 1))
                ins.then_inc(o_up, 1)

            turn(0, 0, 0)
            side(0, 0)
            values(0, 0, 0)
            values(0, 0, 1)

            def body(b, u, i, more):
                before = not isinstance(b, int) or b > 0
                for t in range(T):
                    n, j = T * b + t, t % 2
                    if t == 0:
                        pe.wait_ge(gT_up, b + 1)
                        pe.wait_ge(v_s, 2 * b + 2)
                    wait(pe, s_s, n - 1)
                    for h in range(DH):
                        ins = pe.matmul(ps_s[j][:, :], gT[u][:, h, t * P:(t + 1) * P], cT[u][:, h, :], start=(h == 0), stop=(h == DH - 1))
                    ins.then_inc(s_up, 1)
                    if more and t == 1:
                        turn(b + 1, 1 - u, i + u)
                    if more and t == 2:
                        side(b + 1, 1 - u)
                        values(b + 1, 1 - u, 0)
                    if more and t == 3:
                        values(b + 1, 1 - u, 1)
                    if t > 0 or before:
                        turn_exps(n - 1, 1 - j)
                    if t >= 2:
                        out(n - 2, j, u)
                    elif before:
                        out(n - 2, j, 1 - u)
            batches(pe, body)
            turn_exps(T * B - 1, 1)
            out(T * B - 2, 0, 1)
            out(T * B - 1, 1, 1)


def stage_gated(nc, a):
    THRESHOLD = 0.1
    NV = 9
    with ExitStack() as ctx:
        r = Room(nc, ctx, "ga")
        x_in = [r.sb(f"x{u}", [P, T, D]) for u in range(2)]
        xT = [r.sb(f"xT{u}", [P, DH, S]) for u in range(2)]
        ew = r.sb("ew", [P, DH, E, D])
        eb = r.sb("eb", [E, D])
        gw = r.sb("gw", [P, DH, E])
        gb = r.sb("gb", [P, E])
        lg, ex, pr = (r.sb(n, [P, T, E]) for n in ("lg", "ex", "pr"))
        mx, sm, rs, ws, wz, wr = (r.sb(n, [P, T]) for n in ("mx", "sm", "rs", "ws", "wz", "wr"))
        gate = [r.sb(f"gate{u}", [P, T, E]) for u in range(2)]
        gateT = [r.sb(f"gateT{u}", [E, T, P]) for u in range(2)]
        acc = [r.sb(f"acc{j}", [P, T, D]) for j in range(2)]
        st6, mv = r.sb("st6", [P, T, 6]), r.sb("mv", [P, T, 2])
        ve, rstd, mhalf = (r.sb(n, [P, T]) for n in ("ve", "rstd", "mhalf"))
        out = [r.sb(f"out{u}", [P, T, D]) for u in range(2)]
        ident = r.sb("ident", [P, P])
        ps_t = r.ps("ps_t", [P, DH, S])
        ps_l = r.ps("ps_l", [P, T, E])
        ps_g = r.ps("ps_g", [E, T, P])
        ps_e = [r.ps(f"ps_e{j}", [P, 2, D]) for j in range(2)]
        ps_b = r.ps("ps_b", [P, D])
        c_ld, ew_ld, const_up, v, past_dve = (r.sem(n) for n in ("c_ld", "ew_ld", "const_up", "v", "past_dve"))
        ld, st = ([r.sem(f"{n}{u}") for u in range(2)] for n in ("ld", "st"))
        t_up, xT_up, lg_up, ex_up, gate_up, gt_up, gT_up, e_up, e_free, b_up, acc_up, var_up, rstd_up, out_up, steps, wr_up = (r.sem(n) for n in
            ("t_up", "xT_up", "lg_up", "ex_up", "gate_up", "gt_up", "gT_up", "e_up", "e_free", "b_up", "acc_up", "var_up", "rstd_up", "out_up", "steps", "wr_up"))
        block = ctx.enter_context(nc.Block())
        PAIRS = E // 2

        def batches(eng, body):
            body(0, 0, 0, True)
            body(1, 1, 0, True)
            with eng.Fori(1, B // 2 - 1) as i:
                for u in range(2):
                    body(2 * i + u, u, i, True)
            body(B - 2, 0, B // 2 - 1, True)
            body(B - 1, 1, B // 2 - 1, False)

        @block.sync
        def _(sp):
            for u in range(2):
                sp.dma_start(x_in[u][:, :, :], tok(a["x5"][u])).then_inc(ld[u], 16)
            sp.dma_start(gw[:, :, :], a["L1_ffn_gate_w"].rearrange("(h p) e -> p h e", p=P)).then_inc(c_ld, 16)
            sp.dma_start(gb[:, :], row_bc(a["L1_ffn_gate_b"], P)).then_inc(c_ld, 16)
            sp.dma_start(eb[:, :], a["L1_ffn_expert_b"]).then_inc(c_ld, 16)
            for e in range(E):
                sp.dma_start(ew[:, :, e, :], a["L1_ffn_expert_w"][e].rearrange("(h p) n -> p h n", p=P)).then_inc(ew_ld, 16)

            def store(b, u):
                sp.wait_ge(out_up, b + 1)
                sp.dma_start(tok(a["out"][b]), out[u][:, :, :]).then_inc(st[u], 16)

            with sp.Fori(0, B // 2 - 1) as i:
                for u in range(2):
                    store(2 * i + u, u)
                    sp.dma_start(x_in[u][:, :, :], tok(a["x5"][2 * i + u + 2])).then_inc(ld[u], 16)
            for u in range(2):
                store(B - 2 + u, u)
            for u in range(2):
                sp.wait_ge(st[u], 16 * B // 2)

        @block.gpsimd
        def _(pool):
            pool.memset(mhalf[:, :], -0.5).then_inc(const_up, 1)
            pool.memset(ident[:, :], 0.0).then_inc(const_up, 1)
            pool.wait_ge(const_up, 2)
            pool.affine_select(out=ident[:, :], in_=ident[:, :], compare_op=ALU.not_equal, fill=1.0, base=0,
                               pattern=[[-1, P]], channel_multiplier=1).then_inc(const_up, 1)

            def body(b, u, i, more):
                pool.wait_ge(var_up, b + 1)
                pool.tensor_tensor(rstd[:, :], ve[:, :], mhalf[:, :], ALU.pow).then_inc(rstd_up, 1)
            batches(pool, body)

        @block.scalar
        def _(act):
            def prepare(b, u):
                act.wait_ge(t_up, b + 1)
                wait(act, e_up, T * PAIRS * (b - 1))
                act.activation(xT[u][:, :, :], ps_t[:, :, :], ACT.Copy).then_inc(xT_up, 1)
                act.wait_ge(v, NV * b + 3)
                act.activation(ex[:, :, :], lg[:, :, :], ACT.Exp).then_inc(ex_up, 1)
                act.wait_ge(gt_up, b + 1)
                wait(act, b_up, T * (b - 1))
                act.activation(gateT[u][:, :, :], ps_g[:, :, :], ACT.Copy).then_inc(gT_up, 1)
            prepare(0, 0)

            def body(b, u, i, more):
                if more:
                    prepare(b + 1, 1 - u)
            batches(act, body)

        @block.vector
        def _(dve):
            dve.wait_ge(c_ld, 16 * 3)
            dve.wait_ge(const_up, 3)

            def prepare(b, u):
                step = [0]

                def then(ins):
                    step[0] += 1
                    ins.then_inc(v, 1)
                    dve.wait_ge(v, NV * b + step[0])

                def bc(ap):
                    return col(ap).to_broadcast([P, T, E])

                dve.wait_ge(lg_up, b + 1)
                then(dve.tensor_tensor(lg[:, :, :], ps_l[:, :, :], row(gb[:, :]).to_broadcast([P, T, E]), ALU.add))
                then(dve.tensor_reduce(mx[:, :], lg[:, :, :], AX.X, ALU.max))
                then(dve.tensor_tensor(lg[:, :, :], lg[:, :, :], bc(mx[:, :]), ALU.subtract))
                dve.wait_ge(ex_up, b + 1)
                then(dve.tensor_reduce(sm[:, :], ex[:, :, :], AX.X, ALU.add))
                then(dve.reciprocal(rs[:, :], sm[:, :]))
                then(dve.tensor_tensor(pr[:, :, :], ex[:, :, :], bc(rs[:, :]), ALU.mult))
                then(dve.scalar_tensor_tensor(pr[:, :, :], pr[:, :, :], THRESHOLD, pr[:, :, :], ALU.is_ge, ALU.mult))
                then(dve.tensor_reduce(ws[:, :], pr[:, :, :], AX.X, ALU.add))
                then(dve.scalar_tensor_tensor(wz[:, :], ws[:, :], 0.0, ws[:, :], ALU.is_equal, ALU.add))
                assert step[0] == NV
                dve.reciprocal(wr[:, :], wz[:, :]).then_inc(wr_up, 1)
                dve.wait_ge(wr_up, b + 1)
                wait(dve, gt_up, b - 1)
                dve.tensor_tensor(gate[u][:, :, :], pr[:, :, :], bc(wr[:, :]), ALU.mult).then_inc(gate_up, 1)

            prepare(0, 0)

            def body(b, u, i, more):
                wait(dve, out_up, b)
                for t in range(T):
                    dve.wait_ge(b_up, T * b + t + 1)
                    if t == 0:
                        dve.wait_ge(gate_up, b + 1)
                    acc_n = (E + 1) * (T * b + t)
                    dve.tensor_tensor(acc[0][:, t, :], ps_b[:, :], x_in[u][:, t, :], ALU.add).then_inc(acc_up, 1)
                    for e in range(E):
                        if e % 2 == 0:
                            dve.wait_ge(e_up, PAIRS * (T * b + t) + e // 2 + 1)
                        dve.wait_ge(acc_up, acc_n + e + 1)
                        ins = dve.scalar_tensor_tensor(acc[(e + 1) % 2][:, t, :], ps_e[e // 2 % 2][:, e % 2, :],
                                                       gate[u][:, t, e:e + 1], acc[e % 2][:, t, :], ALU.mult, ALU.add)
                        ins.then_inc(acc_up, 1)
                if more:
                    prepare(b + 1, 1 - u)

                def then(ins):
                    then.n += 1
                    ins.then_inc(steps, 1)
                    dve.wait_ge(steps, 2 * b + then.n)
                then.n = 0
                dve.wait_ge(acc_up, (E + 1) * T * (b + 1))
                moments(dve, then, acc[0], st6, mv, ve, past_dve).then_inc(var_up, 1)
                dve.wait_ge(rstd_up, b + 1)
                wait(dve, st[u], 16 * i)
                normalized(dve, out[u], acc[0], mv, rstd).then_inc(out_up, 1)
            batches(dve, body)

        @block.tensor
        def _(pe):
            pe.wait_ge(const_up, 3)
            pe.wait_ge(c_ld, 48)

            def turn(b, u, i):
                pe.wait_ge(ld[u], 16 * i + 16)
                wait(pe, xT_up, b)
                for h in range(DH):
                    for t in range(T):
                        ins = pe.transpose(ps_t[:, h, t * P:(t + 1) * P], x_in[u][:, t, h * P:(h + 1) * P], ident[:, :])
                ins.then_inc(t_up, 1)
                pe.wait_ge(xT_up, b + 1)
                for t in range(T):
                    for h in range(DH):
                        ins = pe.matmul(ps_l[:, t, :], xT[u][:, h, t * P:(t + 1) * P], gw[:, h, :], start=(h == 0), stop=(h == DH - 1))
                ins.then_inc(lg_up, 1)

            def turn_gates(b, u):
                pe.wait_ge(gate_up, b + 1)
                wait(pe, gT_up, b)
                for t in range(T):
                    ins = pe.transpose(ps_g[:, t, :], gate[u][:, t, :], ident[:, :])
                ins.then_inc(gt_up, 1)

            turn(0, 0, 0)
            turn_gates(0, 0)
            pe.wait_ge(ew_ld, 16 * E)

            def body(b, u, i, more):
                pe.wait_ge(gT_up, b + 1)
                for t in range(T):
                    n = T * b + t
                    wait(pe, acc_up, (E + 1) * (n - 1) + 1)
                    pe.matmul(ps_b[:, :], gateT[u][:, t, :], eb[:, :], start=True, stop=True).then_inc(b_up, 1)
                    for e in range(0, E, 2):
                        wait(pe, acc_up, (E + 1) * n + e - 1 if e >= 4 else (E + 1) * (n - 1) + e + 7)
                        for h in range(DH):
                            ins = pe.matmul(ps_e[e // 2 % 2][:, :, :].rearrange("p e d -> p (e d)"), xT[u][:, h, t * P:(t + 1) * P],
                                            ew[:, h, e:e + 2, :].rearrange("p e d -> p (e d)"), start=(h == 0), stop=(h == DH - 1))
                        ins.then_inc(e_up, 1)
                    if more and t == 0:
                        turn(b + 1, 1 - u, i + u)
                if more:
                    turn_gates(b + 1, 1 - u)
            batches(pe, body)


def decoder(nc, a):
    def scratch(name, shape, dt=F32):
        a[name] = nc.dram_tensor(f"scratch_{name}", shape, dt, kind="Internal").ap()

    for name in ("x1", "x2", "x4", "x5", "v", "fallback"):
        scratch(name, (B, S, D))
    scratch("qk_parts", (B, 2, PARTS, D, S), BF16)
    scratch("buf", (E * CAP, D))
    scratch("results", (E * CAP, D))
    with ExitStack() as ctx:
        w_all = ctx.enter_context(nc.sbuf_tensor("w_all", [P, B, DH, 3 * D], F32))
        stage_mix(nc, a, w_all)
        stage_rec(nc, a, w_all)
    stage_proj(nc, a)
    stage_xattn0(nc, a)
    with ExitStack() as ctx:
        route_w = ctx.enter_context(nc.sbuf_tensor("route_w", [P, B, 3, T], F32))
        route_i = ctx.enter_context(nc.sbuf_tensor("route_i", [P, B, 2, T], U32))
        stage_route(nc, a, route_w, route_i)
        stage_experts(nc, a)
        stage_memory(nc, a, route_w, route_i)
    stage_xattn1(nc, a)
    stage_gated(nc, a)


def kernel(**inputs):
    import numpy as _np
    import concourse.bacc as _bacc
    from concourse import mybir as _mybir
    from concourse.bass_utils import run_bass_kernel_spmd as _run

    given = {name: _np.asarray(value) for name, value in inputs.items()}
    turned = ("L0_xattn_Wq", "L0_xattn_Wk", "L0_xattn_Wv", "L0_xattn_Wo", "L1_xattn_Wo")
    as_given = ("x", "L0_attn_norm_weight", "L0_attn_router_b",
                "L0_xattn_bq", "L0_xattn_bk", "L0_xattn_bv", "L0_xattn_bo",
                "L0_ffn_Wr", "L0_ffn_Wg", "L0_ffn_Wu", "L0_ffn_Wd", "L0_ffn_f_norm", "L0_ffn_fWg", "L0_ffn_fWu", "L0_ffn_fWd",
                "L1_attn_Wq", "L1_attn_Wk", "L1_attn_Wv", "L1_attn_Wo", "L1_attn_bo", "L1_attn_Wg", "L1_attn_bg", "L1_attn_decay_param",
                "L1_xattn_Wq", "L1_xattn_bq", "L1_xattn_Wk", "L1_xattn_bk", "L1_xattn_Wv", "L1_xattn_bv", "L1_xattn_bo",
                "L1_ffn_gate_w", "L1_ffn_gate_b", "L1_ffn_expert_w", "L1_ffn_expert_b")

    def mixed_rows(w):
        return w.reshape(8, -1, 4, 16, 256).transpose(1, 0, 3, 2, 4).reshape(-1, 128, 1024)

    laid = {name: given[name] for name in as_given}
    laid.update({f"{name}T": given[name].T for name in turned})
    laid["ctxT"] = given["ctx_1024"].transpose(0, 2, 1)
    laid["mask"] = given["mask_BxSxS2_bk1"]
    laid["L0_router_wT"] = given["L0_attn_router_w"].T
    laid["L0_mix_w"] = _np.concatenate([mixed_rows(given["L0_attn_w_hg"]), mixed_rows(given["L0_attn_w_out"])])
    laid["L0_ffn_norm_wP"] = given["L0_ffn_norm_w"].reshape(8, 2, 128).transpose(0, 2, 1)

    nc = _bacc.Bacc("TRN2", target_bir_lowering=False, num_devices=1)
    arrays, a = {}, {}
    for name, value in laid.items():
        value = _np.ascontiguousarray(value)
        arrays[f"in_{name}"] = value
        a[name] = nc.dram_tensor(f"in_{name}", value.shape, _mybir.dt.from_np(value.dtype), kind="ExternalInput").ap()
    a["out"] = nc.dram_tensor("out", (8, 512, 256), _mybir.dt.from_np(_np.dtype("float32")), kind="ExternalOutput").ap()
    decoder(nc, a)
    r = _run(nc, [arrays], core_ids=[0])
    return r.results[0]["out"]
```

```python
from contextlib import ExitStack

import concourse.bass as bass
from concourse import mybir

F32 = mybir.dt.float32
BF16 = mybir.dt.bfloat16
U8 = mybir.dt.uint8
U32 = mybir.dt.uint32
ALU = mybir.AluOpType
ACT = mybir.ActivationFunctionType
AX = mybir.AxisListType

P = 128
B = 8
S = 512
D = 256
T = S // P
DH = D // P
E = 8


class Room:

    def __init__(self, nc, ctx, stage):
        self.nc, self.ctx, self.stage, self.sems = nc, ctx, stage, []
        ctx.callback(self.clear)

    def clear(self):
        self.nc.clear_and_free_semaphores(self.sems)
        self.nc.all_engine_barrier()

    def sb(self, name, shape, dt=F32):
        return self.ctx.enter_context(self.nc.sbuf_tensor(f"{self.stage}_{name}", shape, dt))

    def ps(self, name, shape, dt=F32):
        return self.ctx.enter_context(self.nc.psum_tensor(f"{self.stage}_{name}", shape, dt))

    def sem(self, name):
        self.sems.append(self.nc.alloc_semaphore(f"{self.stage}_{name}"))
        return self.sems[-1]


def tok(ap):
    return ap.rearrange("(t p) n -> p t n", p=P)


def apart(eng, past):
    eng.sem_inc(past, 1)


def wait(eng, sem, count):
    if not isinstance(count, int) or count > 0:
        eng.wait_ge(sem, count)


def stage_mix(nc, a, x_all, inv_all, w_all):
    KC = P // E
    C = 4
    G = 3 * D // (KC * C)
    with ExitStack() as ctx:
        r = Room(nc, ctx, "mix")
        junk = r.sb("junk", [P, B, T, D], BF16)
        ssq, msq = r.sb("ssq", [P, B, T]), r.sb("msq", [P, B, T])
        mhalf = r.sb("mhalf", [P, T])
        meanT = r.sb("meanT", [P, B, DH])
        nw = r.sb("nw", [P, DH])
        rwT = r.sb("rwT", [P, DH, E])
        rb = r.sb("rb", [B, E])
        lg, ex, pr = (r.sb(n, [B, E]) for n in ("lg", "ex", "pr"))
        nmax, esum, erec = (r.sb(n, [B, 1]) for n in ("nmax", "esum", "erec"))
        prT = r.sb("prT", [E, B])
        prP = r.sb("prP", [P, B, 1])
        ident = r.sb("ident", [P, P])
        sel = r.sb("sel", [E, E, KC])
        mask = r.sb("mask", [P, KC])
        blocks = r.sb("blocks", [P, B, KC])
        chunk = [r.sb(f"chunk{u}", [P, C, D]) for u in range(2)]
        ps_mean = r.ps("ps_mean", [P, B, DH])
        ps_small = r.ps("ps_small", [P, 3, 8])
        ps_w = [[r.ps(f"ps_w{u}{h}", [P, C, B, KC]) for h in range(DH)] for u in range(2)]
        c_ld = r.sem("c_ld")
        x_ld, w_ld = [r.sem(f"x_ld{j}") for j in range(B // 2)], [r.sem(f"w_ld{u}") for u in range(2)]
        ssq_up, msq_up, inv_up, mean_up = (r.sem(n) for n in ("ssq_up", "msq_up", "inv_up", "mean_up"))
        const_up, soft_v, soft_s, soft_t = (r.sem(n) for n in ("const_up", "soft_v", "soft_s", "soft_t"))
        mixed, out_v, out_s = r.sem("mixed"), r.sem("out_v"), r.sem("out_s")
        zeros = r.sb("zeros", [P, 2048])
        zero_up, zero_st = r.sem("zero_up"), r.sem("zero_st")
        block = ctx.enter_context(nc.Block())

        @block.sync
        def _(sp):
            for j in range(B // 2):
                sp.dma_start(x_all[:, j, :, :], tok(a["x"][j])).then_inc(x_ld[j], 16)
            for j in range(B // 2):
                sp.wait_ge(x_ld[j], 16)
                sp.dma_start(x_all[:, B // 2 + j, :, :], tok(a["x"][B // 2 + j])).then_inc(x_ld[j], 16)
            with nc.allow_non_contiguous_dma(reason="256 weights"):
                sp.dma_start(nw[:, :], a["L0_attn_norm_weight"].rearrange("(h p) -> p h", p=P)).then_inc(c_ld, 16)
            sp.dma_start(rwT[:, :, :], a["L0_router_wT"].rearrange("(h p) e -> p h e", p=P)).then_inc(c_ld, 16)
            sp.dma_start(rb[:, :], a["L0_attn_router_b"].rearrange("(o e) -> o e", o=1).to_broadcast([B, E])).then_inc(c_ld, 16)
            with sp.Fori(0, G // 2) as i:
                for u in range(2):
                    g = 2 * i + u
                    sp.wait_ge(mixed, g + 1)
                    sp.dma_start(chunk[u][:, :, :], a["L0_mix_w"][g].rearrange("p (c d) -> p c d", c=C)).then_inc(w_ld[u], 16)

        @block.scalar
        def _(act):
            for b in range(B):
                act.wait_ge(x_ld[b % (B // 2)], 16 * (b // (B // 2) + 1))
                for t in range(T):
                    ins = act.activation(junk[:, b, t, :], x_all[:, b, t, :], ACT.Square, accum_out=ssq[:, b, t:t + 1])
                ins.then_inc(ssq_up, 1)
            act.wait_ge(zero_up, 1)
            buf = a["buf"].rearrange("(n p r) d -> n p (r d)", p=P, r=2048 // D)
            for n in range(buf.shape[0]):
                act.dma_start(buf[n], zeros[:, :]).then_inc(zero_st, 16)
            act.wait_ge(soft_v, 4)
            act.activation(ex[:, :], lg[:, :], ACT.Exp, bias=nmax[:, :], accum_out=esum[:, :]).then_inc(soft_s, 1)
            act.sem_inc(out_s, 2)
            with act.Fori(0, G // 2) as i:
                for u in range(2):
                    g = 2 * i + u
                    act.wait_ge(mixed, g + 3)
                    act.activation(w_all[:, :, 1, bass.ds(g * (C * KC), C * KC)].rearrange("p b (c k) -> p b c k", c=C),
                                   ps_w[u][1][:, :, :, :].rearrange("p c b k -> p b c k"), ACT.Copy).then_inc(out_s, 1)
            act.wait_ge(zero_st, 16 * buf.shape[0])

        @block.gpsimd
        def _(pool):
            pool.memset(mhalf[:, :], -0.5).then_inc(const_up, 1)
            pool.memset(ident[:, :], 0.0).then_inc(const_up, 1)
            pool.memset(sel[:, :, :], 1.0).then_inc(const_up, 1)
            pool.wait_ge(const_up, 3)
            pool.affine_select(out=ident[:, :], in_=ident[:, :], compare_op=ALU.not_equal, fill=1.0, base=0,
                               pattern=[[-1, P]], channel_multiplier=1).then_inc(const_up, 1)
            pool.affine_select(out=sel[:, :, :], in_=sel[:, :, :], compare_op=ALU.is_equal, fill=0.0, base=0,
                               pattern=[[-1, E], [0, KC]], channel_multiplier=1).then_inc(const_up, 1)
            pool.memset(zeros[:, :], 0.0).then_inc(zero_up, 1)
            for b in range(B):
                pool.wait_ge(msq_up, b + 1)
                pool.tensor_tensor(inv_all[:, b, :], msq[:, b, :], mhalf[:, :], ALU.pow).then_inc(inv_up, 1)

        @block.vector
        def _(dve):
            dve.wait_ge(const_up, 5)
            dve.tensor_reduce(mask[:, :], ident[:, :].rearrange("p (e k) -> p k e", e=E), AX.X, ALU.add).then_inc(soft_v, 1)
            for b in range(B):
                dve.wait_ge(ssq_up, b + 1)
                dve.tensor_scalar(msq[:, b, :], ssq[:, b, :], 1.0 / D, 1e-6, ALU.mult, ALU.add).then_inc(msq_up, 1)
            dve.wait_ge(mean_up, B)
            dve.wait_ge(c_ld, 48)
            for h in range(DH):
                ins = dve.tensor_scalar(meanT[:, :, h], ps_mean[:, :, h], nw[:, h:h + 1], 1.0 / S, ALU.mult, ALU.mult)
            ins.then_inc(soft_v, 1)
            dve.wait_ge(soft_t, 1)
            dve.tensor_tensor(lg[:, :], ps_small[0:B, 0, 0:E], rb[:, :], ALU.add).then_inc(soft_v, 1)
            dve.wait_ge(soft_v, 3)
            dve.tensor_reduce(nmax[:, :], lg[:, :], AX.X, ALU.max, negate=True).then_inc(soft_v, 1)
            dve.wait_ge(soft_s, 1)
            dve.reciprocal(erec[:, :], esum[:, :]).then_inc(soft_v, 1)
            dve.wait_ge(soft_v, 5)
            dve.tensor_scalar(pr[:, :], ex[:, :], erec[:, :], None, ALU.mult).then_inc(soft_v, 1)
            dve.wait_ge(soft_t, 2)
            dve.tensor_copy(prT[:, :], ps_small[0:E, 1, 0:B]).then_inc(soft_v, 1)
            dve.wait_ge(soft_t, 3)
            dve.tensor_copy(prP[:, :, 0], ps_small[:, 2, 0:B]).then_inc(soft_v, 1)
            dve.wait_ge(soft_v, 8)
            dve.tensor_tensor(blocks[:, :, :], prP[:, :, :].to_broadcast([P, B, KC]),
                              mask[:, :].rearrange("p (o k) -> p o k", o=1).to_broadcast([P, B, KC]), ALU.mult).then_inc(soft_v, 1)
            dve.sem_inc(out_v, 2)
            with dve.Fori(0, G // 2) as i:
                for u in range(2):
                    g = 2 * i + u
                    dve.wait_ge(mixed, g + 3)
                    dve.tensor_copy(w_all[:, :, 0, bass.ds(g * (C * KC), C * KC)].rearrange("p b (c k) -> p b c k", c=C),
                                    ps_w[u][0][:, :, :, :].rearrange("p c b k -> p b c k")).then_inc(out_v, 1)

        @block.tensor
        def _(pe):
            for b in range(B):
                pe.wait_ge(inv_up, b + 1)
                for h in range(DH):
                    for t in range(T):
                        ins = pe.matmul(ps_mean[:, b, h:h + 1], x_all[:, b, t, h * P:(h + 1) * P], inv_all[:, b, t:t + 1],
                                        start=(t == 0), stop=(t == T - 1))
                ins.then_inc(mean_up, 1)
            pe.wait_ge(soft_v, 2)
            for h in range(DH):
                ins = pe.matmul(ps_small[0:B, 0, 0:E], meanT[:, :, h], rwT[:, h, :], start=(h == 0), stop=(h == DH - 1))
            ins.then_inc(soft_t, 1)
            pe.wait_ge(soft_v, 6)
            pe.transpose(ps_small[0:E, 1, 0:B], pr[:, :], ident[0:B, 0:B]).then_inc(soft_t, 1)
            pe.wait_ge(soft_v, 7)
            pe.matmul(ps_small[:, 2, 0:B], sel[:, :, :].rearrange("p e k -> p (e k)"), prT[:, :], start=True, stop=True).then_inc(soft_t, 1)
            pe.wait_ge(soft_v, 9)
            pe.sem_inc(mixed, 2)
            with pe.Fori(0, G // 2) as i:
                for u in range(2):
                    g = 2 * i + u
                    pe.wait_ge(w_ld[u], i * 16 + 16)
                    pe.wait_ge(out_v, g + 1)
                    pe.wait_ge(out_s, g + 1)
                    for h in range(DH):
                        for c in range(C):
                            ins = pe.matmul(ps_w[u][h][:, c, :, :].rearrange("p b k -> p (b k)"), chunk[u][:, c, h * P:(h + 1) * P],
                                            blocks[:, :, :].rearrange("p b k -> p (b k)"), start=True, stop=True)
                    ins.then_inc(mixed, 1)


def stage_rec(nc, a, x_all, inv_all, w_all):
    with ExitStack() as ctx:
        r = Room(nc, ctx, "rec")
        whg = [r.sb(f"whg{u}", [P, DH, 2 * D]) for u in range(2)]
        wout = [r.sb(f"wout{u}", [P, DH, D]) for u in range(2)]
        xn = [r.sb(f"xn{u}", [P, T, D]) for u in range(2)]
        xnT = [r.sb(f"xnT{u}", [P, DH, S]) for u in range(2)]
        nw = r.sb("nw", [P, DH])
        keep = [r.sb(f"keep{u}", [P, DH, S]) for u in range(2)]
        take = [r.sb(f"take{u}", [P, DH, S]) for u in range(2)]
        val = [r.sb(f"val{u}", [P, DH, S]) for u in range(2)]
        h = [r.sb(f"h{u}", [P, DH, S]) for u in range(2)]
        z = r.sb("z", [P, T, D])
        st6, mv = r.sb("st6", [P, T, 6]), r.sb("mv", [P, T, 2])
        ve, rstd, mhalf = (r.sb(n, [P, T]) for n in ("ve", "rstd", "mhalf"))
        x1 = [r.sb(f"x1{u}", [P, T, D]) for u in range(2)]
        ident = r.sb("ident", [P, P])
        ps_t, ps_h, ps_g = (r.ps(n, [P, DH, S]) for n in ("ps_t", "ps_h", "ps_g"))
        ps_o = r.ps("ps_o", [P, T, D])
        c_ld, const_up, past_dve = (r.sem(n) for n in ("c_ld", "const_up", "past_dve"))
        hg_ld, wo_ld, st = ([r.sem(f"{n}{u}") for u in range(2)] for n in ("hg_ld", "wo_ld", "st"))
        xn_up, t_up, xnT_up, hg_up, sig_up, g_up, val_up, h_up, o_up, z_up, steps, var_up, rstd_up, x1_up = (r.sem(n) for n in
            ("xn_up", "t_up", "xnT_up", "hg_up", "sig_up", "g_up", "val_up", "h_up", "o_up", "z_up", "steps", "var_up", "rstd_up", "x1_up"))
        block = ctx.enter_context(nc.Block())

        def rounds(eng, body):
            body(0, 0, 0)
            body(1, 1, 0)
            with eng.Fori(1, B // 2 - 1) as i:
                for u in range(2):
                    body(2 * i + u, u, i)
            body(B - 2, 0, B // 2 - 1)
            body(B - 1, 1, B // 2 - 1)
            body(B, 0, B // 2)

        def inside(b, first, last):
            return not isinstance(b, int) or first <= b <= last

        @block.sync
        def _(sp):
            with nc.allow_non_contiguous_dma(reason="256 weights"):
                sp.dma_start(nw[:, :], a["L0_attn_norm_weight"].rearrange("(h p) -> p h", p=P)).then_inc(c_ld, 16)

            def load_hg(b, u):
                sp.dma_start(whg[u][:, :, :], w_all[:, bass.ds(b, 1), :, 0:2 * D].rearrange("p o h n -> p (o h) n")).then_inc(hg_ld[u], 16)

            def load_out(b, u):
                sp.dma_start(wout[u][:, :, :], w_all[:, bass.ds(b, 1), :, 2 * D:3 * D].rearrange("p o h n -> p (o h) n")).then_inc(wo_ld[u], 16)

            for u in range(2):
                load_hg(u, u)
                load_out(u, u)

            def body(b, u, i):
                if inside(b, 0, B - 3):
                    sp.wait_ge(hg_up, b + 1)
                    load_hg(b + 2, u)
                if inside(b, 1, B - 2):
                    sp.wait_ge(o_up, b)
                    load_out(b + 1, 1 - u)
                if inside(b, 1, B):
                    sp.wait_ge(x1_up, b)
                    sp.dma_start(tok(a["x1"][b - 1]), x1[1 - u][:, :, :]).then_inc(st[1 - u], 16)
            rounds(sp, body)
            for u in range(2):
                sp.wait_ge(st[u], 16 * B // 2)

        @block.gpsimd
        def _(pool):
            pool.memset(mhalf[:, :], -0.5).then_inc(const_up, 1)
            pool.memset(ident[:, :], 0.0).then_inc(const_up, 1)
            pool.wait_ge(const_up, 2)
            pool.affine_select(out=ident[:, :], in_=ident[:, :], compare_op=ALU.not_equal, fill=1.0, base=0,
                               pattern=[[-1, P]], channel_multiplier=1).then_inc(const_up, 1)
            with pool.Fori(0, B) as b:
                pool.wait_ge(var_up, b + 1)
                pool.tensor_tensor(rstd[:, :], ve[:, :], mhalf[:, :], ALU.pow).then_inc(rstd_up, 1)

        @block.scalar
        def _(act):
            act.wait_ge(c_ld, 16)

            def turned(b, u):
                act.wait_ge(t_up, b + 1)
                wait(act, hg_up, b - 1)
                for k in range(DH):
                    ins = act.activation(xnT[u][:, k, :], ps_t[:, k, :], ACT.Copy, scale=nw[:, k:k + 1])
                ins.then_inc(xnT_up, 1)
            turned(0, 0)

            def body(b, u, i):
                if inside(b, 0, B - 1):
                    act.wait_ge(hg_up, b + 1)
                    wait(act, h_up, b - 1)
                    act.activation(val[u][:, :, :], ps_h[:, :, :], ACT.Sigmoid).then_inc(sig_up, 1)
                    act.activation(take[u][:, :, :], ps_g[:, :, :], ACT.Sigmoid).then_inc(sig_up, 1)
                    act.activation(keep[u][:, :, :], ps_g[:, :, :], ACT.Sigmoid, scale=-1.0).then_inc(sig_up, 1)
                if inside(b, 0, B - 2):
                    turned(b + 1, 1 - u)
            rounds(act, body)

        @block.vector
        def _(dve):
            def normalize(b, u):
                wait(dve, t_up, b - 1)
                for t in range(T):
                    ins = dve.tensor_scalar(xn[u][:, t, :], x_all[:, bass.ds(b, 1), t, :].rearrange("p o d -> p (o d)"),
                                            inv_all[:, bass.ds(b, 1), t], None, ALU.mult)
                ins.then_inc(xn_up, 1)
            normalize(0, 0)
            normalize(1, 1)

            def body(b, u, i):
                if inside(b, 0, B - 1):
                    dve.wait_ge(sig_up, 3 * b + 1)
                    dve.scalar_tensor_tensor(val[u][:, :, :], ps_h[:, :, :], 0.5, val[u][:, :, :], ALU.add, ALU.max).then_inc(g_up, 1)
                if inside(b, 1, B):
                    dve.wait_ge(o_up, b)
                    wait(dve, x1_up, b - 1)
                    for t in range(T):
                        ins = dve.scalar_tensor_tensor(z[:, t, :], x_all[:, bass.ds(b - 1, 1), t, :].rearrange("p o d -> p (o d)"), 2.0,
                                                       ps_o[:, t, :], ALU.mult, ALU.add)
                    ins.then_inc(z_up, 1)
                if inside(b, 0, B - 1):
                    dve.wait_ge(g_up, b + 1)
                    dve.wait_ge(sig_up, 3 * b + 2)
                    dve.tensor_tensor(val[u][:, :, :], val[u][:, :, :], take[u][:, :, :], ALU.mult).then_inc(val_up, 1)
                if inside(b, 1, B):
                    dve.wait_ge(z_up, b)
                    for t in range(T):
                        ins = dve.bn_stats(st6[:, t, :], z[:, t, :])
                    ins.then_inc(steps, 1)
                if inside(b, 0, B - 1):
                    dve.wait_ge(val_up, b + 1)
                    dve.wait_ge(sig_up, 3 * b + 3)
                    wait(dve, o_up, b - 1)
                    for k in range(DH):
                        ins = dve.tensor_tensor_scan(h[u][:, k, :], keep[u][:, k, :], val[u][:, k, :], 0.0, ALU.mult, ALU.add)
                    ins.then_inc(h_up, 1)
                if inside(b, 1, B):
                    dve.wait_ge(steps, 2 * b - 1)
                    apart(dve, past_dve)
                    for t in range(T):
                        ins = dve.bn_aggr(mv[:, t, :], st6[:, t, :])
                    ins.then_inc(steps, 1)
                    dve.wait_ge(steps, 2 * b)
                    dve.tensor_scalar(ve[:, :], mv[:, :, 1], 1e-5, None, ALU.add).then_inc(var_up, 1)
                if inside(b, 0, B - 3):
                    normalize(b + 2, u)
                if inside(b, 1, B):
                    dve.wait_ge(rstd_up, b)
                    wait(dve, st[1 - u], 16 * (i - 1 + u) if inside(b, 3, B) else 0)
                    for t in range(T):
                        ins = dve.tensor_scalar(x1[1 - u][:, t, :], z[:, t, :], mv[:, t, 0:1], rstd[:, t:t + 1], ALU.subtract, ALU.mult)
                    ins.then_inc(x1_up, 1)
            rounds(dve, body)

        @block.tensor
        def _(pe):
            pe.wait_ge(const_up, 3)

            def turn(b, u):
                pe.wait_ge(xn_up, b + 1)
                wait(pe, xnT_up, b)
                for k in range(DH):
                    for t in range(T):
                        ins = pe.transpose(ps_t[:, k, t * P:(t + 1) * P], xn[u][:, t, k * P:(k + 1) * P], ident[:, :])
                ins.then_inc(t_up, 1)
            turn(0, 0)

            def body(b, u, i):
                if inside(b, 0, B - 1):
                    pe.wait_ge(hg_ld[u], 16 * i + 16)
                    pe.wait_ge(xnT_up, b + 1)
                    wait(pe, g_up, b)
                    wait(pe, sig_up, 3 * b)
                    for out, first in ((ps_h, 0), (ps_g, DH)):
                        for n in range(DH):
                            for k in range(DH):
                                ins = pe.matmul(out[:, n, :], whg[u][:, k, (first + n) * P:(first + n + 1) * P], xnT[u][:, k, :],
                                                start=(k == 0), stop=(k == DH - 1))
                    ins.then_inc(hg_up, 1)
                if inside(b, 0, B - 2):
                    turn(b + 1, 1 - u)
                if inside(b, 1, B):
                    pe.wait_ge(wo_ld[1 - u], 16 * (i + u))
                    pe.wait_ge(h_up, b)
                    wait(pe, z_up, b - 1)
                    for t in range(T):
                        for k in range(DH):
                            ins = pe.matmul(ps_o[:, t, :], h[1 - u][:, k, t * P:(t + 1) * P], wout[1 - u][:, k, :],
                                            start=(k == 0), stop=(k == DH - 1))
                    ins.then_inc(o_up, 1)
            rounds(pe, body)


H0 = 16
DK = D // H0
QH = 4
PARTS = 3


def row_bc(vec, n):
    return vec.rearrange("(o e) -> o e", o=1).to_broadcast([n, vec.shape[0]])


def stage_proj(nc, a):
    SC = DK ** -0.5
    with ExitStack() as ctx:
        r = Room(nc, ctx, "proj")
        x_in = [r.sb(f"x{u}", [P, T, D]) for u in range(2)]
        cT = [r.sb(f"cT{u}", [P, DH, S]) for u in range(2)]
        xT = [r.sb(f"xT{u}", [P, DH, S]) for u in range(2)]
        wq, wk, wv = (r.sb(n, [P, DH, D]) for n in ("wq", "wk", "wv"))
        bq, bqs, bk = (r.sb(n, [P, DH]) for n in ("bq", "bqs", "bk"))
        bv = r.sb("bv", [P, D])
        full = [[r.sb(f"full{n}{u}", [P, DH, S]) for u in range(2)] for n in "qk"]
        rest = [[r.sb(f"rest{n}{u}", [P, DH, S]) for u in range(2)] for n in "qk"]
        parts = [[r.sb(f"parts{n}{u}", [P, PARTS, DH, S], BF16) for u in range(2)] for n in "qk"]
        v = [r.sb(f"v{u}", [P, T, D]) for u in range(2)]
        ident = r.sb("ident", [P, P])
        ps_t, ps_q, ps_k = (r.ps(n, [P, DH, S]) for n in ("ps_t", "ps_q", "ps_k"))
        ps_v = r.ps("ps_v", [P, T, D])
        ps_qk = [ps_q, ps_k]
        c_ld, const_up, bqs_up = (r.sem(n) for n in ("c_ld", "const_up", "bqs_up"))
        ld, st = [r.sem(f"ld{u}") for u in range(2)], [r.sem(f"st{u}") for u in range(2)]
        t_up, xT_up, mm_up, high_up, rest_up, mid_up, low_up, v_up = (r.sem(n) for n in
            ("t_up", "xT_up", "mm_up", "high_up", "rest_up", "mid_up", "low_up", "v_up"))
        block = ctx.enter_context(nc.Block())

        @block.sync
        def _(sp):
            for w, n in ((wq, "L0_xattn_WqT"), (wk, "L0_xattn_WkT"), (wv, "L0_xattn_WvT")):
                sp.dma_start(w[:, :, :], a[n].rearrange("(h p) n -> p h n", p=P)).then_inc(c_ld, 16)
            with nc.allow_non_contiguous_dma(reason="256 biases"):
                for w, n in ((bq, "L0_xattn_bq"), (bk, "L0_xattn_bk")):
                    sp.dma_start(w[:, :], a[n].rearrange("(h p) -> p h", p=P)).then_inc(c_ld, 16)
            sp.dma_start(bv[:, :], row_bc(a["L0_xattn_bv"], P)).then_inc(c_ld, 16)

            def load(b, u):
                sp.dma_start(x_in[u][:, :, :], tok(a["x1"][b])).then_inc(ld[u], 16)
                sp.dma_start(cT[u][:, :, :], a["ctxT"][b].rearrange("(h p) s -> p h s", p=P)).then_inc(ld[u], 16)

            def store(b, u):
                sp.wait_ge(low_up, 2 * b + 2)
                for n in range(2):
                    sp.dma_start(a["qk_parts"][b, n].rearrange("c (h p) s -> p (c h) s", p=P),
                                 parts[n][u][:, :, :, :].rearrange("p c h s -> p (c h) s")).then_inc(st[u], 16)
                sp.wait_ge(v_up, b + 1)
                sp.dma_start(tok(a["v"][b]), v[u][:, :, :]).then_inc(st[u], 16)

            for u in range(2):
                load(u, u)
            with sp.Fori(0, B // 2 - 1) as i:
                for u in range(2):
                    sp.wait_ge(mm_up, 3 * (2 * i + u) + 3)
                    load(2 * i + u + 2, u)
                    store(2 * i + u, u)
            for u in range(2):
                store(B - 2 + u, u)
            for u in range(2):
                sp.wait_ge(st[u], 48 * B // 2)

        @block.gpsimd
        def _(pool):
            pool.memset(ident[:, :], 0.0).then_inc(const_up, 1)
            pool.wait_ge(const_up, 1)
            pool.affine_select(out=ident[:, :], in_=ident[:, :], compare_op=ALU.not_equal, fill=1.0, base=0,
                               pattern=[[-1, P]], channel_multiplier=1).then_inc(const_up, 1)

        def pairs(eng, body):
            for u in range(2):
                body(u, u, 0)
            with eng.Fori(1, B // 2) as i:
                for u in range(2):
                    body(2 * i + u, u, i)

        @block.scalar
        def _(act):
            act.wait_ge(c_ld, 96)
            act.mul(bqs[:, :], bq[:, :], SC).then_inc(bqs_up, 1)
            act.wait_ge(bqs_up, 1)

            def body(b, u, i):
                act.wait_ge(t_up, b + 1)
                act.activation(xT[u][:, :, :], ps_t[:, :, :], ACT.Copy).then_inc(xT_up, 1)
                for n in range(2):
                    act.wait_ge(mm_up, 3 * b + n + 1)
                    wait(act, low_up, 2 * b + n - 3)
                    wait(act, st[u], 48 * i)
                    for h in range(DH):
                        kw = dict(scale=SC, bias=bqs[:, h:h + 1]) if n == 0 else dict(bias=bk[:, h:h + 1])
                        act.activation(full[n][u][:, h, :], ps_qk[n][:, h, :], ACT.Identity, **kw)
                        ins = act.activation(parts[n][u][:, 0, h, :], ps_qk[n][:, h, :], ACT.Identity, **kw)
                    ins.then_inc(high_up, 1)
                for n in range(2):
                    act.wait_ge(rest_up, 2 * b + n + 1)
                    act.activation(parts[n][u][:, 1, :, :], rest[n][u][:, :, :], ACT.Copy).then_inc(mid_up, 1)
            pairs(act, body)

        @block.vector
        def _(dve):
            dve.wait_ge(c_ld, 96)

            def body(b, u, i):
                for n in range(2):
                    dve.wait_ge(high_up, 2 * b + n + 1)
                    dve.tensor_tensor(rest[n][u][:, :, :], full[n][u][:, :, :], parts[n][u][:, 0, :, :], ALU.subtract).then_inc(rest_up, 1)
                for n in range(2):
                    dve.wait_ge(mid_up, 2 * b + n + 1)
                    dve.tensor_tensor(parts[n][u][:, 2, :, :], rest[n][u][:, :, :], parts[n][u][:, 1, :, :], ALU.subtract).then_inc(low_up, 1)
                dve.wait_ge(mm_up, 3 * b + 3)
                wait(dve, st[u], 48 * i)
                dve.tensor_tensor(v[u][:, :, :], ps_v[:, :, :], bv[:, :].rearrange("p (o d) -> p o d", o=1).to_broadcast([P, T, D]),
                                  ALU.add).then_inc(v_up, 1)
            pairs(dve, body)

        @block.tensor
        def _(pe):
            pe.wait_ge(const_up, 2)
            pe.wait_ge(c_ld, 96)

            def body(b, u, i):
                pe.wait_ge(ld[u], 32 * i + 32)
                wait(pe, xT_up, b)
                for h in range(DH):
                    for t in range(T):
                        ins = pe.transpose(ps_t[:, h, t * P:(t + 1) * P], x_in[u][:, t, h * P:(h + 1) * P], ident[:, :])
                ins.then_inc(t_up, 1)
                pe.wait_ge(xT_up, b + 1)
                for n, (w, src) in enumerate(((wq, xT[u]), (wk, cT[u]))):
                    wait(pe, high_up, 2 * b + n - 1)
                    for m in range(DH):
                        for h in range(DH):
                            ins = pe.matmul(ps_qk[n][:, m, :], w[:, h, m * P:(m + 1) * P], src[:, h, :], start=(h == 0), stop=(h == DH - 1))
                    ins.then_inc(mm_up, 1)
                wait(pe, v_up, b)
                for t in range(T):
                    for h in range(DH):
                        ins = pe.matmul(ps_v[:, t, :], cT[u][:, h, t * P:(t + 1) * P], wv[:, h, :], start=(h == 0), stop=(h == DH - 1))
                ins.then_inc(mm_up, 1)
            pairs(pe, body)


def stage_xattn0(nc, a):
    HU = H0 // 2
    NK = 6 * DK
    QP, KP = (0, 0, 1, 1, 0, 2), (0, 1, 0, 1, 2, 0)
    CH = 4
    NP = 4
    DROP = S - int(S * 0.9)
    ROUNDS = -(-DROP // 8)
    PICK = 2 * ROUNDS + 1
    GONE = -3.0e38
    with ExitStack() as ctx:
        r = Room(nc, ctx, "xa")
        probT = [r.sb(f"probT{u}", [P, HU, T, S]) for u in range(2)]
        probs = [r.sb(f"probs{u}", [P, T, S]) for u in range(NP)]
        q = [r.sb(f"q{u}", [NK, CH, S], BF16) for u in range(2)]
        k = [r.sb(f"k{u}", [NK, CH, S], BF16) for u in range(2)]
        v = [r.sb(f"v{u}", [P, T, HU * DK]) for u in range(2)]
        vm = r.sb("vm", [P, T, 2, QH, 2 * DK])
        oT = r.sb("oT", [P, 2, S])
        wo = r.sb("wo", [P, 2, D])
        bo = r.sb("bo", [P, D])
        x_in = r.sb("x_in", [P, T, D])
        ident = r.sb("ident", [P, P])
        colsum = [r.sb(f"colsum{u}", [P, T, HU]) for u in range(2)]
        left = r.sb("left", [HU, S])
        m8 = r.sb("m8", [HU, 8])
        kept = r.sb("kept", [HU, S])
        nmax, rsum, rinv = ([r.sb(f"{n}{u}", [P, T]) for u in range(2)] for n in ("nmax", "rsum", "rinv"))
        st6, mv = r.sb("st6", [P, T, 6]), r.sb("mv", [P, T, 2])
        ve, rstd, mhalf = (r.sb(n, [P, T]) for n in ("ve", "rstd", "mhalf"))
        ps_s = [r.ps(f"ps_s{j}", [P, 2, S]) for j in range(2)]
        ps_t = [r.ps(f"ps_t{j}", [P, S]) for j in range(2)]
        ps_v = r.ps("ps_v", [P, S])
        ps_m = r.ps("ps_m", [P, S])
        c_ld, const_up, pad_up = r.sem("c_ld"), r.sem("const_up"), r.sem("pad_up")
        past_dve, past_pool, past_pe = (r.sem(n) for n in ("past_dve", "past_pool", "past_pe"))
        qk_ld, v_ld = [r.sem(f"qk_ld{u}") for u in range(2)], [r.sem(f"v_ld{u}") for u in range(2)]
        x_ld, x2_st = r.sem("x_ld"), r.sem("x2_st")
        s_up, max_up, exp_up, rinv_up, norm_up, t_up = (r.sem(n) for n in
            ("s_up", "max_up", "exp_up", "rinv_up", "norm_up", "t_up"))
        copied = [r.sem(f"copied{t}") for t in range(T)]
        sums_up, left_up, kept_up, vm_up, first_up, vals_up, oT_up, y_up, add_up = (r.sem(n) for n in
            ("sums_up", "left_up", "kept_up", "vm_up", "first_up", "vals_up", "oT_up", "y_up", "add_up"))
        pick, found, xb_up, ln, rstd_up = (r.sem(n) for n in ("pick", "found", "xb_up", "ln", "rstd_up"))
        block = ctx.enter_context(nc.Block())


        def since(b, first):
            return not isinstance(b, int) or b >= first

        def batches(eng, body):
            body(0)
            body(1)
            with eng.Fori(2, B) as b:
                body(b)
            body(B)

        def slots(b):
            for u in range(2):
                for h in range(HU):
                    yield u, h, HU * u + h, 2 * HU * b + HU * u + h, not isinstance(b, int) or b < B

        def has_before(b, u):
            return not isinstance(b, int) or 1 <= 2 * b + u <= 2 * B

        def has_before2(b, u):
            return not isinstance(b, int) or 2 <= 2 * b + u <= 2 * B + 1

        def by_vector(h, t):
            return t == 2 or (t == 3 and h == 1)

        def turning(b, u, h, n, real):
            return not (isinstance(b, int) and n < 2) and (real or (u == 0 and h < 2))

        def turned(eng, b, u, h, n, real, t):
            if not turning(b, u, h, n, real):
                return
            bb, g, hp = (b, u, h - 2) if h >= 2 else (b + u - 1, 1 - u, HU - 2 + h)
            if hp % QH == 0 and t in (0, 2):
                wait(eng, first_up if hp < QH else vals_up, 2 * bb + g - 1)
            eng.wait_ge(t_up, 4 * (n - 2) + t + 1)
            dst, src, out = probT[g][:, hp, t, :], ps_t[t % 2][:, :], colsum[g][:, t, hp:hp + 1]
            if by_vector(h, t):
                eng.tensor_scalar(dst, src, 1.0, 0.0, ALU.mult, ALU.add, accum_out=out).then_inc(copied[t], 1)
            else:
                eng.activation(dst, src, ACT.Copy, accum_out=out).then_inc(copied[t], 1)

        @block.sync
        def _(sp):
            def chunk(b, c):
                wait(sp, s_up, 32 * b + 8 * c - 8)
                for n, dst in ((0, q[c % 2]), (1, k[c % 2])):
                    for g in range(6):
                        src = a["qk_parts"][b, n, (QP, KP)[n][g], CH * DK * c:CH * DK * (c + 1), :]
                        sp.dma_start(dst[g * DK:(g + 1) * DK, :, :], src.rearrange("(h d) s -> d h s", d=DK)).then_inc(qk_ld[c % 2], 16)

            def value(b, u):
                wait(sp, vm_up, 2 * b + u - 1)
                sp.dma_start(v[u][:, :, :], tok(a["v"][b])[:, :, u * P:(u + 1) * P]).then_inc(v_ld[u], 16)

            def store(b):
                sp.wait_ge(ln, 4 * b + 4)
                sp.dma_start(tok(a["x2"][b]), x_in[:, :, :]).then_inc(x2_st, 16)

            def body(b):
                if isinstance(b, int) and b == B:
                    store(b - 2)
                    sp.wait_ge(x2_st, 16 * (b - 1))
                    sp.dma_start(x_in[:, :, :], tok(a["x1"][b - 1])).then_inc(x_ld, 16)
                    return
                if not isinstance(b, int) or b > 0:
                    chunk(b, 0)
                    chunk(b, 1)
                value(b, 0)
                chunk(b, 2)
                if since(b, 2):
                    store(b - 2)
                if since(b, 1):
                    wait(sp, x2_st, 16 * (b - 1))
                    sp.dma_start(x_in[:, :, :], tok(a["x1"][b - 1])).then_inc(x_ld, 16)
                chunk(b, 3)
                value(b, 1)
            chunk(0, 0)
            chunk(0, 1)
            sp.dma_start(bo[:, :], row_bc(a["L0_xattn_bo"], P)).then_inc(c_ld, 16)
            sp.dma_start(wo[:, :, :], a["L0_xattn_WoP"].rearrange("u p n -> p u n")).then_inc(c_ld, 16)
            batches(sp, body)
            store(B - 1)
            sp.wait_ge(x2_st, 16 * B)

        @block.gpsimd
        def _(pool):
            pool.memset(vm[:, :, :, :, :], 0.0).then_inc(pad_up, 1)
            pool.memset(mhalf[:, :], -0.5).then_inc(const_up, 1)
            pool.memset(ident[:, :], 0.0).then_inc(const_up, 1)
            pool.wait_ge(const_up, 2)
            pool.affine_select(out=ident[:, :], in_=ident[:, :], compare_op=ALU.not_equal, fill=1.0, base=0,
                               pattern=[[-1, P]], channel_multiplier=1).then_inc(const_up, 1)
            def root(b):
                pool.wait_ge(ln, 4 * b + 3)
                pool.tensor_tensor(rstd[:, :], ve[:, :], mhalf[:, :], ALU.pow).then_inc(rstd_up, 1)

            def body(b):
                for u, h, hh, n, real in slots(b):
                    if (u, h) == (0, 1) and since(b, 2):
                        root(b - 2)
                    if real:
                        pool.wait_ge(rinv_up, n + 1)
                        apart(pool, past_pool)
                        for t in range(T):
                            ins = pool.tensor_scalar(probs[h % NP][:, t, :], probs[h % NP][:, t, :], rinv[h % 2][:, t:t + 1], 1.0,
                                                     ALU.mult, ALU.mult)
                        ins.then_inc(norm_up, 1)
                    if (u, h) == (1, 2) and since(b, 1):
                        if isinstance(b, int) and b == 1:
                            pool.wait_ge(c_ld, 32)
                        pool.wait_ge(x_ld, 16 * b)
                        pool.tensor_tensor(x_in[:, :, :], x_in[:, :, :], bo[:, :].rearrange("p (o d) -> p o d", o=1).to_broadcast([P, T, D]),
                                           ALU.add).then_inc(xb_up, 1)
            batches(pool, body)
            root(B - 1)

        @block.scalar
        def _(act):
            def body(b):
                def exponentials(h, n, j):
                    act.wait_ge(max_up, 2 * n + j + 1)
                    for t in (2 * j, 2 * j + 1):
                        ins = act.activation(probs[h % NP][:, t, :], ps_s[j][:, t % 2, :], ACT.Exp,
                                             bias=nmax[h % 2][:, t:t + 1], accum_out=rsum[h % 2][:, t:t + 1])
                    ins.then_inc(exp_up, 1)

                for u, h, hh, n, real in slots(b):
                    if h == 6 and has_before2(b, u):
                        act.wait_ge(vals_up, 2 * b + u - 1)
                        wait(act, y_up, 2 * (b - 1))
                        act.activation(oT[:, u, :], ps_v[:, :], ACT.Copy).then_inc(oT_up, 1)
                    turned(act, b, u, h, n, real, 0)
                    if real:
                        wait(act, t_up, 4 * (n - 3))
                        exponentials(h, n, 0)
                    turned(act, b, u, h, n, real, 1)
                    if real:
                        exponentials(h, n, 1)
                    if not by_vector(h, 3):
                        turned(act, b, u, h, n, real, 3)
            batches(act, body)

        @block.vector
        def _(dve):
            dve.wait_ge(pad_up, 1)

            def reciprocal(n, h):
                dve.wait_ge(exp_up, 2 * n + 2)
                wait(dve, norm_up, n - 1)
                dve.reciprocal(rinv[h % 2][:, :], rsum[h % 2][:, :]).then_inc(rinv_up, 1)

            def maxima(n, h, j):
                dve.wait_ge(s_up, 2 * n + j + 1)
                dve.tensor_reduce(nmax[h % 2][:, 2 * j:2 * j + 2], ps_s[j][:, :, :], AX.X, ALU.max, negate=True).then_inc(max_up, 1)

            def search(b, u, h, places):
                if not has_before(b, u) or h < 3:
                    return
                base = PICK * (2 * b + u - 1)
                for step in (3 * (h - 3) + place for place in places):
                    n = (step - 1) // 2
                    if step == 0:
                        dve.wait_ge(sums_up, 2 * b + u)
                        wait(dve, pick, base)
                        dve.tensor_scalar(left[:, ::-1], ps_m[0:HU, :], -1.0, None, ALU.mult).then_inc(left_up, 1)
                    elif step == 2 * ROUNDS + 1:
                        dve.wait_ge(found, 2 * b + u)
                        dve.tensor_scalar(kept[:, ::-1], left[:, :], GONE, None, ALU.not_equal).then_inc(pick, 1)
                    elif step % 2:
                        if n == 0:
                            dve.wait_ge(left_up, 2 * b + u)
                        else:
                            wait(dve, pick, base + 2 * n)
                        apart(dve, past_dve)
                        dve.max(m8[:, :], left[:, :]).then_inc(pick, 1)
                        if n == ROUNDS - 1:
                            dve.wait_ge(pick, base + 2 * n + 1)
                            dve.memset(m8[:, DROP - 8 * n:8], GONE).then_inc(pick, 1)
                    else:
                        last = n == ROUNDS - 1
                        dve.wait_ge(pick, base + 2 * n + 1 + last)
                        apart(dve, past_dve)
                        dve.match_replace(left[:, :], m8[:, :], left[:, :], GONE).then_inc(found if last else pick, 1)

            def stats(b):
                dve.wait_ge(add_up, 2 * b + 2)
                for t in range(T):
                    ins = dve.bn_stats(st6[:, t, :], x_in[:, t, :])
                ins.then_inc(ln, 1)
                dve.wait_ge(ln, 4 * b + 1)
                apart(dve, past_dve)
                for t in range(T):
                    ins = dve.bn_aggr(mv[:, t, :], st6[:, t, :])
                ins.then_inc(ln, 1)
                dve.wait_ge(ln, 4 * b + 2)
                dve.tensor_scalar(ve[:, :], mv[:, :, 1], 1e-5, None, ALU.add).then_inc(ln, 1)

            def body(b):
                for u, h, hh, n, real in slots(b):
                    if real:
                        maxima(n, h, 0)
                    search(b, u, h, (0,))
                    if (real or (u, h) == (0, 0)) and not (isinstance(b, int) and n == 0):
                        reciprocal(n - 1, h - 1)
                    if real:
                        maxima(n, h, 1)
                    if h == 0 and has_before2(b, u):
                        dve.wait_ge(kept_up, 2 * b + u - 1)
                        dve.wait_ge(v_ld[u], 16 * b)
                        for q4 in range(2):
                            ins = dve.tensor_tensor(vm[:, :, q4, :, q4 * DK:(q4 + 1) * DK],
                                                    v[u][:, :, q4 * QH * DK:(q4 + 1) * QH * DK].rearrange("p t (j d) -> p t j d", d=DK),
                                                    ps_m[:, 0:T * HU].rearrange("p (t q j o) -> p t q j o", t=T, q=2, o=1)[:, :, q4, :, :]
                                                    .to_broadcast([P, T, QH, DK]), ALU.mult)
                        ins.then_inc(vm_up, 1)
                    search(b, u, h, (1,))
                    turned(dve, b, u, h, n, real, 2)
                    if by_vector(h, 3):
                        turned(dve, b, u, h, n, real, 3)
                    search(b, u, h, (2, 3) if h == HU - 1 else (2,))
                    if u == 1 and h in (6, 7) and since(b, 1):
                        i = h - 6
                        dve.wait_ge(y_up, 2 * b - 1 + i)
                        dve.wait_ge(xb_up, b)
                        dve.tensor_tensor(x_in[:, 2 * i:2 * i + 2, :], ps_m[:, :].rearrange("p (t d) -> p t d", t=2),
                                          x_in[:, 2 * i:2 * i + 2, :], ALU.add).then_inc(add_up, 1)
                    if (u, h) == (0, 0) and since(b, 2):
                        stats(b - 2)
                    if (u, h) == (0, 2) and since(b, 2):
                        finish(b - 2)

            def finish(b):
                dve.wait_ge(rstd_up, b + 1)
                for t in range(T):
                    ins = dve.tensor_scalar(x_in[:, t, :], x_in[:, t, :], mv[:, t, 0:1], rstd[:, t:t + 1], ALU.subtract, ALU.mult)
                ins.then_inc(ln, 1)
            batches(dve, body)
            stats(B - 1)
            finish(B - 1)

        @block.tensor
        def _(pe):
            pe.wait_ge(const_up, 3)

            def values(u, four, t):
                for j in range(QH):
                    ins = pe.matmul(ps_v[32 * j:32 * j + 32, :], vm[:, t, four, j, :], probT[u][:, QH * four + j, t, :],
                                    start=(four == 0 and t == 0), stop=(four == 1 and t == T - 1))
                if t == T - 1:
                    ins.then_inc((first_up, vals_up)[four], 1)

            def scores(b, hh, n, j):
                c = hh // CH
                if j == 0 and hh % CH == 0:
                    pe.wait_ge(qk_ld[c % 2], 192 * (2 * b + c // 2 + 1))
                wait(pe, exp_up, 2 * (n - 1) + j + 1)
                for t in (2 * j, 2 * j + 1):
                    ins = pe.matmul(ps_s[j][:, t % 2, :], q[c % 2][:, hh % CH, t * P:(t + 1) * P], k[c % 2][:, hh % CH, :],
                                    start=True, stop=True)
                ins.then_inc(s_up, 1)

            def turn(h, m, t):
                wait(pe, copied[(t + 2) % T], m + (t >= 2))
                for i in range(T):
                    ins = pe.transpose(ps_t[t % 2][:, i * P:(i + 1) * P], probs[(h - 2) % NP][:, i, t * P:(t + 1) * P], ident[:, :])
                ins.then_inc(t_up, 1)

            def body(b):
                for u, h, hh, n, real in slots(b):
                    if real and hh == 0:
                        scores(b, hh, n, 0)
                    if h == 2 and has_before2(b, u):
                        values(u, 0, 3)
                    if turning(b, u, h, n, real):
                        pe.wait_ge(norm_up, n - 1)
                        turn(h, n - 2, 0)
                    if real:
                        scores(b, hh, n, 1)
                    if h == 0 and has_before2(b, u):
                        pe.wait_ge(pick, PICK * (2 * b + u - 1))
                        if u == 0:
                            wait(pe, add_up, 2 * (b - 1))
                        else:
                            pe.wait_ge(left_up, 2 * b)
                        apart(pe, past_pe)
                        for t in range(T):
                            ins = pe.transpose(ps_m[:, t * HU:(t + 1) * HU], kept[:, t * P:(t + 1) * P], ident[0:HU, 0:HU])
                        ins.then_inc(kept_up, 1)
                    if h == 3 and has_before(b, u):
                        for t in range(T):
                            pe.wait_ge(copied[t], HU * (2 * b + u))
                        wait(pe, vm_up, 2 * b + u - 1)
                        for t in range(T):
                            ins = pe.transpose(ps_m[0:HU, t * P:(t + 1) * P], colsum[1 - u][:, t, :], ident[:, :])
                        ins.then_inc(sums_up, 1)
                    if turning(b, u, h, n, real):
                        turn(h, n - 2, 1)
                    if 2 <= h < 2 + T and has_before2(b, u):
                        values(u, 1, h - 2)
                    if u == 1 and h in (6, 7) and since(b, 1):
                        i = h - 6
                        if isinstance(b, int) and (b, h) == (1, 6):
                            pe.wait_ge(c_ld, 32)
                        pe.wait_ge(oT_up, 2 * b)
                        if i == 0:
                            pe.wait_ge(left_up, min(2 * b + 1, 2 * B) if isinstance(b, int) else 2 * b + 1)
                        else:
                            pe.wait_ge(add_up, 2 * b - 1)
                        for t in (2 * i, 2 * i + 1):
                            for g in range(2):
                                ins = pe.matmul(ps_m[:, (t % 2) * D:(t % 2 + 1) * D], oT[:, g, t * P:(t + 1) * P], wo[:, g, :],
                                                start=(g == 0), stop=(g == 1))
                        ins.then_inc(y_up, 1)
                    if h == 1 and has_before2(b, u):
                        values(u, 0, 1)
                        values(u, 0, 2)
                    if turning(b, u, h, n, real):
                        turn(h, n - 2, 2)
                    if real and hh < H0 - 1:
                        scores(b, hh + 1, n + 1, 0)
                    if turning(b, u, h, n, real):
                        turn(h, n - 2, 3)
                    if h == 0 and has_before2(b, u):
                        pe.wait_ge(vm_up, 2 * b + u - 1)
                        wait(pe, oT_up, 2 * b + u - 2)
                        values(u, 0, 0)
            batches(pe, body)


CAP = 1024
F = 512
FF = 128


def pairs(eng, body):
    for u in range(2):
        body(u, u, 0)
    with eng.Fori(1, B // 2) as i:
        for u in range(2):
            body(2 * i + u, u, i)


def col(ap):
    return ap.rearrange("p (n o) -> p n o", o=1)


def row(ap):
    return ap.rearrange("p (o n) -> p o n", o=1)


def stage_route(nc, a, route_w, route_i):
    BIG = 16384.0
    with ExitStack() as ctx:
        r = Room(nc, ctx, "ro")
        x_all = r.sb("x_all", [P, B, T, D])
        xd, xs, xsT, fo = ([r.sb(f"{n}{u}", s) for u in range(2)] for n, s in
                             (("xd", [P, T, D]), ("xs", [P, T, D]), ("xsT", [P, DH, S]), ("fo", [P, T, D])))
        junk = [r.sb(f"junk{u}", [P, T, D], BF16) for u in range(2)]
        ssq, msq, inv, rms = ([r.sb(f"{n}{u}", [P, T]) for u in range(2)] for n in ("ssq", "msq", "inv", "rms"))
        act_f = [r.sb(f"act_f{u}", [FF, S]) for u in range(2)]
        mhalf = r.sb("mhalf", [P, T])
        ident, before, ones = (r.sb(n, [P, P]) for n in ("ident", "before", "ones"))
        base_i = r.sb("base_i", [P, E], mybir.dt.int32)
        base = r.sb("base", [P, E])
        wr = r.sb("wr", [P, DH, E])
        fn = r.sb("fn", [P, DH])
        fwg, fwu = r.sb("fwg", [P, DH, FF]), r.sb("fwu", [P, DH, FF])
        fwd = r.sb("fwd", [FF, D])
        lg, ex, sel, pos, place, ap_, far, one, two = (r.sb(n, [P, T, E]) for n in
            ("lg", "ex", "sel", "pos", "place", "ap", "far", "one", "two"))
        pr, rep = r.sb("pr", [P, T, 2 * E]), r.sb("rep", [P, T, 2 * E])
        m8 = r.sb("m8", [P, T, 8])
        mx, sm, rs, top, tot, wab, ovf, nov = (r.sb(n, [P, T]) for n in ("mx", "sm", "rs", "top", "tot", "wab", "ovf", "nov"))
        pf = r.sb("pf", [P, 2, T])
        pi = [r.sb(f"pi{u}", [P, 2, T], U32) for u in range(2)]
        carry = r.sb("carry", [P, E])
        ps_t = r.ps("ps_t", [P, DH, S])
        ps_g, ps_u = r.ps("ps_g", [FF, S]), r.ps("ps_u", [FF, S])
        ps_f = r.ps("ps_f", [P, T, D])
        ps_l, ps_p = r.ps("ps_l", [P, T, E]), r.ps("ps_p", [P, 2, T, E])
        c_ld, const_up, const_v, past_dve, past_pool = (r.sem(n) for n in ("c_ld", "const_up", "const_v", "past_dve", "past_pool"))
        ld = [r.sem(f"ld{j}") for j in range(B)]
        st, sent = ([r.sem(f"{n}{u}") for u in range(2)] for n in ("st", "sent"))
        xd_up, past_act = r.sem("xd_up"), r.sem("past_act")
        sq_up, msq_up, inv_up, xs_up, t_up, xsT_up, lg_up, ffn_up, soft, soft_s, gelu_up, hid_up, f_up, fo_up, v, pos_up, ind_up = (
            r.sem(n) for n in ("sq_up", "msq_up", "inv_up", "xs_up", "t_up", "xsT_up", "lg_up", "ffn_up", "soft", "soft_s",
                               "gelu_up", "hid_up", "f_up", "fo_up", "v", "pos_up", "ind_up"))
        NV = 24
        block = ctx.enter_context(nc.Block())

        def rounds(eng, body):
            body(0, 0, 0, True)
            body(1, 1, 0, True)
            with eng.Fori(1, B // 2 - 1) as i:
                for u in range(2):
                    body(2 * i + u, u, i, True)
            body(B - 2, 0, B // 2 - 1, True)
            body(B - 1, 1, B // 2 - 1, False)

        @block.sync
        def _(sp):
            for b in range(B):
                sp.dma_start(x_all[:, b, :, :], tok(a["x2"][b])).then_inc(ld[b], 16)
            with nc.allow_non_contiguous_dma(reason="small weights"):
                sp.dma_start(fn[:, :], a["L0_ffn_f_norm"].rearrange("(h p) -> p h", p=P)).then_inc(c_ld, 16)
            sp.dma_start(wr[:, :, :], a["L0_ffn_Wr"].rearrange("(h p) e -> p h e", p=P)).then_inc(c_ld, 16)
            sp.dma_start(fwg[:, :, :], a["L0_ffn_fWg"].rearrange("(h p) f -> p h f", p=P)).then_inc(c_ld, 16)
            sp.dma_start(fwu[:, :, :], a["L0_ffn_fWu"].rearrange("(h p) f -> p h f", p=P)).then_inc(c_ld, 16)
            sp.dma_start(fwd[:, :], a["L0_ffn_fWd"]).then_inc(c_ld, 16)

            def body(b, u, i, more):
                sp.wait_ge(fo_up, b + 1)
                sp.dma_start(tok(a["fallback"][b]), fo[u][:, :, :]).then_inc(st[u], 16)
            rounds(sp, body)
            for u in range(2):
                sp.wait_ge(st[u], 16 * B // 2)
                sp.wait_ge(sent[u], 16 * 2 * T * B // 2)

        @block.gpsimd
        def _(pool):
            pool.memset(mhalf[:, :], -0.5).then_inc(const_up, 1)
            pool.memset(ident[:, :], 0.0).then_inc(const_up, 1)
            pool.memset(before[:, :], 1.0).then_inc(const_up, 1)
            pool.memset(ones[:, :], 1.0).then_inc(const_up, 1)
            pool.memset(pr[:, :, :], -1.0).then_inc(const_up, 1)
            pool.memset(carry[:, :], 0.0).then_inc(const_up, 1)
            pool.iota(base_i[:, :], pattern=[[CAP, E]], base=1, channel_multiplier=0).then_inc(const_up, 1)
            pool.wait_ge(const_up, 7)
            pool.tensor_copy(base[:, :], base_i[:, :]).then_inc(const_up, 1)
            pool.affine_select(out=ident[:, :], in_=ident[:, :], compare_op=ALU.not_equal, fill=1.0, base=0,
                               pattern=[[-1, P]], channel_multiplier=1).then_inc(const_up, 1)
            pool.affine_select(out=before[:, :], in_=before[:, :], compare_op=ALU.is_gt, fill=0.0, base=0,
                               pattern=[[1, P]], channel_multiplier=-1).then_inc(const_up, 1)

            def root(b, u):
                pool.wait_ge(msq_up, b + 1)
                pool.tensor_tensor(inv[u][:, :], msq[u][:, :], mhalf[:, :], ALU.pow).then_inc(inv_up, 1)
            root(0, 0)

            def body(b, u, i, more):
                if more:
                    root(b + 1, 1 - u)
                pool.wait_ge(xd_up, b + 1)
                pool.wait_ge(ind_up, b + 1)
                apart(pool, past_pool)
                for n in range(2):
                    for t in range(T):
                        pool.indirect_dma_start(out=a["buf"], out_offset=bass.IndirectOffsetOnAxis(ap=pi[u][:, n, t:t + 1], axis=0),
                                                in_=xd[u][:, t, :], in_offset=None, bounds_check=E * CAP - 1,
                                                oob_is_err=False).then_inc(sent[u], 16)
            rounds(pool, body)

        @block.scalar
        def _(act):
            def square(b, u):
                wait(act, msq_up, b - 1)
                for t in range(T):
                    ins = act.activation(junk[u][:, t, :], x_all[:, bass.ds(b, 1), t, :].rearrange("p o d -> p (o d)"), ACT.Square,
                                         accum_out=ssq[u][:, t:t + 1])
                ins.then_inc(sq_up, 1)

            def turned(b, u):
                act.wait_ge(t_up, b + 1)
                wait(act, lg_up, b - 1)
                wait(act, ffn_up, b - 1)
                act.activation(xsT[u][:, :, :], ps_t[:, :, :], ACT.Copy).then_inc(xsT_up, 1)

            act.wait_ge(ld[0], 16)
            square(0, 0)
            turned(0, 0)
            for b in range(1, B):
                act.wait_ge(ld[b], 16)

            def body(b, u, i, more):
                act.wait_ge(v, NV * b + 3)
                act.activation(ex[:, :, :], lg[:, :, :], ACT.Exp).then_inc(soft_s, 1)
                if more:
                    square(b + 1, 1 - u)
                wait(act, sent[u], 16 * 2 * T * i)
                apart(act, past_act)
                act.activation(xd[u][:, :, :], x_all[:, bass.ds(b, 1), :, :].rearrange("p o t d -> p (o t) d"), ACT.Copy).then_inc(xd_up, 1)
                if more:
                    turned(b + 1, 1 - u)
                act.wait_ge(ffn_up, b + 1)
                wait(act, f_up, b - 1)
                act.activation(act_f[u][:, :], ps_g[:, :], ACT.Gelu).then_inc(gelu_up, 1)
            rounds(act, body)

        @block.vector
        def _(dve):
            dve.wait_ge(c_ld, 80)
            dve.wait_ge(const_up, 10)
            for h in range(DH):
                dve.tensor_scalar(fwg[:, h, :], fwg[:, h, :], fn[:, h:h + 1], None, ALU.mult).then_inc(const_v, 1)
                dve.tensor_scalar(fwu[:, h, :], fwu[:, h, :], fn[:, h:h + 1], None, ALU.mult).then_inc(const_v, 1)

            def square(b, u):
                dve.wait_ge(sq_up, b + 1)
                wait(dve, inv_up, b - 1)
                dve.tensor_scalar(msq[u][:, :], ssq[u][:, :], 1.0 / D, 1e-6, ALU.mult, ALU.add).then_inc(msq_up, 1)

            def normalize(b, u):
                dve.wait_ge(inv_up, b + 1)
                wait(dve, t_up, b - 1)
                dve.reciprocal(rms[u][:, :], inv[u][:, :])
                for t in range(T):
                    ins = dve.tensor_scalar(xs[u][:, t, :], x_all[:, bass.ds(b, 1), t, :].rearrange("p o d -> p (o d)"),
                                            inv[u][:, t:t + 1], None, ALU.mult)
                ins.then_inc(xs_up, 1)

            square(0, 0)
            normalize(0, 0)
            for b in range(1, B):
                dve.wait_ge(ld[b], 16)

            def body(b, u, i, more):
                step = [0]

                def then(ins):
                    step[0] += 1
                    ins.then_inc(v, 1)
                    dve.wait_ge(v, NV * b + step[0])
                    if step[0] in (6, 8):
                        apart(dve, past_dve)

                dve.wait_ge(lg_up, b + 1)
                dve.wait_ge(xs_up, b + 1)
                then(dve.tensor_tensor(lg[:, :, :], ps_l[:, :, :], col(rms[u][:, :]).to_broadcast([P, T, E]), ALU.mult))
                then(dve.tensor_reduce(mx[:, :], lg[:, :, :], AX.X, ALU.max))
                then(dve.tensor_tensor(lg[:, :, :], lg[:, :, :], col(mx[:, :]).to_broadcast([P, T, E]), ALU.subtract))
                dve.wait_ge(soft_s, b + 1)
                then(dve.tensor_reduce(sm[:, :], ex[:, :, :], AX.X, ALU.add))
                then(dve.reciprocal(rs[:, :], sm[:, :]))
                then(dve.tensor_tensor(pr[:, :, 0:E], ex[:, :, :], col(rs[:, :]).to_broadcast([P, T, E]), ALU.mult))
                for t in range(T):
                    ins = dve.max(m8[:, t, :], pr[:, t, :])
                then(ins)
                then(dve.memset(m8[:, :, 2:8], -1.0))
                for t in range(T):
                    ins = dve.match_replace(rep[:, t, :], m8[:, t, :], pr[:, t, :], -1.0)
                then(ins)
                then(dve.tensor_tensor(sel[:, :, :], pr[:, :, 0:E], rep[:, :, 0:E], ALU.not_equal))
                if more:
                    square(b + 1, 1 - u)
                    normalize(b + 1, 1 - u)
                dve.wait_ge(pos_up, b + 1)
                then(dve.tensor_tensor(pos[:, :, :], ps_p[:, 0, :, :], row(carry[:, :]).to_broadcast([P, T, E]), ALU.add))
                then(dve.tensor_tensor(carry[:, :], carry[:, :], ps_p[:, 1, 0, :], ALU.add))
                then(dve.tensor_scalar(far[:, :, :], pos[:, :, :], float(CAP), BIG, ALU.is_ge, ALU.mult))
                then(dve.tensor_tensor(pos[:, :, :], pos[:, :, :], far[:, :, :], ALU.add))
                then(dve.tensor_tensor(pos[:, :, :], pos[:, :, :], row(base[:, :]).to_broadcast([P, T, E]), ALU.add))
                then(dve.tensor_tensor(place[:, :, :], pos[:, :, :], sel[:, :, :], ALU.mult))
                then(dve.tensor_reduce(top[:, :], place[:, :, :], AX.X, ALU.max))
                dve.tensor_reduce(tot[:, :], place[:, :, :], AX.X, ALU.add)
                dve.tensor_scalar(ovf[:, :], top[:, :], BIG, None, ALU.is_gt)
                dve.tensor_tensor(ap_[:, :, :], pr[:, :, 0:E], sel[:, :, :], ALU.mult)
                dve.tensor_tensor(one[:, :, :], place[:, :, :], col(top[:, :]).to_broadcast([P, T, E]), ALU.is_equal)
                then(dve.tensor_tensor(two[:, :, :], place[:, :, :], col(top[:, :]).to_broadcast([P, T, E]), ALU.not_equal))
                dve.tensor_scalar(pf[:, 0, :], top[:, :], -1.0, None, ALU.add)
                dve.tensor_scalar(nov[:, :], ovf[:, :], -1.0, 1.0, ALU.mult, ALU.add)
                dve.tensor_tensor(one[:, :, :], one[:, :, :], ap_[:, :, :], ALU.mult)
                dve.tensor_tensor(two[:, :, :], two[:, :, :], ap_[:, :, :], ALU.mult)
                then(dve.scalar_tensor_tensor(pf[:, 1, :], tot[:, :], -1.0, top[:, :], ALU.add, ALU.subtract))
                wait(dve, sent[u], 16 * 2 * T * i)
                dve.tensor_copy(pi[u][:, :, :], pf[:, :, :]).then_inc(ind_up, 1)
                dve.tensor_scalar(route_i[:, bass.ds(b, 1), :, :].rearrange("p o n t -> p (o n) t"), pf[:, :, :], float(E * CAP - 1), None, ALU.min)
                dve.tensor_copy(route_w[:, bass.ds(b, 1), 2, :].rearrange("p o t -> p (o t)"), ovf[:, :])
                dve.tensor_reduce(wab[:, :], one[:, :, :], AX.X, ALU.add)
                then(dve.tensor_reduce(mx[:, :], two[:, :, :], AX.X, ALU.add))
                dve.tensor_tensor(route_w[:, bass.ds(b, 1), 0, :].rearrange("p o t -> p (o t)"), wab[:, :], nov[:, :], ALU.mult)
                then(dve.tensor_tensor(route_w[:, bass.ds(b, 1), 1, :].rearrange("p o t -> p (o t)"), mx[:, :], nov[:, :], ALU.mult))
                while step[0] < NV:
                    then(dve.memset(m8[:, 0, 0:1], -1.0))
                dve.wait_ge(gelu_up, b + 1)
                dve.tensor_tensor(act_f[u][:, :], act_f[u][:, :], ps_u[:, :], ALU.mult).then_inc(hid_up, 1)
                dve.wait_ge(f_up, b + 1)
                wait(dve, st[u], 16 * i)
                dve.tensor_tensor(fo[u][:, :, :], ps_f[:, :, :], x_all[:, bass.ds(b, 1), :, :].rearrange("p o t d -> p (o t) d"), ALU.add).then_inc(fo_up, 1)
            rounds(dve, body)

        @block.tensor
        def _(pe):
            pe.wait_ge(const_v, 4)

            def turn(b, u):
                pe.wait_ge(xs_up, b + 1)
                wait(pe, xsT_up, b)
                for h in range(DH):
                    for t in range(T):
                        ins = pe.transpose(ps_t[:, h, t * P:(t + 1) * P], xs[u][:, t, h * P:(h + 1) * P], ident[:, :])
                ins.then_inc(t_up, 1)

            def logits(b, u):
                pe.wait_ge(xsT_up, b + 1)
                for t in range(T):
                    for h in range(DH):
                        ins = pe.matmul(ps_l[:, t, :], xsT[u][:, h, t * P:(t + 1) * P], wr[:, h, :], start=(h == 0), stop=(h == DH - 1))
                ins.then_inc(lg_up, 1)

            turn(0, 0)
            logits(0, 0)

            def body(b, u, i, more):
                wait(pe, hid_up, b)
                for w, ps in ((fwg, ps_g), (fwu, ps_u)):
                    for h in range(DH):
                        ins = pe.matmul(ps[:, :], w[:, h, :], xsT[u][:, h, :], start=(h == 0), stop=(h == DH - 1))
                ins.then_inc(ffn_up, 1)
                pe.wait_ge(v, NV * b + 10)
                for t in range(T):
                    for s in range(t + 1):
                        pe.matmul(ps_p[:, 0, t, :], (before if s == t else ones)[:, :], sel[:, s, :], start=(s == 0), stop=(s == t))
                for s in range(T):
                    ins = pe.matmul(ps_p[:, 1, 0, :], ones[:, :], sel[:, s, :], start=(s == 0), stop=(s == T - 1))
                ins.then_inc(pos_up, 1)
                if more:
                    turn(b + 1, 1 - u)
                    logits(b + 1, 1 - u)
                pe.wait_ge(hid_up, b + 1)
                wait(pe, fo_up, b)
                for t in range(T):
                    ins = pe.matmul(ps_f[:, t, :], act_f[u][:, t * P:(t + 1) * P], fwd[:, :], start=True, stop=True)
                ins.then_inc(f_up, 1)
            rounds(pe, body)


def stage_experts(nc, a):
    FT = F // P
    NU = 2 * E
    with ExitStack() as ctx:
        r = Room(nc, ctx, "ex")
        x_in = [r.sb(f"x{j}", [P, T, D]) for j in range(4)]
        xs, xsT, out = ([r.sb(f"{n}{u}", s) for u in range(2)] for n, s in
                              (("xs", [P, T, D]), ("xsT", [P, DH, S]), ("out", [P, T, D])))
        junk = [r.sb(f"junk{u}", [P, T, D], BF16) for u in range(2)]
        ssq, msq, inv = ([r.sb(f"{n}{u}", [P, T]) for u in range(2)] for n in ("ssq", "msq", "inv"))
        hid = [r.sb(f"hid{u}", [P, FT, S]) for u in range(2)]
        wg, wu = ([r.sb(f"{n}{u}", [P, DH, F]) for u in range(2)] for n in ("wg", "wu"))
        wd = [r.sb(f"wd{u}", [P, FT, D]) for u in range(2)]
        nw = [r.sb(f"nw{u}", [P, DH]) for u in range(2)]
        mhalf = r.sb("mhalf", [P, T])
        ident = r.sb("ident", [P, P])
        ps_t = r.ps("ps_t", [P, DH, S])
        ps_g = [r.ps(f"ps_g{j}", [P, S]) for j in range(2)]
        ps_u = [r.ps(f"ps_u{j}", [P, S]) for j in range(2)]
        ps_d = r.ps("ps_d", [P, T, D])
        const_up = r.sem("const_up")
        ld = [r.sem(f"ld{j}") for j in range(4)]
        st, w_ld = ([r.sem(f"{n}{u}") for u in range(2)] for n in ("st", "w_ld"))
        sq_up, msq_up, inv_up, xs_up, t_up, xsT_up, gu_up, gelu_up, hid_up, d_up, out_up = (r.sem(n) for n in
            ("sq_up", "msq_up", "inv_up", "xs_up", "t_up", "xsT_up", "gu_up", "gelu_up", "hid_up", "d_up", "out_up"))
        block = ctx.enter_context(nc.Block())

        def quads(eng, body, first=None):
            if first:
                first()
            for j in range(4):
                body(j, j, 0, True)
            with eng.Fori(1, E // 2 - 1) as i:
                for j in range(4):
                    body(4 * i + j, j, i, True)
            for j in range(4):
                body(NU - 4 + j, j, E // 2 - 1, j < 3)

        @block.sync
        def _(sp):
            def weights(e, w):
                sp.dma_start(wg[w][:, :, :], a["L0_ffn_Wg"][e].rearrange("(h p) f -> p h f", p=P)).then_inc(w_ld[w], 16)
                sp.dma_start(wu[w][:, :, :], a["L0_ffn_Wu"][e].rearrange("(h p) f -> p h f", p=P)).then_inc(w_ld[w], 16)
                sp.dma_start(wd[w][:, :, :], a["L0_ffn_Wd"][e].rearrange("(h p) n -> p h n", p=P)).then_inc(w_ld[w], 16)
                sp.dma_start(nw[w][:, :], a["L0_ffn_norm_wP"][e]).then_inc(w_ld[w], 16)

            def rows(ap, m):
                return ap[bass.ds(m * S, S), :] if not isinstance(m, int) else ap[m * S:(m + 1) * S, :]

            def load(m, j):
                sp.dma_start(x_in[j][:, :, :], tok(rows(a["buf"], m))).then_inc(ld[j], 16)

            for j in range(2):
                load(j, j)
            weights(0, 0)
            weights(1, 1)
            for j in range(2, 4):
                load(j, j)

            def body(m, j, u, last):
                sp.wait_ge(out_up, m + 1)
                sp.dma_start(tok(rows(a["results"], m)), out[u][:, :, :]).then_inc(st[u], 16)
                if not last:
                    load(m + 4, j)

            with sp.Fori(0, E // 2 - 1) as i:
                for j in range(4):
                    body(4 * i + j, j, j % 2, False)
                    if j % 2:
                        weights(2 * i + 2 + j // 2, j // 2)
            for j in range(4):
                body(NU - 4 + j, j, j % 2, True)
            for u in range(2):
                sp.wait_ge(st[u], 16 * NU // 2)

        @block.gpsimd
        def _(pool):
            pool.memset(mhalf[:, :], -0.5).then_inc(const_up, 1)
            pool.memset(ident[:, :], 0.0).then_inc(const_up, 1)
            pool.wait_ge(const_up, 2)
            pool.affine_select(out=ident[:, :], in_=ident[:, :], compare_op=ALU.not_equal, fill=1.0, base=0,
                               pattern=[[-1, P]], channel_multiplier=1).then_inc(const_up, 1)

            def body(m, j4, i, more):
                u = j4 % 2
                pool.wait_ge(msq_up, m + 1)
                pool.tensor_tensor(inv[u][:, :], msq[u][:, :], mhalf[:, :], ALU.pow).then_inc(inv_up, 1)
            quads(pool, body)

        @block.scalar
        def _(act):
            def square(m, j4, i):
                u = j4 % 2
                act.wait_ge(ld[j4], 16 * i + 16)
                wait(act, msq_up, m - 1)
                for t in range(T):
                    ins = act.activation(junk[u][:, t, :], x_in[j4][:, t, :], ACT.Square, accum_out=ssq[u][:, t:t + 1])
                ins.then_inc(sq_up, 1)

            def turn(m, w, u):
                act.wait_ge(t_up, m + 1)
                wait(act, gu_up, FT * (m - 1))
                for h in range(DH):
                    ins = act.activation(xsT[u][:, h, :], ps_t[:, h, :], ACT.Copy, scale=nw[w][:, h:h + 1])
                ins.then_inc(xsT_up, 1)

            def first():
                act.wait_ge(w_ld[0], 64)
                square(0, 0, 0)
                turn(0, 0, 0)

            def body(m, j4, i, more):
                w, u, follows, fi = j4 // 2, j4 % 2, (j4 + 1) % 4, i + (j4 == 3)
                if more:
                    square(m + 1, follows, fi)
                wait(act, d_up, m - 1)
                for j in range(FT):
                    act.wait_ge(gu_up, FT * m + j + 1)
                    act.activation(hid[u][:, j, :], ps_g[j % 2][:, :], ACT.Gelu).then_inc(gelu_up, 1)
                if more:
                    if u:
                        act.wait_ge(w_ld[1 - w], 64 * (i + 1 + w))
                    turn(m + 1, w if u == 0 else 1 - w, 1 - u)
            quads(act, body, first)

        @block.vector
        def _(dve):
            def norm(m, j4):
                u = j4 % 2
                dve.wait_ge(sq_up, m + 1)
                wait(dve, inv_up, m - 1)
                dve.tensor_scalar(msq[u][:, :], ssq[u][:, :], 1.0 / D, 1e-6, ALU.mult, ALU.add).then_inc(msq_up, 1)
                dve.wait_ge(inv_up, m + 1)
                wait(dve, t_up, m - 1)
                for t in range(T):
                    ins = dve.tensor_scalar(xs[u][:, t, :], x_in[j4][:, t, :], inv[u][:, t:t + 1], None, ALU.mult)
                ins.then_inc(xs_up, 1)

            def body(m, j4, i, more):
                w, u, follows, fi = j4 // 2, j4 % 2, (j4 + 1) % 4, i + (j4 == 3)
                if more:
                    norm(m + 1, follows)
                for j in range(FT):
                    dve.wait_ge(gelu_up, FT * m + j + 1)
                    dve.tensor_tensor(hid[u][:, j, :], hid[u][:, j, :], ps_u[j % 2][:, :], ALU.mult).then_inc(hid_up, 1)
                dve.wait_ge(d_up, m + 1)
                wait(dve, st[u], 16 * (m // 2) if isinstance(m, int) else 8 * (m - u))
                dve.tensor_tensor(out[u][:, :, :], ps_d[:, :, :], x_in[j4][:, :, :], ALU.add).then_inc(out_up, 1)
            quads(dve, body, lambda: norm(0, 0))

        @block.tensor
        def _(pe):
            pe.wait_ge(const_up, 3)

            def turn(m, u):
                pe.wait_ge(xs_up, m + 1)
                wait(pe, xsT_up, m)
                for h in range(DH):
                    for t in range(T):
                        ins = pe.transpose(ps_t[:, h, t * P:(t + 1) * P], xs[u][:, t, h * P:(h + 1) * P], ident[:, :])
                ins.then_inc(t_up, 1)

            def body(m, j4, i, more):
                w, u, follows, fi = j4 // 2, j4 % 2, (j4 + 1) % 4, i + (j4 == 3)
                if u == 0:
                    pe.wait_ge(w_ld[w], 64 * (i + 1))
                pe.wait_ge(xsT_up, m + 1)
                for j in range(FT):
                    wait(pe, hid_up, FT * m + j - 1)
                    for wt, ps in ((wg[w], ps_g[j % 2]), (wu[w], ps_u[j % 2])):
                        for h in range(DH):
                            ins = pe.matmul(ps[:, :], wt[:, h, j * P:(j + 1) * P], xsT[u][:, h, :], start=(h == 0), stop=(h == DH - 1))
                    ins.then_inc(gu_up, 1)
                if more:
                    turn(m + 1, 1 - u)
                pe.wait_ge(hid_up, FT * m + FT - 1)
                wait(pe, out_up, m)
                for t in range(T):
                    for j in range(FT):
                        if (t, j) == (0, FT - 1):
                            pe.wait_ge(hid_up, FT * m + FT)
                        ins = pe.matmul(ps_d[:, t, :], hid[u][:, j, t * P:(t + 1) * P], wd[w][:, j, :], start=(j == 0), stop=(j == FT - 1))
                ins.then_inc(d_up, 1)
            quads(pe, body, lambda: turn(0, 0))


M = 64


def moments(dve, then, z, st6, mv, ve, past_dve):
    for t in range(T):
        ins = dve.bn_stats(st6[:, t, :], z[:, t, :])
    then(ins)
    apart(dve, past_dve)
    for t in range(T):
        ins = dve.bn_aggr(mv[:, t, :], st6[:, t, :])
    then(ins)
    return dve.tensor_scalar(ve[:, :], mv[:, :, 1], 1e-5, None, ALU.add)


def normalized(dve, out, z, mv, rstd):
    for t in range(T):
        ins = dve.tensor_scalar(out[:, t, :], z[:, t, :], mv[:, t, 0:1], rstd[:, t:t + 1], ALU.subtract, ALU.mult)
    return ins


def stage_memory(nc, a, route_w, route_i):
    FADE = S.bit_length() - 1
    with ExitStack() as ctx:
        r = Room(nc, ctx, "me")
        x_in, fb = ([r.sb(f"{n}{u}", [P, T, D]) for u in range(2)] for n in ("x", "fb"))
        rows = [r.sb(f"rows{u}", [P, 2, T, D]) for u in range(2)]
        idx = [r.sb(f"idx{u}", [P, 2, T], U32) for u in range(2)]
        wt = [r.sb(f"wt{u}", [P, 4, T]) for u in range(2)]
        x3, x3b, x4 = ([r.sb(f"{n}{u}", [P, T, D]) for u in range(2)] for n in ("x3", "x3b", "x4"))
        x3T = [r.sb(f"x3T{u}", [P, DH, S]) for u in range(2)]
        z, z2 = r.sb("z", [P, T, D]), r.sb("z2", [P, T, D])
        st6, st6b, mv, mvb = r.sb("st6", [P, T, 6]), r.sb("st6b", [P, T, 6]), r.sb("mv", [P, T, 2]), r.sb("mvb", [P, T, 2])
        ve, veb, rstd, rstdb, mhalf = (r.sb(n, [P, T]) for n in ("ve", "veb", "rstd", "rstdb", "mhalf"))
        wq, wk = r.sb("wq", [P, DH, P]), r.sb("wk", [P, DH, P])
        wv = r.sb("wv", [P, DH, M + 2])
        wo = r.sb("wo", [P, D])
        bo = r.sb("bo", [P, D])
        bg, dp, sg = (r.sb(n, [P, 1]) for n in ("bg", "dp", "sg"))
        decay = r.sb("decay", [P, FADE + 1])
        age_i = r.sb("age_i", [P, 1], mybir.dt.int32)
        age, fade = r.sb("age", [P, 1]), r.sb("fade", [P, S])
        ident = r.sb("ident", [P, P])
        qT, kT, oT = ([r.sb(f"{n}{u}", [P, S]) for u in range(2)] for n in ("qT", "kT", "oT"))
        gv = r.sb("gv", [P, T, P])
        g, g2 = r.sb("g", [P, T]), r.sb("g2", [P, T])
        aT = [r.sb(f"aT{j}", [P, S]) for j in range(2)]
        ps_t, ps_y = r.ps("ps_t", [P, DH, S]), r.ps("ps_y", [P, T, D])
        ps_v, ps_o = r.ps("ps_v", [P, T, P]), r.ps("ps_o", [P, S])
        ps_a = [r.ps(f"ps_a{j}", [P, S]) for j in range(2)]
        c_ld, const_up, pad_up, fade_up, past_dve, past_pool = (r.sem(n) for n in
            ("c_ld", "const_up", "pad_up", "fade_up", "past_dve", "past_pool"))
        ld, gat, st = ([r.sem(f"{n}{u}") for u in range(2)] for n in ("ld", "gat", "st"))
        idx_up, vf, vb, var_up, rstd_up, x3_up, xb_up, varb_up, rstdb_up = (r.sem(n) for n in
            ("idx_up", "vf", "vb", "var_up", "rstd_up", "x3_up", "xb_up", "varb_up", "rstdb_up"))
        t_up, xT_up, q_up, qk_s, v_up, g_up, gv_up, a_up, at_up, o_up, oT_up, y_up, z2_up, x4_up = (r.sem(n) for n in
            ("t_up", "xT_up", "q_up", "qk_s", "v_up", "g_up", "gv_up", "a_up", "at_up", "o_up", "oT_up", "y_up", "z2_up", "x4_up"))
        grown = r.sem("grown")
        z_up, at_free = r.sem("z_up"), r.sem("at_free")
        NF, NB = 6, 3
        block = ctx.enter_context(nc.Block())

        @block.sync
        def _(sp):
            sp.wait_ge(pad_up, 4)
            for w, n in ((wq, "Wq"), (wk, "Wk"), (wv, "Wv")):
                sp.dma_start(w[:, :, 0:M], a[f"L1_attn_{n}"].rearrange("(h p) m -> p h m", p=P)).then_inc(c_ld, 16)
            with nc.allow_non_contiguous_dma(reason="256 weights"):
                sp.dma_start(wv[:, :, M:M + 1], a["L1_attn_Wg"].rearrange("(h p) m -> p h m", p=P)).then_inc(c_ld, 16)
            sp.dma_start(wo[0:M, :], a["L1_attn_Wo"]).then_inc(c_ld, 16)
            for w, n in ((bo, "bo"), (bg, "bg"), (dp, "decay_param")):
                sp.dma_start(w[:, :], row_bc(a[f"L1_attn_{n}"], P)).then_inc(c_ld, 16)

            def load(b, u):
                sp.dma_start(x_in[u][:, :, :], tok(a["x2"][b])).then_inc(ld[u], 16)
                sp.dma_start(fb[u][:, :, :], tok(a["fallback"][b])).then_inc(ld[u], 16)

            def store(b, u):
                sp.wait_ge(x4_up, b + 1)
                sp.dma_start(tok(a["x4"][b]), x4[u][:, :, :]).then_inc(st[u], 16)

            for u in range(2):
                load(u, u)
            with sp.Fori(0, B // 2 - 1) as i:
                for u in range(2):
                    sp.wait_ge(x3_up, 2 * i + u + 1)
                    load(2 * i + u + 2, u)
                    store(2 * i + u, u)
            for u in range(2):
                store(B - 2 + u, u)
            for u in range(2):
                sp.wait_ge(st[u], 16 * B // 2)

        @block.gpsimd
        def _(pool):
            for w in (wq[:, :, :], wk[:, :, :], wv[:, :, :], wo[:, :]):
                pool.memset(w, 0.0).then_inc(pad_up, 1)
            pool.memset(gv[:, :, :], 0.0).then_inc(const_up, 1)
            pool.memset(mhalf[:, :], -0.5).then_inc(const_up, 1)
            pool.memset(ident[:, :], 0.0).then_inc(const_up, 1)
            pool.iota(age_i[:, :], pattern=[[1, 1]], base=0, channel_multiplier=-1).then_inc(const_up, 1)
            pool.wait_ge(const_up, 4)
            pool.tensor_copy(age[:, :], age_i[:, :]).then_inc(const_up, 1)
            pool.affine_select(out=ident[:, :], in_=ident[:, :], compare_op=ALU.not_equal, fill=1.0, base=0,
                               pattern=[[-1, P]], channel_multiplier=1).then_inc(const_up, 1)

            def gather(b, u):
                pool.wait_ge(idx_up, b + 1)
                apart(pool, past_pool)
                for n in range(2):
                    for t in range(T):
                        pool.indirect_dma_start(out=rows[u][:, n, t, :], out_offset=None, in_=a["results"],
                                                in_offset=bass.IndirectOffsetOnAxis(ap=idx[u][:, n, t:t + 1], axis=0)).then_inc(gat[u], 16)

            gather(0, 0)
            pool.wait_ge(fade_up, 2)
            pool.wait_ge(const_up, 6)
            pool.tensor_tensor(fade[:, 0:1], decay[:, 0:1], age[:, 0:1], ALU.pow).then_inc(fade_up, 1)
            gather(1, 1)
            pool.wait_ge(c_ld, 128)

            def front(b, u, i):
                pool.wait_ge(var_up, b + 1)
                pool.tensor_tensor(rstd[:, :], ve[:, :], mhalf[:, :], ALU.pow).then_inc(rstd_up, 1)
                pool.wait_ge(x3_up, b + 1)
                wait(pool, z2_up, b - 1)
                pool.tensor_tensor(x3b[u][:, :, :], x3[u][:, :, :], row(bo[:, :]).to_broadcast([P, T, D]), ALU.add).then_inc(xb_up, 1)

            def back(b):
                pool.wait_ge(varb_up, b + 1)
                pool.tensor_tensor(rstdb[:, :], veb[:, :], mhalf[:, :], ALU.pow).then_inc(rstdb_up, 1)

            front(0, 0, 0)
            pool.wait_ge(grown, 2 * FADE)
            pool.affine_select(out=fade[:, :], in_=fade[:, :], compare_op=ALU.is_ge, fill=0.0, base=0,
                               pattern=[[1, S]], channel_multiplier=-1).then_inc(fade_up, 1)
            gather(2, 0)
            front(1, 1, 0)
            back(0)
            gather(3, 1)
            with pool.Fori(1, B // 2 - 1) as i:
                for u in range(2):
                    front(2 * i + u, u, i)
                    back(2 * i + u - 1)
                    gather(2 * i + u + 2, u)
            for u in range(2):
                front(B - 2 + u, u, B // 2 - 1)
                back(B - 3 + u)
            back(B - 1)

        @block.scalar
        def _(act):
            act.wait_ge(c_ld, 128)
            act.activation(sg[:, :], dp[:, :], ACT.Sigmoid).then_inc(fade_up, 1)

            def body(b, u, i):
                act.wait_ge(t_up, b + 1)
                wait(act, v_up, b - 1)
                act.activation(x3T[u][:, :, :], ps_t[:, :, :], ACT.Copy).then_inc(xT_up, 1)
                for n, dst in enumerate((qT, kT)):
                    act.wait_ge(q_up, 2 * b + n + 1)
                    wait(act, a_up, 4 * (b - 1))
                    act.activation(dst[u][:, :], ps_a[n][:, :], ACT.Copy).then_inc(qk_s, 1)
                act.wait_ge(v_up, b + 1)
                wait(act, gv_up, b)
                act.activation(g[:, :], ps_v[:, :, M], ACT.Sigmoid, bias=bg[:, 0:1]).then_inc(g_up, 1)
                act.wait_ge(o_up, b + 1)
                wait(act, y_up, b - 1)
                act.activation(oT[u][:, :], ps_o[:, :], ACT.Copy).then_inc(oT_up, 1)
            pairs(act, body)

        @block.vector
        def _(dve):
            def stepper(sem, steps, b):
                step = [0]

                def then(ins):
                    step[0] += 1
                    ins.then_inc(sem, 1)
                    dve.wait_ge(sem, steps * b + step[0])
                return then

            def indices(b, u):
                wait(dve, gat[u], 64 * (b - u))
                dve.tensor_copy(idx[u][:, :, :], route_i[:, bass.ds(b, 1), :, :].rearrange("p o n t -> p (o n) t")).then_inc(idx_up, 1)

            def round_(b, u, i, first=True, second=True, more=True):
                then, then2 = stepper(vf, NF, b), stepper(vb, NB, b - 1)
                c, cu, ci = b - 1, 1 - u, i - 1 + u

                def faded(j):
                    dve.wait_ge(a_up, 4 * c + j + 1)
                    if j < 2:
                        wait(dve, o_up, c)
                    else:
                        dve.wait_ge(at_free, 2 * c + j - 1)
                    dve.tensor_tensor(aT[j % 2][:, 0:S - j * P], ps_a[j % 2][:, 0:S - j * P], fade[:, 0:S - j * P], ALU.mult).then_inc(at_up, 1)

                if first:
                    rw = route_w[:, bass.ds(b, 1), :, :]
                    dve.tensor_scalar(wt[u][:, 0, :], rw[:, :, 2, :].rearrange("p o t -> p (o t)"), -1.0, 2.0, ALU.mult, ALU.add)
                    dve.tensor_copy(wt[u][:, 1, :], rw[:, :, 2, :].rearrange("p o t -> p (o t)"))
                    then(dve.tensor_copy(wt[u][:, 2:4, :], rw[:, :, 0:2, :].rearrange("p o n t -> p (o n) t")))
                    dve.wait_ge(ld[u], 32 * i + 32)
                    for t in range(T):
                        ins = dve.tensor_scalar(z[:, t, :], x_in[u][:, t, :], wt[u][:, 0, t:t + 1], None, ALU.mult)
                    then(ins)
                    dve.wait_ge(gat[u], 128 * i + 128)
                    for n, src in ((1, fb[u]), (2, rows[u][:, 0, :, :]), (3, rows[u][:, 1, :, :])):
                        for t in range(T):
                            ins = dve.scalar_tensor_tensor(z[:, t, :], src[:, t, :], wt[u][:, n, t:t + 1], z[:, t, :], ALU.mult, ALU.add)
                        if n < 3:
                            then(ins)
                        else:
                            ins.then_inc(z_up, 1)
                    if more:
                        indices(b + 2, u)
                if second:
                    dve.wait_ge(g_up, c + 1)
                    then2(dve.tensor_tensor(g2[:, :], g[:, :], g[:, :], ALU.mult))
                    wait(dve, o_up, c)
                    dve.tensor_tensor(gv[:, :, 0:M], ps_v[:, :, 0:M], col(g2[:, :]).to_broadcast([P, T, M]), ALU.mult).then_inc(gv_up, 1)
                    faded(0)
                    faded(1)
                if first:
                    dve.wait_ge(z_up, b + 1)
                    for t in range(T):
                        ins = dve.bn_stats(st6[:, t, :], z[:, t, :])
                    ins.then_inc(vf, 1)
                if second:
                    faded(2)
                if first:
                    dve.wait_ge(vf, NF * b + 5)
                    apart(dve, past_dve)
                    for t in range(T):
                        ins = dve.bn_aggr(mv[:, t, :], st6[:, t, :])
                    ins.then_inc(vf, 1)
                if second:
                    faded(3)
                if first:
                    dve.wait_ge(vf, NF * b + 6)
                    dve.tensor_scalar(ve[:, :], mv[:, :, 1], 1e-5, None, ALU.add).then_inc(var_up, 1)
                    dve.wait_ge(rstd_up, b + 1)
                    normalized(dve, x3[u], z, mv, rstd).then_inc(x3_up, 1)
                if second:
                    dve.wait_ge(y_up, c + 1)
                    dve.wait_ge(xb_up, c + 1)
                    dve.tensor_tensor(z2[:, :, :], ps_y[:, :, :], x3b[cu][:, :, :], ALU.add).then_inc(z2_up, 1)
                    dve.wait_ge(z2_up, c + 1)
                    moments(dve, then2, z2, st6b, mvb, veb, past_dve).then_inc(varb_up, 1)
                    dve.wait_ge(rstdb_up, c + 1)
                    wait(dve, st[cu], 16 * ci)
                    normalized(dve, x4[cu], z2, mvb, rstdb).then_inc(x4_up, 1)

            indices(0, 0)
            indices(1, 1)
            dve.wait_ge(fade_up, 1)
            dve.tensor_scalar(decay[:, 0:1], sg[:, :], 0.999 - 0.9, 0.9, ALU.mult, ALU.add).then_inc(fade_up, 1)
            round_(0, 0, 0, second=False)
            dve.wait_ge(fade_up, 3)
            for n in range(FADE):
                dve.tensor_tensor(decay[:, n + 1:n + 2], decay[:, n:n + 1], decay[:, n:n + 1], ALU.mult).then_inc(grown, 1)
                dve.tensor_scalar(fade[:, 1 << n:2 << n], fade[:, 0:1 << n], decay[:, n:n + 1], None, ALU.mult).then_inc(grown, 1)
                dve.wait_ge(grown, 2 * n + 2)
            dve.wait_ge(fade_up, 4)
            dve.wait_ge(const_up, 6)
            round_(1, 1, 0)
            with dve.Fori(1, B // 2 - 1) as i:
                for u in range(2):
                    round_(2 * i + u, u, i)
            for u in range(2):
                round_(B - 2 + u, u, B // 2 - 1, more=False)
            round_(B, 0, B // 2, first=False)

        @block.tensor
        def _(pe):
            pe.wait_ge(const_up, 6)
            pe.wait_ge(c_ld, 128)

            def body(b, u, i):
                pe.wait_ge(x3_up, b + 1)
                for h in range(DH):
                    for t in range(T):
                        ins = pe.transpose(ps_t[:, h, t * P:(t + 1) * P], x3[u][:, t, h * P:(h + 1) * P], ident[:, :])
                ins.then_inc(t_up, 1)
                pe.wait_ge(xT_up, b + 1)
                wait(pe, at_up, 4 * b)
                for n, w in enumerate((wq, wk)):
                    for h in range(DH):
                        ins = pe.matmul(ps_a[n][:, :], w[:, h, :], x3T[u][:, h, :], start=(h == 0), stop=(h == DH - 1))
                    ins.then_inc(q_up, 1)
                wait(pe, gv_up, b)
                for t in range(T):
                    for h in range(DH):
                        ins = pe.matmul(ps_v[:, t, 0:M + 2], x3T[u][:, h, t * P:(t + 1) * P], wv[:, h, :], start=(h == 0), stop=(h == DH - 1))
                ins.then_inc(v_up, 1)
                pe.wait_ge(qk_s, 2 * b + 2)

                def scores(j):
                    pe.matmul(ps_a[j % 2][:, 0:S - j * P], kT[u][:, j * P:(j + 1) * P], qT[u][:, j * P:S], start=True, stop=True).then_inc(a_up, 1)

                def reading(j):
                    pe.wait_ge(at_up, 4 * b + j + 1)
                    if j == 0:
                        pe.wait_ge(gv_up, b + 1)
                        wait(pe, oT_up, b)
                    ins = pe.matmul(ps_o[:, j * P:S], gv[:, j, :], aT[j % 2][:, 0:S - j * P], start=(j == 0), stop=(j == T - 1))
                    ins.then_inc(at_free if j < 2 else o_up, 1) if j != 2 else None

                scores(0)
                scores(1)
                for j in range(T):
                    reading(j)
                    if j < 2:
                        scores(j + 2)
                pe.wait_ge(oT_up, b + 1)
                wait(pe, z2_up, b)
                for t in range(T):
                    ins = pe.matmul(ps_y[:, t, :], oT[u][:, t * P:(t + 1) * P], wo[:, :], start=True, stop=True)
                ins.then_inc(y_up, 1)
            pairs(pe, body)


def stage_xattn1(nc, a):
    MASKED = -1.0e9
    with ExitStack() as ctx:
        r = Room(nc, ctx, "xb")
        x_in, xb = ([r.sb(f"{n}{u}", [P, T, D]) for u in range(2)] for n in ("x", "xb"))
        cT = [r.sb(f"cT{u}", [P, DH, S]) for u in range(2)]
        mask = [r.sb(f"mask{u}", [P, T, S], U8) for u in range(2)]
        wq, wk, wv, woT = (r.sb(n, [P, DH, D]) for n in ("wq", "wk", "wv", "woT"))
        wqk, wvo = r.sb("wqk", [P, DH, D]), r.sb("wvo", [P, DH, D])
        bq, bk, bv = (r.sb(n, [P, DH]) for n in ("bq", "bk", "bv"))
        bqw, bvw = r.sb("bqw", [P, DH, P]), r.sb("bvw", [P, DH, P])
        g_bias, cq_w = r.sb("g_bias", [P, DH]), r.sb("cq_w", [P, DH, 2])
        cq_b, v_bias, bo = r.sb("cq_b", [P, 1]), r.sb("v_bias", [P, D]), r.sb("bo", [P, D])
        xT, gT = ([r.sb(f"{n}{u}", [P, DH, S]) for u in range(2)] for n in ("xT", "gT"))
        v = [r.sb(f"v{u}", [P, T, D]) for u in range(2)]
        cq = [r.sb(f"cq{u}", [P, T]) for u in range(2)]
        s = [r.sb(f"s{j}", [P, S]) for j in range(2)]
        ex = [r.sb(f"ex{j}", [P, S]) for j in range(2)]
        exT = [r.sb(f"exT{j}", [P, T, P]) for j in range(2)]
        nmax, rsum, rinv = ([r.sb(f"{n}{j}", [P, 1]) for j in range(2)] for n in ("nmax", "rsum", "rinv"))
        masked = r.sb("masked", [P, S])
        z = r.sb("z", [P, T, D])
        st6, mv = r.sb("st6", [P, T, 6]), r.sb("mv", [P, T, 2])
        ve, rstd, mhalf = (r.sb(n, [P, T]) for n in ("ve", "rstd", "mhalf"))
        x5 = [r.sb(f"x5{u}", [P, T, D]) for u in range(2)]
        ident = r.sb("ident", [P, P])
        ps_x = r.ps("ps_x", [P, DH, S])
        ps_s = [r.ps(f"ps_s{j}", [P, S]) for j in range(2)]
        ps_t = r.ps("ps_t", [P, T, P])
        ps_o = r.ps("ps_o", [P, D])
        ps_v = r.ps("ps_v", [P, 2, D])
        ps_q = r.ps("ps_q", [P, T, 2])
        c_ld, const_up, w_up, wc, past_dve, past_sp = (r.sem(n) for n in ("c_ld", "const_up", "w_up", "wc", "past_dve", "past_sp"))
        ld, st = ([r.sem(f"{n}{u}") for u in range(2)] for n in ("ld", "st"))
        t_up, xT_up, g_up, gT_up, v_up, v_s, cq_up, cq_s = (r.sem(n) for n in ("t_up", "xT_up", "g_up", "gT_up", "v_up", "v_s", "cq_up", "cq_s"))
        s_up, s_s, s_m, max_up, exp_up, et_up, eT_up, o_up, rinv_up, z_up = (r.sem(n) for n in
            ("s_up", "s_s", "s_m", "max_up", "exp_up", "et_up", "eT_up", "o_up", "rinv_up", "z_up"))
        xb_up, steps, var_up, rstd_up, x5_up = (r.sem(n) for n in ("xb_up", "steps", "var_up", "rstd_up", "x5_up"))
        block = ctx.enter_context(nc.Block())

        def batches(eng, body):
            body(0, 0, 0, True)
            body(1, 1, 0, True)
            with eng.Fori(1, B // 2 - 1) as i:
                for u in range(2):
                    body(2 * i + u, u, i, True)
            body(B - 2, 0, B // 2 - 1, True)
            body(B - 1, 1, B // 2 - 1, False)

        @block.sync
        def _(sp):
            for w, n in ((wq, "Wq"), (wk, "Wk"), (wv, "Wv"), (woT, "WoT")):
                sp.dma_start(w[:, :, :], a[f"L1_xattn_{n}"].rearrange("(h p) n -> p h n", p=P)).then_inc(c_ld, 16)
            with nc.allow_non_contiguous_dma(reason="256 biases"):
                for w, n in ((bq, "bq"), (bk, "bk"), (bv, "bv")):
                    sp.dma_start(w[:, :], a[f"L1_xattn_{n}"].rearrange("(h p) -> p h", p=P)).then_inc(c_ld, 16)
            sp.dma_start(bo[:, :], row_bc(a["L1_xattn_bo"], P)).then_inc(c_ld, 16)

            def load(b, u):
                sp.dma_start(x_in[u][:, :, :], tok(a["x4"][b])).then_inc(ld[u], 16)
                sp.dma_start(cT[u][:, :, :], a["ctxT"][b].rearrange("(h p) s -> p h s", p=P)).then_inc(ld[u], 16)
                sp.dma_start(mask[u][:, :, :], a["mask"][b].rearrange("(t p) s -> p t s", p=P)).then_inc(ld[u], 16)

            def store(b, u):
                sp.wait_ge(x5_up, b + 1)
                sp.dma_start(tok(a["x5"][b]), x5[u][:, :, :]).then_inc(st[u], 16)

            for u in range(2):
                load(u, u)
            with sp.Fori(0, B // 2 - 1) as i:
                for u in range(2):
                    b = 2 * i + u
                    sp.wait_ge(s_m, T * b + T)
                    apart(sp, past_sp)
                    sp.wait_ge(t_up, b + 1)
                    sp.wait_ge(xb_up, b + 1)
                    load(b + 2, u)
                    store(b, u)
            for u in range(2):
                store(B - 2 + u, u)
            for u in range(2):
                sp.wait_ge(st[u], 16 * B // 2)

        @block.gpsimd
        def _(pool):
            pool.memset(mhalf[:, :], -0.5).then_inc(const_up, 1)
            pool.memset(masked[:, :], MASKED).then_inc(const_up, 1)
            pool.memset(ident[:, :], 0.0).then_inc(const_up, 1)
            pool.wait_ge(const_up, 3)
            pool.affine_select(out=ident[:, :], in_=ident[:, :], compare_op=ALU.not_equal, fill=1.0, base=0,
                               pattern=[[-1, P]], channel_multiplier=1).then_inc(const_up, 1)
            pool.wait_ge(c_ld, 128)
            pool.tensor_copy(bqw[:, :, :], col(bq[:, :]).to_broadcast([P, DH, P])).then_inc(wc, 1)
            pool.tensor_copy(bvw[:, :, :], col(bv[:, :]).to_broadcast([P, DH, P])).then_inc(wc, 1)

            def residual(b, u, i):
                pool.wait_ge(ld[u], 48 * i + 48)
                wait(pool, z_up, T * (b - 1))
                pool.tensor_tensor(xb[u][:, :, :], x_in[u][:, :, :], row(bo[:, :]).to_broadcast([P, T, D]), ALU.add).then_inc(xb_up, 1)

            def root(b):
                pool.wait_ge(var_up, b + 1)
                pool.tensor_tensor(rstd[:, :], ve[:, :], mhalf[:, :], ALU.pow).then_inc(rstd_up, 1)

            def body(b, u, i, more):
                residual(b, u, i)
                if not isinstance(b, int) or b > 0:
                    root(b - 1)
            batches(pool, body)
            root(B - 1)

        @block.scalar
        def _(act):
            act.wait_ge(w_up, 1)
            for h in range(DH):
                ins = act.activation(wqk[:, h, :], ps_x[:, h, 0:D], ACT.Copy)
                ins = act.activation(wvo[:, h, :], ps_x[:, h, D:2 * D], ACT.Copy)
            act.activation(v_bias[:, :], ps_v[:, 0, :], ACT.Copy)
            act.activation(g_bias[:, :], ps_q[:, 0, :], ACT.Copy)
            act.activation(cq_w[:, :, 0], ps_q[:, 1, :], ACT.Copy)
            act.activation(cq_w[:, :, 1], ps_q[:, 1, :], ACT.Copy)
            act.activation(cq_b[:, :], ps_q[:, 2, 0:1], ACT.Copy).then_inc(wc, 1)
            act.wait_ge(wc, 3)

            def turned(b, u):
                act.wait_ge(t_up, b + 1)
                wait(act, g_up, b - 1)
                wait(act, cq_up, b - 1)
                act.activation(xT[u][:, :, :], ps_x[:, :, :], ACT.Copy).then_inc(xT_up, 1)

            def side(b, u):
                act.wait_ge(cq_up, b + 1)
                wait(act, s_s, T * (b - 1))
                act.activation(cq[u][:, :], ps_q[:, :, 0], ACT.Identity, bias=cq_b[:, 0:1]).then_inc(cq_s, 1)
                act.wait_ge(g_up, b + 1)
                for h in range(DH):
                    ins = act.activation(gT[u][:, h, :], ps_x[:, h, :], ACT.Identity, bias=g_bias[:, h:h + 1])
                ins.then_inc(gT_up, 1)

            turned(0, 0)
            side(0, 0)
            act.wait_ge(cq_s, 1)

            def body(b, u, i, more):
                for t in range(T):
                    n, j = T * b + t, t % 2
                    if more and t == 3:
                        side(b + 1, 1 - u)
                        act.wait_ge(cq_s, b + 2)
                    act.wait_ge(s_up, n + 1)
                    wait(act, exp_up, n - 1)
                    act.activation(s[j][:, :], ps_s[j][:, :], ACT.Identity, bias=cq[u][:, t:t + 1]).then_inc(s_s, 1)
                    if more and t == 1:
                        turned(b + 1, 1 - u)
                    act.wait_ge(max_up, n + 1)
                    wait(act, et_up, n - 1)
                    wait(act, rinv_up, n - 1)
                    act.activation(ex[j][:, :], s[j][:, :], ACT.Exp, bias=nmax[j][:, 0:1], accum_out=rsum[j][:, 0:1]).then_inc(exp_up, 1)
            batches(act, body)

        @block.vector
        def _(dve):
            dve.wait_ge(wc, 3)

            def values(b, u, half):
                dve.wait_ge(v_up, 2 * b + half + 1)
                if half == 0:
                    wait(dve, o_up, T * (b - 1))
                dve.tensor_tensor(v[u][:, 2 * half:2 * half + 2, :], ps_v[:, :, :], row(v_bias[:, :]).to_broadcast([P, 2, D]), ALU.add).then_inc(v_s, 1)

            def exps(n, j, real=True):
                dve.wait_ge(et_up, n + 1)
                wait(dve, o_up, n - 1)
                dve.tensor_copy(exT[j][:, :, :], ps_t[:, :, :]).then_inc(eT_up, 1)

            def out(n, b, t, j, u):
                dve.wait_ge(exp_up, n + 1)
                dve.wait_ge(o_up, n + 1)
                dve.reciprocal(rinv[j][:, :], rsum[j][:, :]).then_inc(rinv_up, 1)
                dve.wait_ge(rinv_up, n + 1)
                dve.wait_ge(xb_up, b + 1)
                dve.scalar_tensor_tensor(z[:, t, :], ps_o[:, :], rinv[j][:, 0:1], xb[u][:, t, :], ALU.mult, ALU.add).then_inc(z_up, 1)

            def norm(b, u, i):
                def then(ins):
                    then.n += 1
                    ins.then_inc(steps, 1)
                    dve.wait_ge(steps, 2 * b + then.n)
                then.n = 0
                dve.wait_ge(z_up, T * b + T)
                moments(dve, then, z, st6, mv, ve, past_dve).then_inc(var_up, 1)

            def finish(b, u, i):
                dve.wait_ge(rstd_up, b + 1)
                wait(dve, st[u], 16 * i)
                normalized(dve, x5[u], z, mv, rstd).then_inc(x5_up, 1)

            values(0, 0, 0)
            values(0, 0, 1)

            def body(b, u, i, more):
                before = not isinstance(b, int) or b > 0
                pb, pu, pi = b - 1, 1 - u, i - 1 + u
                for t in range(T):
                    n, j = T * b + t, t % 2
                    dve.wait_ge(s_s, n + 1)
                    apart(dve, past_dve)
                    dve.copy_predicated(s[j][:, :], mask[u][:, t, :], masked[:, :]).then_inc(s_m, 1)
                    dve.wait_ge(s_m, n + 1)
                    dve.tensor_reduce(nmax[j][:, :], s[j][:, :], AX.X, ALU.max, negate=True).then_inc(max_up, 1)
                    if t > 0 or before:
                        exps(n - 1, 1 - j)
                    if t == 2 and before:
                        finish(pb, pu, pi)
                    if t >= 2:
                        out(n - 2, b, t - 2, j, u)
                    elif before:
                        out(n - 2, pb, t + 2, j, pu)
                    if t == 1 and before:
                        norm(pb, pu, pi)
                    if more and t >= 2:
                        values(b + 1, 1 - u, t - 2)
            batches(dve, body)
            exps(T * B - 1, 1)
            out(T * B - 2, B - 1, 2, 0, 1)
            out(T * B - 1, B - 1, 3, 1, 1)
            norm(B - 1, 1, B // 2 - 1)
            finish(B - 1, 1, B // 2 - 1)

        @block.tensor
        def _(pe):
            pe.wait_ge(const_up, 4)
            pe.wait_ge(wc, 2)
            for m in range(DH):
                for c, (lw, rw_) in enumerate(((wq, wk), (wv, woT))):
                    for h in range(DH):
                        pe.matmul(ps_x[:, m, c * D:(c + 1) * D], lw[:, h, m * P:(m + 1) * P], rw_[:, h, :], start=(h == 0), stop=(h == DH - 1))
                for c, (lw, rb_) in enumerate(((wk, bq), (wq, bk))):
                    for h in range(DH):
                        pe.matmul(ps_q[:, c, m:m + 1], lw[:, h, m * P:(m + 1) * P], rb_[:, h:h + 1], start=(h == 0), stop=(h == DH - 1))
            for h in range(DH):
                pe.matmul(ps_v[:, 0, :], bvw[:, h, :], woT[:, h, :], start=(h == 0), stop=(h == DH - 1))
            for h in range(DH):
                ins = pe.matmul(ps_q[:, 2, 0:1], bqw[:, h, :], bk[:, h:h + 1], start=(h == 0), stop=(h == DH - 1))
            ins.then_inc(w_up, 1)
            pe.wait_ge(wc, 3)

            def turn(b, u, i):
                pe.wait_ge(ld[u], 48 * i + 48)
                wait(pe, gT_up, b)
                for h in range(DH):
                    for t in range(T):
                        ins = pe.transpose(ps_x[:, h, t * P:(t + 1) * P], x_in[u][:, t, h * P:(h + 1) * P], ident[:, :])
                ins.then_inc(t_up, 1)

            def side(b, u):
                pe.wait_ge(xT_up, b + 1)
                wait(pe, cq_s, b)
                for t in range(T):
                    for h in range(DH):
                        ins = pe.matmul(ps_q[:, t, :], xT[u][:, h, t * P:(t + 1) * P], cq_w[:, h, :], start=(h == 0), stop=(h == DH - 1))
                ins.then_inc(cq_up, 1)
                for m in range(DH):
                    for h in range(DH):
                        ins = pe.matmul(ps_x[:, m, :], wqk[:, h, m * P:(m + 1) * P], xT[u][:, h, :], start=(h == 0), stop=(h == DH - 1))
                ins.then_inc(g_up, 1)

            def values(b, u, half):
                wait(pe, v_s, 2 * b + half)
                for t in range(2):
                    for h in range(DH):
                        ins = pe.matmul(ps_v[:, t, :], cT[u][:, h, (2 * half + t) * P:(2 * half + t + 1) * P], wvo[:, h, :],
                                        start=(h == 0), stop=(h == DH - 1))
                ins.then_inc(v_up, 1)

            def turn_exps(n, j):
                pe.wait_ge(exp_up, n + 1)
                wait(pe, eT_up, n)
                for k in range(T):
                    ins = pe.transpose(ps_t[:, k, :], ex[j][:, k * P:(k + 1) * P], ident[:, :])
                ins.then_inc(et_up, 1)

            def out(n, j, u):
                pe.wait_ge(eT_up, n + 1)
                wait(pe, z_up, n)
                for k in range(T):
                    ins = pe.matmul(ps_o[:, :], exT[j][:, k, :], v[u][:, k, :], start=(k == 0), stop=(k == T - 1))
                ins.then_inc(o_up, 1)

            turn(0, 0, 0)
            side(0, 0)
            values(0, 0, 0)
            values(0, 0, 1)

            def body(b, u, i, more):
                before = not isinstance(b, int) or b > 0
                for t in range(T):
                    n, j = T * b + t, t % 2
                    if t == 0:
                        pe.wait_ge(gT_up, b + 1)
                        pe.wait_ge(v_s, 2 * b + 2)
                    wait(pe, s_s, n - 1)
                    for h in range(DH):
                        ins = pe.matmul(ps_s[j][:, :], gT[u][:, h, t * P:(t + 1) * P], cT[u][:, h, :], start=(h == 0), stop=(h == DH - 1))
                    ins.then_inc(s_up, 1)
                    if more and t == 1:
                        turn(b + 1, 1 - u, i + u)
                    if more and t == 2:
                        side(b + 1, 1 - u)
                        values(b + 1, 1 - u, 0)
                    if more and t == 3:
                        values(b + 1, 1 - u, 1)
                    if t > 0 or before:
                        turn_exps(n - 1, 1 - j)
                    if t >= 2:
                        out(n - 2, j, u)
                    elif before:
                        out(n - 2, j, 1 - u)
            batches(pe, body)
            turn_exps(T * B - 1, 1)
            out(T * B - 2, 0, 1)
            out(T * B - 1, 1, 1)


def stage_gated(nc, a):
    THRESHOLD = 0.1
    NV = 9
    with ExitStack() as ctx:
        r = Room(nc, ctx, "ga")
        x_in = [r.sb(f"x{u}", [P, T, D]) for u in range(2)]
        xT = [r.sb(f"xT{u}", [P, DH, S]) for u in range(2)]
        ew = r.sb("ew", [P, DH, E, D])
        eb = r.sb("eb", [E, D])
        gw = r.sb("gw", [P, DH, E])
        gb = r.sb("gb", [P, E])
        lg, ex, pr = (r.sb(n, [P, T, E]) for n in ("lg", "ex", "pr"))
        mx, sm, rs, ws, wz, wr = (r.sb(n, [P, T]) for n in ("mx", "sm", "rs", "ws", "wz", "wr"))
        gate = [r.sb(f"gate{u}", [P, T, E]) for u in range(2)]
        gateT = [r.sb(f"gateT{u}", [E, T, P]) for u in range(2)]
        acc = [r.sb(f"acc{j}", [P, T, D]) for j in range(2)]
        st6, mv = r.sb("st6", [P, T, 6]), r.sb("mv", [P, T, 2])
        ve, rstd, mhalf = (r.sb(n, [P, T]) for n in ("ve", "rstd", "mhalf"))
        out = [r.sb(f"out{u}", [P, T, D]) for u in range(2)]
        ident = r.sb("ident", [P, P])
        ps_t = r.ps("ps_t", [P, DH, S])
        ps_l = r.ps("ps_l", [P, T, E])
        ps_g = ps_t[0:E, 0, :].rearrange("e (t q) -> e t q", t=T)
        ps_e = [r.ps(f"ps_e{j}", [P, 2, D]) for j in range(E // 2)]
        ps_b = r.ps("ps_b", [P, D])
        c_ld, ew_ld, const_up, v, past_dve = (r.sem(n) for n in ("c_ld", "ew_ld", "const_up", "v", "past_dve"))
        ld, st = ([r.sem(f"{n}{u}") for u in range(2)] for n in ("ld", "st"))
        t_up, xT_up, lg_up, ex_up, gate_up, gt_up, gT_up, e_up, e_free, b_up, acc_up, var_up, rstd_up, out_up, steps, wr_up = (r.sem(n) for n in
            ("t_up", "xT_up", "lg_up", "ex_up", "gate_up", "gt_up", "gT_up", "e_up", "e_free", "b_up", "acc_up", "var_up", "rstd_up", "out_up", "steps", "wr_up"))
        block = ctx.enter_context(nc.Block())
        PAIRS = E // 2

        def batches(eng, body):
            body(0, 0, 0, True)
            body(1, 1, 0, True)
            with eng.Fori(1, B // 2 - 1) as i:
                for u in range(2):
                    body(2 * i + u, u, i, True)
            body(B - 2, 0, B // 2 - 1, True)
            body(B - 1, 1, B // 2 - 1, False)

        @block.sync
        def _(sp):
            for u in range(2):
                sp.dma_start(x_in[u][:, :, :], tok(a["x5"][u])).then_inc(ld[u], 16)
            sp.dma_start(gw[:, :, :], a["L1_ffn_gate_w"].rearrange("(h p) e -> p h e", p=P)).then_inc(c_ld, 16)
            sp.dma_start(gb[:, :], row_bc(a["L1_ffn_gate_b"], P)).then_inc(c_ld, 16)
            sp.dma_start(eb[:, :], a["L1_ffn_expert_b"]).then_inc(c_ld, 16)
            for e in range(E):
                sp.dma_start(ew[:, :, e, :], a["L1_ffn_expert_w"][e].rearrange("(h p) n -> p h n", p=P)).then_inc(ew_ld, 16)

            def store(b, u):
                sp.wait_ge(out_up, b + 1)
                sp.dma_start(tok(a["out"][b]), out[u][:, :, :]).then_inc(st[u], 16)

            with sp.Fori(0, B // 2 - 1) as i:
                for u in range(2):
                    store(2 * i + u, u)
                    sp.dma_start(x_in[u][:, :, :], tok(a["x5"][2 * i + u + 2])).then_inc(ld[u], 16)
            for u in range(2):
                store(B - 2 + u, u)
            for u in range(2):
                sp.wait_ge(st[u], 16 * B // 2)

        @block.gpsimd
        def _(pool):
            pool.memset(mhalf[:, :], -0.5).then_inc(const_up, 1)
            pool.memset(ident[:, :], 0.0).then_inc(const_up, 1)
            pool.wait_ge(const_up, 2)
            pool.affine_select(out=ident[:, :], in_=ident[:, :], compare_op=ALU.not_equal, fill=1.0, base=0,
                               pattern=[[-1, P]], channel_multiplier=1).then_inc(const_up, 1)

            def body(b, u, i, more):
                pool.wait_ge(var_up, b + 1)
                pool.tensor_tensor(rstd[:, :], ve[:, :], mhalf[:, :], ALU.pow).then_inc(rstd_up, 1)
            batches(pool, body)

        @block.scalar
        def _(act):
            def prepare(b, u):
                act.wait_ge(t_up, b + 1)
                wait(act, e_up, T * PAIRS * (b - 1))
                act.activation(xT[u][:, :, :], ps_t[:, :, :], ACT.Copy).then_inc(xT_up, 1)
                act.wait_ge(v, NV * b + 3)
                act.activation(ex[:, :, :], lg[:, :, :], ACT.Exp).then_inc(ex_up, 1)
                act.wait_ge(gt_up, b + 1)
                wait(act, b_up, T * (b - 1))
                act.activation(gateT[u][:, :, :], ps_g, ACT.Copy).then_inc(gT_up, 1)
            prepare(0, 0)

            def body(b, u, i, more):
                if more:
                    prepare(b + 1, 1 - u)
            batches(act, body)

        @block.vector
        def _(dve):
            dve.wait_ge(c_ld, 16 * 3)
            dve.wait_ge(const_up, 3)

            def prepare(b, u):
                step = [0]

                def then(ins):
                    step[0] += 1
                    ins.then_inc(v, 1)
                    dve.wait_ge(v, NV * b + step[0])

                def bc(ap):
                    return col(ap).to_broadcast([P, T, E])

                dve.wait_ge(lg_up, b + 1)
                then(dve.tensor_tensor(lg[:, :, :], ps_l[:, :, :], row(gb[:, :]).to_broadcast([P, T, E]), ALU.add))
                then(dve.tensor_reduce(mx[:, :], lg[:, :, :], AX.X, ALU.max))
                then(dve.tensor_tensor(lg[:, :, :], lg[:, :, :], bc(mx[:, :]), ALU.subtract))
                dve.wait_ge(ex_up, b + 1)
                then(dve.tensor_reduce(sm[:, :], ex[:, :, :], AX.X, ALU.add))
                then(dve.reciprocal(rs[:, :], sm[:, :]))
                then(dve.tensor_tensor(pr[:, :, :], ex[:, :, :], bc(rs[:, :]), ALU.mult))
                then(dve.scalar_tensor_tensor(pr[:, :, :], pr[:, :, :], THRESHOLD, pr[:, :, :], ALU.is_ge, ALU.mult))
                then(dve.tensor_reduce(ws[:, :], pr[:, :, :], AX.X, ALU.add))
                then(dve.scalar_tensor_tensor(wz[:, :], ws[:, :], 0.0, ws[:, :], ALU.is_equal, ALU.add))
                assert step[0] == NV
                dve.reciprocal(wr[:, :], wz[:, :]).then_inc(wr_up, 1)
                dve.wait_ge(wr_up, b + 1)
                wait(dve, gt_up, b - 1)
                dve.tensor_tensor(gate[u][:, :, :], pr[:, :, :], bc(wr[:, :]), ALU.mult).then_inc(gate_up, 1)

            prepare(0, 0)

            def body(b, u, i, more):
                wait(dve, out_up, b)
                for t in range(T):
                    dve.wait_ge(b_up, T * b + t + 1)
                    if t == 0:
                        dve.wait_ge(gate_up, b + 1)
                    acc_n = (E + 1) * (T * b + t)
                    dve.tensor_tensor(acc[0][:, t, :], ps_b[:, :], x_in[u][:, t, :], ALU.add).then_inc(acc_up, 1)
                    for e in range(E):
                        if e % 2 == 0:
                            dve.wait_ge(e_up, PAIRS * (T * b + t) + e // 2 + 1)
                        dve.wait_ge(acc_up, acc_n + e + 1)
                        ins = dve.scalar_tensor_tensor(acc[(e + 1) % 2][:, t, :], ps_e[e // 2][:, e % 2, :],
                                                       gate[u][:, t, e:e + 1], acc[e % 2][:, t, :], ALU.mult, ALU.add)
                        ins.then_inc(acc_up, 1)
                    if more and t == 1:
                        prepare(b + 1, 1 - u)

                def then(ins):
                    then.n += 1
                    ins.then_inc(steps, 1)
                    dve.wait_ge(steps, 2 * b + then.n)
                then.n = 0
                dve.wait_ge(acc_up, (E + 1) * T * (b + 1))
                moments(dve, then, acc[0], st6, mv, ve, past_dve).then_inc(var_up, 1)
                dve.wait_ge(rstd_up, b + 1)
                wait(dve, st[u], 16 * i)
                normalized(dve, out[u], acc[0], mv, rstd).then_inc(out_up, 1)
            batches(dve, body)

        @block.tensor
        def _(pe):
            pe.wait_ge(const_up, 3)
            pe.wait_ge(c_ld, 48)

            def turn(b, u, i):
                pe.wait_ge(ld[u], 16 * i + 16)
                wait(pe, xT_up, b)
                wait(pe, gT_up, b)
                for h in range(DH):
                    for t in range(T):
                        ins = pe.transpose(ps_t[:, h, t * P:(t + 1) * P], x_in[u][:, t, h * P:(h + 1) * P], ident[:, :])
                ins.then_inc(t_up, 1)

            def logits(b, u):
                pe.wait_ge(xT_up, b + 1)
                for t in range(T):
                    for h in range(DH):
                        ins = pe.matmul(ps_l[:, t, :], xT[u][:, h, t * P:(t + 1) * P], gw[:, h, :], start=(h == 0), stop=(h == DH - 1))
                ins.then_inc(lg_up, 1)

            def turn_gates(b, u):
                pe.wait_ge(gate_up, b + 1)
                wait(pe, gT_up, b)
                for t in range(T):
                    ins = pe.transpose(ps_g[:, t, :], gate[u][:, t, :], ident[:, :])
                ins.then_inc(gt_up, 1)

            turn(0, 0, 0)
            logits(0, 0)
            turn_gates(0, 0)
            pe.wait_ge(ew_ld, 16 * E)

            def body(b, u, i, more):
                pe.wait_ge(gT_up, b + 1)
                for t in range(T):
                    n = T * b + t
                    wait(pe, acc_up, (E + 1) * (n - 1) + 1)
                    pe.matmul(ps_b[:, :], gateT[u][:, t, :], eb[:, :], start=True, stop=True).then_inc(b_up, 1)
                    for e in range(0, E, 2):
                        wait(pe, acc_up, (E + 1) * (n - 1) + e + 3)
                        for h in range(DH):
                            ins = pe.matmul(ps_e[e // 2][:, :, :].rearrange("p e d -> p (e d)"), xT[u][:, h, t * P:(t + 1) * P],
                                            ew[:, h, e:e + 2, :].rearrange("p e d -> p (e d)"), start=(h == 0), stop=(h == DH - 1))
                        ins.then_inc(e_up, 1)
                        if more and (t, e) == (1, 2):
                            turn(b + 1, 1 - u, i + u)
                        if more and (t, e) == (1, 6):
                            logits(b + 1, 1 - u)
                        if more and (t, e) == (3, 4):
                            turn_gates(b + 1, 1 - u)
            batches(pe, body)


def decoder(nc, a):
    def scratch(name, shape, dt=F32):
        a[name] = nc.dram_tensor(f"scratch_{name}", shape, dt, kind="Internal").ap()

    for name in ("x1", "x2", "x4", "x5", "v", "fallback"):
        scratch(name, (B, S, D))
    scratch("qk_parts", (B, 2, PARTS, D, S), BF16)
    scratch("buf", (E * CAP, D))
    scratch("results", (E * CAP, D))
    with ExitStack() as ctx:
        w_all = ctx.enter_context(nc.sbuf_tensor("w_all", [P, B, DH, 3 * D], F32))
        x_all = ctx.enter_context(nc.sbuf_tensor("x_all", [P, B, T, D], F32))
        inv_all = ctx.enter_context(nc.sbuf_tensor("inv_all", [P, B, T], F32))
        stage_mix(nc, a, x_all, inv_all, w_all)
        stage_rec(nc, a, x_all, inv_all, w_all)
    stage_proj(nc, a)
    stage_xattn0(nc, a)
    with ExitStack() as ctx:
        route_w = ctx.enter_context(nc.sbuf_tensor("route_w", [P, B, 3, T], F32))
        route_i = ctx.enter_context(nc.sbuf_tensor("route_i", [P, B, 2, T], U32))
        stage_route(nc, a, route_w, route_i)
        stage_experts(nc, a)
        stage_memory(nc, a, route_w, route_i)
    stage_xattn1(nc, a)
    stage_gated(nc, a)


def kernel(**inputs):
    import numpy as _np
    import concourse.bacc as _bacc
    from concourse import mybir as _mybir
    from concourse.bass_utils import run_bass_kernel_spmd as _run

    given = {name: _np.asarray(value) for name, value in inputs.items()}
    turned = ("L0_xattn_Wq", "L0_xattn_Wk", "L0_xattn_Wv", "L1_xattn_Wo")
    as_given = ("x", "L0_attn_norm_weight", "L0_attn_router_b",
                "L0_xattn_bq", "L0_xattn_bk", "L0_xattn_bv", "L0_xattn_bo",
                "L0_ffn_Wr", "L0_ffn_Wg", "L0_ffn_Wu", "L0_ffn_Wd", "L0_ffn_f_norm", "L0_ffn_fWg", "L0_ffn_fWu", "L0_ffn_fWd",
                "L1_attn_Wq", "L1_attn_Wk", "L1_attn_Wv", "L1_attn_Wo", "L1_attn_bo", "L1_attn_Wg", "L1_attn_bg", "L1_attn_decay_param",
                "L1_xattn_Wq", "L1_xattn_bq", "L1_xattn_Wk", "L1_xattn_bk", "L1_xattn_Wv", "L1_xattn_bv", "L1_xattn_bo",
                "L1_ffn_gate_w", "L1_ffn_gate_b", "L1_ffn_expert_w", "L1_ffn_expert_b")

    def mixed_rows(w):
        return w.reshape(8, -1, 4, 16, 256).transpose(1, 0, 3, 2, 4).reshape(-1, 128, 1024)

    laid = {name: given[name] for name in as_given}
    laid.update({f"{name}T": given[name].T for name in turned})
    laid["ctxT"] = given["ctx_1024"].transpose(0, 2, 1)
    laid["mask"] = given["mask_BxSxS2_bk1"]
    laid["L0_router_wT"] = given["L0_attn_router_w"].T
    laid["L0_mix_w"] = _np.concatenate([mixed_rows(given["L0_attn_w_hg"]), mixed_rows(given["L0_attn_w_out"])])
    laid["L0_xattn_WoP"] = given["L0_xattn_Wo"].T.reshape(2, 2, 4, 16, 256).transpose(0, 2, 1, 3, 4).reshape(2, 128, 256)
    laid["L0_ffn_norm_wP"] = given["L0_ffn_norm_w"].reshape(8, 2, 128).transpose(0, 2, 1)

    nc = _bacc.Bacc("TRN2", target_bir_lowering=False, num_devices=1)
    arrays, a = {}, {}
    for name, value in laid.items():
        value = _np.ascontiguousarray(value)
        arrays[f"in_{name}"] = value
        a[name] = nc.dram_tensor(f"in_{name}", value.shape, _mybir.dt.from_np(value.dtype), kind="ExternalInput").ap()
    a["out"] = nc.dram_tensor("out", (8, 512, 256), _mybir.dt.from_np(_np.dtype("float32")), kind="ExternalOutput").ap()
    decoder(nc, a)
    r = _run(nc, [arrays], core_ids=[0])
    return r.results[0]["out"]
```
